# Optimizing a Trainium2 kernel written in Bass

```python
import numpy as np
import jax
import jax.numpy as jnp

def _softmax(x, axis=-1):
    return jax.nn.softmax(x, axis=axis)

def _gelu(x):
    return jax.nn.gelu(x, approximate=True)

def _silu(x):
    return jax.nn.silu(x)

def _sigmoid(x):
    return jax.nn.sigmoid(x)

def _layernorm(x, axis=-1, eps=1e-05):
    m = jnp.mean(x, axis=axis, keepdims=True)
    v = jnp.var(x, axis=axis, keepdims=True)
    return (x - m) / jnp.sqrt(v + eps)

def _scatter_add(tgt, idx, src, axis=0):
    return tgt.at[idx].add(src)

def _segment_sum(src, seg, n):
    return jax.ops.segment_sum(src, seg, n)
kernel_name = 'mk_hybrid_d1_jaxref_r8_23bac2'

def setup_inputs(seed: int=0):
    np.random.seed(seed)
    _w = jnp.asarray

    def _L0_attn_a_setup():
        import jax, jax.numpy as jnp
        import numpy as np
        from jax import lax
        D_MODEL = 128
        D_STATE = 16
        D_CONV = 4
        EXPAND = 2
        D_INNER = EXPAND * D_MODEL
        DT_RANK = (D_MODEL + 15) // 16
        B, T = (2, 256)

        def _silu(v):
            return v * jax.nn.sigmoid(v)

        def _mamba_forward(x, in_proj_w, conv_w, conv_b, x_proj_w, dt_proj_w, dt_proj_b, A_log, Dp, out_proj_w):
            xz = jnp.einsum('btd,ed->bte', x, in_proj_w)
            xi, z = jnp.split(xz, 2, axis=-1)
            xt = jnp.pad(jnp.transpose(xi, (0, 2, 1)), ((0, 0), (0, 0), (D_CONV - 1, 0)))
            xc = lax.conv_general_dilated(xt, conv_w[:, None, :], window_strides=(1,), padding='VALID', feature_group_count=D_INNER, dimension_numbers=('NCH', 'OIH', 'NCH'))
            xc = _silu(xc + conv_b[None, :, None])
            xc = jnp.transpose(xc, (0, 2, 1))
            x_dbl = jnp.einsum('bti,ei->bte', xc, x_proj_w)
            dt_lo, Bp, Cp = jnp.split(x_dbl, [DT_RANK, DT_RANK + D_STATE], axis=-1)
            dt = jax.nn.softplus(jnp.einsum('btr,ir->bti', dt_lo, dt_proj_w) + dt_proj_b)
            A = -jnp.exp(A_log)
            h0 = jnp.zeros((x.shape[0], D_INNER, D_STATE), dtype=jnp.float32)

            def step(h, inp):
                dt_t, B_t, C_t, x_t = inp
                dA = jnp.exp(dt_t[..., None] * A[None])
                dBx = dt_t[..., None] * B_t[:, None, :] * x_t[..., None]
                h = dA * h + dBx
                y_t = jnp.sum(h * C_t[:, None, :], axis=-1)
                return (h, y_t)
            scan_in = (jnp.moveaxis(dt, 1, 0), jnp.moveaxis(Bp, 1, 0), jnp.moveaxis(Cp, 1, 0), jnp.moveaxis(xc, 1, 0))
            _, ys = lax.scan(step, h0, scan_in)
            y = jnp.moveaxis(ys, 0, 1) + Dp * xc
            y = y * _silu(z)
            return jnp.einsum('bti,di->btd', y, out_proj_w)
        key = jax.random.key(seed)
        ks = jax.random.split(key, 10)
        s = lambda n: 1.0 / np.sqrt(n)
        x = jax.random.normal(ks[0], (B, T, D_MODEL), dtype=jnp.float32)
        in_proj_w = jax.random.uniform(ks[1], (2 * D_INNER, D_MODEL), minval=-s(D_MODEL), maxval=s(D_MODEL))
        conv_w = jax.random.uniform(ks[2], (D_INNER, D_CONV), minval=-s(D_CONV), maxval=s(D_CONV))
        conv_b = jax.random.uniform(ks[3], (D_INNER,), minval=-s(D_CONV), maxval=s(D_CONV))
        x_proj_w = jax.random.uniform(ks[4], (DT_RANK + 2 * D_STATE, D_INNER), minval=-s(D_INNER), maxval=s(D_INNER))
        dt_proj_w = jax.random.uniform(ks[5], (D_INNER, DT_RANK), minval=-s(DT_RANK), maxval=s(DT_RANK))
        dt_proj_b = jax.random.uniform(ks[6], (D_INNER,), minval=-s(DT_RANK), maxval=s(DT_RANK))
        A_log = jnp.log(jnp.tile(jnp.arange(1, D_STATE + 1, dtype=jnp.float32), (D_INNER, 1)))
        Dp = jnp.ones((D_INNER,), dtype=jnp.float32)
        out_proj_w = jax.random.uniform(ks[7], (D_MODEL, D_INNER), minval=-s(D_INNER), maxval=s(D_INNER))
        return {'x': x, 'in_proj_w': in_proj_w, 'conv_w': conv_w, 'conv_b': conv_b, 'x_proj_w': x_proj_w, 'dt_proj_w': dt_proj_w, 'dt_proj_b': dt_proj_b, 'A_log': A_log, 'Dp': Dp, 'out_proj_w': out_proj_w}
    _L0_attn_a_in = _L0_attn_a_setup()

    def _L0_attn_b_setup():
        import jax, jax.numpy as jnp
        import numpy as np
        B, S, D, H = (2, 256, 128, 16)
        DEPTH = D // H
        EPS = 1e-06

        def _split_heads(t):
            b, s, _ = t.shape
            return t.reshape(b, s, H, DEPTH).transpose(0, 2, 1, 3)
        key = jax.random.key(seed)
        ks = jax.random.split(key, 6)
        glorot = lambda k: jax.random.uniform(k, (D, D), jnp.float32, -1.0, 1.0) * np.sqrt(6.0 / (D + D))
        return {'x': jax.random.normal(ks[0], (B, S, D), jnp.float32), 'Wq': glorot(ks[1]), 'bq': jnp.zeros((D,), jnp.float32), 'Wk': glorot(ks[2]), 'bk': jnp.zeros((D,), jnp.float32), 'Wv': glorot(ks[3]), 'bv': jnp.zeros((D,), jnp.float32), 'Wo': glorot(ks[4]), 'bo': jnp.zeros((D,), jnp.float32), 'gamma': jnp.ones((D,), jnp.float32), 'beta': jnp.zeros((D,), jnp.float32)}
    _L0_attn_b_in = _L0_attn_b_setup()

    def _L0_ffn_setup():
        import jax, jax.numpy as jnp
        import numpy as np
        D = 128
        H = 16
        HD = D // H
        L = 64
        E = 8
        B, T = (4, 256)
        EPS = 1e-06

        def _glorot(k, shape):
            fan_in, fan_out = (shape[-2], shape[-1])
            lim = np.sqrt(6.0 / (fan_in + fan_out)).astype(np.float32)
            return jax.random.uniform(k, shape, jnp.float32, -lim, lim)

        def _rmsnorm(x, gamma):
            return gamma * x * jax.lax.rsqrt(jnp.mean(x * x, axis=-1, keepdims=True) + EPS)
        key = jax.random.key(seed)
        ks = jax.random.split(key, 8)
        return {'x': jax.random.normal(ks[0], (B, T, D), jnp.float32), 'gamma1': jnp.ones((D,), jnp.float32), 'Wq': _glorot(ks[1], (D, D)), 'bq': jnp.zeros((D,), jnp.float32), 'Wdown': _glorot(ks[2], (D, L)), 'bdown': jnp.zeros((L,), jnp.float32), 'Wup': _glorot(ks[3], (L, 2 * D)), 'bup': jnp.zeros((2 * D,), jnp.float32), 'Wo': _glorot(ks[4], (D, D)), 'bo': jnp.zeros((D,), jnp.float32), 'gamma2': jnp.ones((D,), jnp.float32), 'Wg': _glorot(ks[5], (D, E)), 'bg': jnp.zeros((E,), jnp.float32), 'We': _glorot(ks[6], (E, D, D))}
    _L0_ffn_in = _L0_ffn_setup()
    _d = {'L0_attn_a_x': _L0_attn_a_in['x'], 'L0_attn_a_in_proj_w': _L0_attn_a_in['in_proj_w'], 'L0_attn_a_conv_w': _L0_attn_a_in['conv_w'], 'L0_attn_a_conv_b': _L0_attn_a_in['conv_b'], 'L0_attn_a_x_proj_w': _L0_attn_a_in['x_proj_w'], 'L0_attn_a_dt_proj_w': _L0_attn_a_in['dt_proj_w'], 'L0_attn_a_dt_proj_b': _L0_attn_a_in['dt_proj_b'], 'L0_attn_a_A_log': _L0_attn_a_in['A_log'], 'L0_attn_a_Dp': _L0_attn_a_in['Dp'], 'L0_attn_a_out_proj_w': _L0_attn_a_in['out_proj_w'], 'L0_attn_b_Wq': _L0_attn_b_in['Wq'], 'L0_attn_b_bq': _L0_attn_b_in['bq'], 'L0_attn_b_Wk': _L0_attn_b_in['Wk'], 'L0_attn_b_bk': _L0_attn_b_in['bk'], 'L0_attn_b_Wv': _L0_attn_b_in['Wv'], 'L0_attn_b_bv': _L0_attn_b_in['bv'], 'L0_attn_b_Wo': _L0_attn_b_in['Wo'], 'L0_attn_b_bo': _L0_attn_b_in['bo'], 'L0_attn_b_gamma': _L0_attn_b_in['gamma'], 'L0_attn_b_beta': _L0_attn_b_in['beta'], 'L0_ffn_gamma1': _L0_ffn_in['gamma1'], 'L0_ffn_Wq': _L0_ffn_in['Wq'], 'L0_ffn_bq': _L0_ffn_in['bq'], 'L0_ffn_Wdown': _L0_ffn_in['Wdown'], 'L0_ffn_bdown': _L0_ffn_in['bdown'], 'L0_ffn_Wup': _L0_ffn_in['Wup'], 'L0_ffn_bup': _L0_ffn_in['bup'], 'L0_ffn_Wo': _L0_ffn_in['Wo'], 'L0_ffn_bo': _L0_ffn_in['bo'], 'L0_ffn_gamma2': _L0_ffn_in['gamma2'], 'L0_ffn_Wg': _L0_ffn_in['Wg'], 'L0_ffn_bg': _L0_ffn_in['bg'], 'L0_ffn_We': _L0_ffn_in['We']}
    _x0 = _d['L0_attn_a_x']
    _d['L0_attn_a_x'] = jax.random.normal(jax.random.fold_in(jax.random.key(seed), 1), (16, 512, 128), dtype=_x0.dtype)
    del _x0
    return _d

def reference(L0_attn_a_x, L0_attn_a_in_proj_w, L0_attn_a_conv_w, L0_attn_a_conv_b, L0_attn_a_x_proj_w, L0_attn_a_dt_proj_w, L0_attn_a_dt_proj_b, L0_attn_a_A_log, L0_attn_a_Dp, L0_attn_a_out_proj_w, L0_attn_b_Wq, L0_attn_b_bq, L0_attn_b_Wk, L0_attn_b_bk, L0_attn_b_Wv, L0_attn_b_bv, L0_attn_b_Wo, L0_attn_b_bo, L0_attn_b_gamma, L0_attn_b_beta, L0_ffn_gamma1, L0_ffn_Wq, L0_ffn_bq, L0_ffn_Wdown, L0_ffn_bdown, L0_ffn_Wup, L0_ffn_bup, L0_ffn_Wo, L0_ffn_bo, L0_ffn_gamma2, L0_ffn_Wg, L0_ffn_bg, L0_ffn_We):

    def _L0_attn_a_ref(x, in_proj_w, conv_w, conv_b, x_proj_w, dt_proj_w, dt_proj_b, A_log, Dp, out_proj_w):
        import jax, jax.numpy as jnp
        import numpy as np
        from jax import lax
        D_MODEL = 128
        D_STATE = 16
        D_CONV = 4
        EXPAND = 2
        D_INNER = EXPAND * D_MODEL
        DT_RANK = (D_MODEL + 15) // 16
        B, T = (2, 256)

        def _silu(v):
            return v * jax.nn.sigmoid(v)

        def _mamba_forward(x, in_proj_w, conv_w, conv_b, x_proj_w, dt_proj_w, dt_proj_b, A_log, Dp, out_proj_w):
            xz = jnp.einsum('btd,ed->bte', x, in_proj_w)
            xi, z = jnp.split(xz, 2, axis=-1)
            xt = jnp.pad(jnp.transpose(xi, (0, 2, 1)), ((0, 0), (0, 0), (D_CONV - 1, 0)))
            xc = lax.conv_general_dilated(xt, conv_w[:, None, :], window_strides=(1,), padding='VALID', feature_group_count=D_INNER, dimension_numbers=('NCH', 'OIH', 'NCH'))
            xc = _silu(xc + conv_b[None, :, None])
            xc = jnp.transpose(xc, (0, 2, 1))
            x_dbl = jnp.einsum('bti,ei->bte', xc, x_proj_w)
            dt_lo, Bp, Cp = jnp.split(x_dbl, [DT_RANK, DT_RANK + D_STATE], axis=-1)
            dt = jax.nn.softplus(jnp.einsum('btr,ir->bti', dt_lo, dt_proj_w) + dt_proj_b)
            A = -jnp.exp(A_log)
            h0 = jnp.zeros((x.shape[0], D_INNER, D_STATE), dtype=jnp.float32)

            def step(h, inp):
                dt_t, B_t, C_t, x_t = inp
                dA = jnp.exp(dt_t[..., None] * A[None])
                dBx = dt_t[..., None] * B_t[:, None, :] * x_t[..., None]
                h = dA * h + dBx
                y_t = jnp.sum(h * C_t[:, None, :], axis=-1)
                return (h, y_t)
            scan_in = (jnp.moveaxis(dt, 1, 0), jnp.moveaxis(Bp, 1, 0), jnp.moveaxis(Cp, 1, 0), jnp.moveaxis(xc, 1, 0))
            _, ys = lax.scan(step, h0, scan_in)
            y = jnp.moveaxis(ys, 0, 1) + Dp * xc
            y = y * _silu(z)
            return jnp.einsum('bti,di->btd', y, out_proj_w)
        return _mamba_forward(x, in_proj_w, conv_w, conv_b, x_proj_w, dt_proj_w, dt_proj_b, A_log, Dp, out_proj_w)

    def _L0_attn_b_ref(x, Wq, bq, Wk, bk, Wv, bv, Wo, bo, gamma, beta):
        import jax, jax.numpy as jnp
        import numpy as np
        B, S, D, H = (2, 256, 128, 16)
        DEPTH = D // H
        EPS = 1e-06

        def _split_heads(t):
            b, s, _ = t.shape
            return t.reshape(b, s, H, DEPTH).transpose(0, 2, 1, 3)
        b, s, d = x.shape
        q = _split_heads(x @ Wq + bq)
        k = _split_heads(x @ Wk + bk)
        v = _split_heads(x @ Wv + bv)
        q = jax.nn.elu(q) + 1.0
        k = jax.nn.elu(k) + 1.0
        k = k / jnp.sqrt(jnp.sum(k * k, axis=-1, keepdims=True) + EPS)
        scores = jnp.einsum('bhqd,bhkd->bhqk', q, k)
        attn = jnp.einsum('bhqk,bhkd->bhqd', scores, v)
        attn = attn.transpose(0, 2, 1, 3).reshape(b, s, d)
        out = attn @ Wo + bo
        y = x + out
        mu = jnp.mean(y, axis=-1, keepdims=True)
        var = jnp.mean(jnp.square(y - mu), axis=-1, keepdims=True)
        return (y - mu) / jnp.sqrt(var + EPS) * gamma + beta

    def _L0_ffn_ref(x, gamma1, Wq, bq, Wdown, bdown, Wup, bup, Wo, bo, gamma2, Wg, bg, We):
        import jax, jax.numpy as jnp
        import numpy as np
        D = 128
        H = 16
        HD = D // H
        L = 64
        E = 8
        B, T = (4, 256)
        EPS = 1e-06

        def _glorot(k, shape):
            fan_in, fan_out = (shape[-2], shape[-1])
            lim = np.sqrt(6.0 / (fan_in + fan_out)).astype(np.float32)
            return jax.random.uniform(k, shape, jnp.float32, -lim, lim)

        def _rmsnorm(x, gamma):
            return gamma * x * jax.lax.rsqrt(jnp.mean(x * x, axis=-1, keepdims=True) + EPS)
        b, t = (x.shape[0], x.shape[1])
        h = _rmsnorm(x, gamma1)
        q = (h @ Wq + bq).reshape(b, t, H, HD)
        kv = ((h @ Wdown + bdown) @ Wup + bup).reshape(b, t, H, 2 * HD)
        k, v = jnp.split(kv, 2, axis=-1)
        att = jnp.einsum('bthd,btgd->bthg', q, k) / np.sqrt(HD).astype(np.float32)
        att = jax.nn.softmax(att, axis=-1)
        out = jnp.einsum('bthg,btgd->bthd', att, v).reshape(b, t, D)
        x = x + (out @ Wo + bo)
        h2 = _rmsnorm(x, gamma2)
        gate = jax.nn.softmax(h2 @ Wg + bg, axis=-1)
        combined = jnp.einsum('btd,edf,bte->btf', h2, We, gate)
        return x + combined
    x = L0_attn_a_x
    x = x + _L0_attn_a_ref(_layernorm(x, axis=-1), L0_attn_a_in_proj_w, L0_attn_a_conv_w, L0_attn_a_conv_b, L0_attn_a_x_proj_w, L0_attn_a_dt_proj_w, L0_attn_a_dt_proj_b, L0_attn_a_A_log, L0_attn_a_Dp, L0_attn_a_out_proj_w)
    x = x + _L0_ffn_ref(_layernorm(x, axis=-1), L0_ffn_gamma1, L0_ffn_Wq, L0_ffn_bq, L0_ffn_Wdown, L0_ffn_bdown, L0_ffn_Wup, L0_ffn_bup, L0_ffn_Wo, L0_ffn_bo, L0_ffn_gamma2, L0_ffn_Wg, L0_ffn_bg, L0_ffn_We)
    x = x + _L0_attn_b_ref(_layernorm(x, axis=-1), L0_attn_b_Wq, L0_attn_b_bq, L0_attn_b_Wk, L0_attn_b_bk, L0_attn_b_Wv, L0_attn_b_bv, L0_attn_b_Wo, L0_attn_b_bo, L0_attn_b_gamma, L0_attn_b_beta)
    x = x + _L0_ffn_ref(_layernorm(x, axis=-1), L0_ffn_gamma1, L0_ffn_Wq, L0_ffn_bq, L0_ffn_Wdown, L0_ffn_bdown, L0_ffn_Wup, L0_ffn_bup, L0_ffn_Wo, L0_ffn_bo, L0_ffn_gamma2, L0_ffn_Wg, L0_ffn_bg, L0_ffn_We)
    return x

_drawn_inputs = setup_inputs


def setup_inputs(seed=0):
    import zlib

    import numpy as np

    out = dict(_drawn_inputs(seed))
    spreads = {'L0_attn_a_Dp': (1.0, 0.6),
     'L0_attn_b_bq': (0.0, 0.762),
     'L0_attn_b_bk': (0.0, 0.8),
     'L0_attn_b_bv': (0.0, 0.1),
     'L0_attn_b_bo': (0.0, 0.8),
     'L0_attn_b_gamma': (1.0, 0.2),
     'L0_attn_b_beta': (0.0, 0.1),
     'L0_ffn_gamma1': (1.0, 0.2),
     'L0_ffn_bq': (0.0, 0.502),
     'L0_ffn_bdown': (0.0, 0.1),
     'L0_ffn_bup': (0.0, 0.1),
     'L0_ffn_bo': (0.0, 0.1),
     'L0_ffn_gamma2': (1.0, 0.2),
     'L0_ffn_bg': (0.0, 0.468)}
    factors = {'L0_attn_a_x_proj_w': 8.0,
     'L0_attn_a_dt_proj_w': 8.0,
     'L0_attn_a_dt_proj_b': 8.0,
     'L0_attn_a_A_log': 8.0}
    for name, (base, spread) in spreads.items():
        noise = np.random.default_rng([zlib.crc32(name.encode()), seed]).standard_normal(out[name].shape)
        drawn = base * np.exp(spread * noise) if base else spread * noise
        out[name] = jnp.asarray(drawn.astype(out[name].dtype))
    for name, factor in factors.items():
        out[name] = (out[name] * factor).astype(out[name].dtype)
    return out
```

```python
import numpy as np
import concourse.bass as bass
from concourse import mybir
from contextlib import ExitStack

FP32 = mybir.dt.float32
BF16 = mybir.dt.bfloat16
I32 = mybir.dt.int32
ALU = mybir.AluOpType
ACT = mybir.ActivationFunctionType
AX = mybir.AxisListType

P = 128
BATCH, TOK, D = 16, 512, 128
TILES = TOK // P
HALVES = 2
STATE = 16
CONV = 4
RANK = 8
H, HD = 16, 8
LAT = 64
EXP = 8
PAIRS = H * H
LAYERS = 2
LN_EPS, RMS_EPS = 1e-5, 1e-6
SCALE = float(HD) ** -0.5

_nodes = 0.5 - 0.5 * np.cos(np.pi * (np.arange(200) + 0.5) / 200)
LOG1P = [float(c) for c in np.polynomial.Polynomial.fit(
    _nodes, np.log1p(_nodes) / _nodes, 8, domain=[0, 1]).convert().coef]


def hybrid_block_kernel(nc, x_d, in_w_d, conv_w_d, conv_b_d, xp_w_d, dt_w_d, dt_b_d, alog_d, dp_d, out_w_d,
                        l_wq_d, l_bq_d, l_wk_d, l_bk_d, l_wv_d, l_bv_d, l_wo_d, l_bo_d, l_gamma_d, l_beta_d,
                        f_g1_d, f_wq_d, f_bq_d, f_wdown_d, f_bdown_d, f_wupk_d, f_wupv_d, f_wo_d, f_bo_d,
                        f_g2_d, f_wg_d, f_bg_d, f_we_d, ident_d, pick_d, blocks_d, y_d):
    ctx = ExitStack()
    with ctx:
        def sb(name, shape, dt=FP32):
            return ctx.enter_context(nc.sbuf_tensor(name, shape, dt))

        class Signal:

            def __init__(self, name, per):
                self.sem, self.per = ctx.enter_context(nc.semaphore(name)), per

            def at(self, i, k):
                return i * self.per + k

        ident = sb("ident", [P, P])
        pick = sb("pick", [96, 32])
        pickb = sb("pickb", [96, 32, P], BF16)
        blocks = sb("blocks", [P, P])
        in_w = sb("in_w", [P, 2 * HALVES * P])
        conv_w = sb("conv_w", [P, HALVES, CONV])
        conv_b = sb("conv_b", [P, HALVES])
        conv_bh = sb("conv_bh", [P, HALVES])
        xp_w = sb("xp_w", [P, HALVES, P])
        dt_w = sb("dt_w", [P, HALVES * P])
        dt_b = sb("dt_b", [P, HALVES])
        a_neg = sb("a_neg", [P, HALVES, STATE])
        dp = sb("dp", [P, HALVES])
        out_w = sb("out_w", [P, HALVES, D])
        l_wq, l_wk, l_wv, l_wo = (sb(n, [P, D]) for n in ("l_wq", "l_wk", "l_wv", "l_wo"))
        l_bq = sb("l_bq", [P, 1])
        l_bk, l_bv, l_bo, l_gamma, l_beta = (sb(n, [P, D]) for n in ("l_bk", "l_bv", "l_bo", "l_gamma", "l_beta"))
        f_g1, f_g2 = (sb(n, [P, 1]) for n in ("f_g1", "f_g2"))
        f_bq = sb("f_bq", [P, D])
        f_wq = sb("f_wq", [P, D])
        f_wdown = sb("f_wdown", [P, LAT])
        f_bdown = sb("f_bdown", [LAT, 1])
        f_wupk = sb("f_wupk", [LAT + 1, D])
        f_wupv = sb("f_wupv", [LAT + 1, D])
        f_wo = sb("f_wo", [P, D])
        f_bo = sb("f_bo", [P, D])
        f_wg = sb("f_wg", [P, EXP])
        f_bg = sb("f_bg", [P, EXP])
        f_we = sb("f_we", [P, EXP * D])
        minus_half = sb("minus_half", [P, 2 * TILES])
        spare = sb("spare", [P, 1])

        xin = sb("xin", [P, TILES, D])
        xr = sb("xr", [P, TILES, D])
        xo = sb("xo", [P, TILES, D])
        stats = sb("stats", [P, TILES, 6])
        mv = sb("mv", [P, TILES, 2])
        var_in = sb("var_in", [P, 2 * TILES])
        rstd = sb("rstd", [P, 2 * TILES])
        nrm = sb("nrm", [P, TILES, D])
        scaled = sb("scaled", [P, TILES, D])
        nT = sb("nT", [P, TOK])
        xpad = sb("xpad", [P, HALVES, CONV - 1 + TOK])
        cv = sb("cv", [P, HALVES, TOK])
        xc = sb("xc", [P, HALVES, TOK])
        z_h = sb("z_h", [P, HALVES, TOK])
        dt_lo = sb("dt_lo", [P, TOK])
        bc_hi = sb("bc_hi", [96, TOK], BF16)
        bc_rest = sb("bc_rest", [96, TOK])
        bc_mid = sb("bc_mid", [96, TOK], BF16)
        bc_parts = sb("bc_parts", [96, TOK], BF16)
        sp_abs = sb("sp_abs", [P, HALVES, TOK])
        sp_max = sb("sp_max", [P, HALVES, TOK])
        sp_t = sb("sp_t", [P, HALVES, TOK])
        dt = sb("dt", [P, HALVES, TOK])
        u = sb("u", [P, HALVES, TOK])
        cv_t, cv_h, z_t, sp_e = sp_t, u, sp_max, sp_abs
        d_a = sb("d_a", [P, 2, HALVES, TOK])
        d_bx = sb("d_bx", [P, 2, HALVES, TOK])
        hs = sb("hs", [P, 2, HALVES, TOK])
        c_sb = sb("c_sb", [P, 2, TOK])
        hc = sb("hc", [P, 2, HALVES, TOK])
        hT = sb("hT", [P, TOK])
        latT = sb("latT", [LAT + 1, TOK])
        q_tok = sb("q_tok", [P, TILES, D])
        ka_tok = sb("ka_tok", [P, TILES, D])
        va_tok = sb("va_tok", [P, TILES, D])
        qk = sb("qk", [P, 2, PAIRS * HD])
        score = sb("score", [P, TILES, PAIRS])
        peak = sb("peak", [P, TILES, H])
        total = sb("total", [P, TILES, H])
        pv = sb("pv", [P, 2, H, D])
        rec = sb("rec", [P, TILES, H])
        o_tok = sb("o_tok", [P, TILES, D])
        oT = sb("oT", [P, TOK])
        nb = sb("nb", [P, TILES, D])
        x1 = sb("x1", [P, TILES, D])
        xx1 = sb("xx1", [P, TILES, D])
        gate = sb("gate", [P, TILES, EXP])
        g_max = sb("g_max", [P, TILES])
        g_sum = sb("g_sum", [P, TILES])
        q_min = sb("q_min", [P, TOK])
        q_max = sb("q_max", [P, TOK])
        k_tok = sb("k_tok", [P, TILES, D])
        k_min = sb("k_min", [P, TILES, D])
        k_ss = sb("k_ss", [P, TILES * H])
        k_y = sb("k_y", [P, TILES * H])
        k_a = sb("k_a", [P, TILES * H])
        q_exp, qT, k_exp, k_sq = q_min, q_max, k_min, k_min
        v_tok = sb("v_tok", [P, TILES, D])
        kv = sb("kv", [P, D])
        kvo = sb("kvo", [P, D])
        lin = sb("lin", [P, TILES, D])

        bank = ctx.enter_context(nc.psum_tensor("bank", [P, 8, 512], FP32))
        sig = {}

        def signal(name, per):
            sig[name] = Signal(name, per)
            return sig[name]

        s_w = signal("weights_loaded", 0)
        s_const = signal("constants_made", 0)
        s_pool_const = signal("pool_constants_made", 0)
        s_xin = signal("x_loaded", 16)
        s_out = signal("y_stored", 16)
        s_xfree = signal("x_consumed", 1)
        s_var = signal("variance_ready", 7)
        s_rstd = signal("rstd_ready", 7)
        s_nrm = signal("normalized", 6)
        s_nT = signal("normalized_transposed", 6)
        s_nTe = signal("transpose_in_sbuf", 6)
        s_inp = signal("in_projected", 4)
        s_xpad = signal("x_padded", 2)
        s_z = signal("z_tanh_ready", 2)
        s_cv = signal("convolved", 2)
        s_cvt = signal("conv_tanh_ready", 2)
        s_xc = signal("xc_ready", 2)
        s_xp = signal("x_projected", 1)
        s_dtl = signal("dt_low_ready", 1)
        s_bch = signal("bc_high_ready", 1)
        s_bcp = signal("bc_parts_ready", 1)
        s_dtp = signal("dt_projected", 2)
        s_abs = signal("softplus_abs_ready", 1)
        s_spe = signal("softplus_exp_ready", 1)
        s_dt = signal("dt_ready", 1)
        s_da = signal("decay_ready", STATE)
        s_bb = signal("b_broadcast", STATE)
        s_bfree = signal("b_consumed", STATE)
        s_cb = signal("c_broadcast", STATE)
        s_cs = signal("c_in_sbuf", STATE)
        s_scan = signal("scanned", STATE)
        s_hc = signal("h_times_c", STATE)
        s_yacc = signal("y_accumulated", STATE)
        s_yg = signal("y_gated", 1)
        s_mo = signal("mamba_projected", 1)
        s_x = signal("residual_ready", 4)
        s_qp = signal("q_projected", 2)
        s_lat = signal("latent_projected", 2)
        s_late = signal("latent_ready", 2)
        s_kp = signal("k_projected", 2)
        s_vp = signal("v_projected", 2)
        s_qt = signal("q_ready", 2)
        s_kt = signal("k_ready", 2)
        s_vt = signal("v_ready", 2)
        s_qk = signal("qk_products", 2 * TILES)
        s_qkr = signal("scores_summed", 2 * TILES)
        s_sh = signal("scores_shifted", 2 * TILES)
        s_e = signal("probs_ready", 2 * TILES)
        s_pv = signal("pv_products", 2 * TILES)
        s_av = signal("pv_summed", 2 * TILES)
        s_on = signal("attention_normalized", 2)
        s_oT = signal("attention_transposed", 2)
        s_oTe = signal("attention_in_sbuf", 2)
        s_wo = signal("attention_projected", 2)
        s_nb = signal("residual_with_bias", 3)
        s_x1 = signal("x1_ready", 2)
        s_xx = signal("x_plus_x1", 2)
        s_gl = signal("gate_logits", 2)
        s_gs = signal("gate_shifted", 2)
        s_ge = signal("gate_exp", 2)
        s_moe = signal("experts_ready", 2 * 2 * TILES)
        s_moef = signal("banks_free", 2)
        s_lq = signal("lin_q_projected", 1)
        s_lk = signal("lin_k_projected", 1)
        s_lv = signal("lin_v_projected", 1)
        s_qmin = signal("q_min_ready", 1)
        s_qexp = signal("q_exp_ready", 1)
        s_lqT = signal("lin_q_ready", 1)
        s_kmin = signal("k_min_ready", 1)
        s_kexp = signal("k_exp_ready", 1)
        s_lkv = signal("lin_kv_in_sbuf", 1)
        s_kv = signal("kv_summed", 1)
        s_kvm = signal("kv_masked", 1)
        s_g = signal("kv_projected", 1)
        s_ge2 = signal("kvo_in_sbuf", 1)
        s_lo = signal("lin_projected", 1)
        s_xb = signal("x_plus_beta", 1)

        s_aexp = ctx.enter_context(nc.semaphore("decay_rates_ready"))

        small = []
        for t, s in ((ident[:, :], ident_d), (pick[:, :], pick_d), (in_w[:, :], in_w_d),
                     (conv_w[:, :, :], conv_w_d), (conv_b[:, :], conv_b_d), (xp_w[:, :, :], xp_w_d),
                     (dt_w[96:96 + RANK, :], dt_w_d), (dt_b[:, :], dt_b_d), (a_neg[:, :, :], alog_d),
                     (dp[:, :], dp_d), (out_w[:, :, :], out_w_d), (l_wq[:, :], l_wq_d), (l_wk[:, :], l_wk_d),
                     (l_wv[:, :], l_wv_d), (l_wo[:, :], l_wo_d), (l_bq[:, :], l_bq_d), (f_g1[:, :], f_g1_d),
                     (f_g2[:, :], f_g2_d), (f_wq[:, :], f_wq_d), (f_wdown[:, :], f_wdown_d),
                     (f_bdown[:, :], f_bdown_d), (f_wupk[:, :], f_wupk_d), (f_wupv[:, :], f_wupv_d),
                     (f_wo[:, :], f_wo_d), (f_wg[:, :], f_wg_d), (f_we[:, :], f_we_d)):
            small.append((t, s))
        for t, s in ((l_bk, l_bk_d), (l_bv, l_bv_d), (l_bo, l_bo_d), (l_gamma, l_gamma_d), (l_beta, l_beta_d),
                     (f_bo, f_bo_d), (f_bq, f_bq_d), (f_bg, f_bg_d)):
            small.append((t[:, :], s.partition_broadcast(P)))
        WEIGHTS = 16 * len(small)
        DVE_LINKS = 96

        N_MAMBA, N_LIN_IN, N_LIN_OUT = 0, 3, 4
        N_ATT, N_MOE = (1, 5), (2, 6)
        T_MAMBA, T_LIN = 0, 3
        T_ATT, T_MOE = (1, 4), (2, 5)

        def tile_of(l, c):
            return l * TILES + c + 1

        block = ctx.enter_context(nc.Block())

        @block.sync
        def _(sp):
            for t, s in small:
                sp.dma_start(t, s).then_inc(s_w.sem, 16)
            sp.dma_start(blocks[:, :], blocks_d).then_inc(s_out.sem, 16)

            def load(i):
                sp.dma_start(xin[:, :, :], x_d[bass.ds(i, 1), :, :].rearrange("o (c p) d -> p (o c) d", p=P)) \
                    .then_inc(s_xin.sem, 16)

            def store(i):
                sp.wait_ge(s_x.sem, s_x.at(i, 4))
                sp.dma_start(y_d[bass.ds(i, 1), :, :].rearrange("o (c p) d -> p (o c) d", p=P), xo[:, :, :]) \
                    .then_inc(s_out.sem, 16)

            load(0)
            with sp.Fori(0, BATCH - 1) as i:
                sp.wait_ge(s_xfree.sem, s_xfree.at(i, 1))
                load(i + 1)
                store(i)
            store(BATCH - 1)
            sp.wait_ge(s_out.sem, 16 * (BATCH + 1))

        @block.gpsimd
        def _(pool):
            pool.memset(minus_half[:, :], -0.5)
            pool.memset(xpad[:, :, 0:CONV - 1], 0.0).then_inc(s_pool_const.sem, 1)
            pool.wait_ge(s_pool_const.sem, 1)
            pool.wait_ge(s_w.sem, WEIGHTS)

            with pool.Fori(0, BATCH) as i:
                def rsqrt(k, n):
                    pool.wait_ge(s_var.sem, s_var.at(i, k + 1))
                    pool.tensor_tensor(rstd[:, 0:n], var_in[:, 0:n], minus_half[:, 0:n], ALU.pow) \
                        .then_inc(s_rstd.sem, 1)

                rsqrt(N_MAMBA, TILES)
                for n in range(STATE):
                    pool.wait_ge(s_cs.sem, s_cs.at(i, n + 1))
                    pool.wait_ge(s_scan.sem, s_scan.at(i, n + 1))
                    if n >= 2:
                        pool.wait_ge(s_yacc.sem, s_yacc.at(i, n - 1))
                    pool.tensor_tensor(hc[:, n % 2, :, :], hs[:, n % 2, :, :],
                                       c_sb[:, n % 2, None, :].broadcast_to([P, HALVES, TOK]), ALU.mult) \
                        .then_inc(s_hc.sem, 1)

                def softmax_layer(l):
                    rsqrt(N_ATT[l], 2 * TILES)
                    pool.wait_ge(s_nrm.sem, s_nrm.at(i, T_ATT[l] + 1))
                    pool.tensor_tensor(nb[:, :, :], nrm[:, :, :],
                                       f_bo[:, None, :].broadcast_to([P, TILES, D]), ALU.add).then_inc(s_nb.sem, 1)
                    pool.wait_ge(s_qt.sem, s_qt.at(i, l + 1))
                    pool.wait_ge(s_kt.sem, s_kt.at(i, l + 1))
                    for c in range(TILES):
                        if c >= 2:
                            pool.wait_ge(s_qkr.sem, s_qkr.at(i, tile_of(l, c - 2)))
                        pool.tensor_tensor(
                            qk[:, c % 2, :].rearrange("p (h g e) -> p h g e", h=H, g=H),
                            q_tok[:, c, :].rearrange("p (h e) -> p h e", e=HD)[:, :, None, :]
                            .broadcast_to([P, H, H, HD]),
                            ka_tok[:, c, None, :].broadcast_to([P, H, D]).rearrange("p h (g e) -> p h g e", e=HD),
                            ALU.mult).then_inc(s_qk.sem, 1)
                    rsqrt(N_MOE[l], TILES)
                    pool.wait_ge(s_x1.sem, s_x1.at(i, l + 1))
                    pool.tensor_tensor(xx1[:, :, :], xr[:, :, :], x1[:, :, :], ALU.add).then_inc(s_xx.sem, 1)

                softmax_layer(0)
                rsqrt(N_LIN_IN, TILES)
                pool.wait_ge(s_nrm.sem, s_nrm.at(i, T_LIN + 1))
                pool.tensor_tensor(nb[:, :, :], nrm[:, :, :],
                                   l_bo[:, None, :].broadcast_to([P, TILES, D]), ALU.add).then_inc(s_nb.sem, 1)
                pool.tensor_tensor(xx1[:, :, :], xr[:, :, :],
                                   l_beta[:, None, :].broadcast_to([P, TILES, D]), ALU.add).then_inc(s_xb.sem, 1)
                rsqrt(N_LIN_OUT, TILES)
                softmax_layer(1)

        @block.vector
        def _(dve):
            dve.memset(latT[LAT:LAT + 1, :], 1.0)
            dve.wait_ge(s_pool_const.sem, 1)
            dve.wait_ge(s_w.sem, WEIGHTS)
            dve.wait_ge(s_out.sem, 16)
            dve.tensor_copy(pickb[:, :, :], pick[:, :, None].broadcast_to([96, 32, P]))
            dve.tensor_scalar(conv_bh[:, :], conv_b[:, :], 0.5, None, ALU.mult).then_inc(s_const.sem, 1)
            chain = ctx.enter_context(nc.semaphore("vector_step_done"))
            count = [0]

            with dve.Fori(0, BATCH) as i:
                def link(ins):
                    count[0] += 1
                    ins.then_inc(chain, 1)
                    dve.wait_ge(chain, i * DVE_LINKS + count[0])

                def moments(src):
                    for c in range(TILES):
                        ins = dve.bn_stats(stats[:, c, :], src[:, c, :])
                    link(ins)
                    dve.memset(spare[:, :], 0.0)
                    for c in range(TILES):
                        ins = dve.bn_aggr(mv[:, c, :], stats[:, c, :])
                    link(ins)

                def scale_tokens(dst, src, column, centre=True):
                    for c in range(TILES):
                        if centre:
                            ins = dve.tensor_scalar(dst[:, c, :], src[:, c, :], mv[:, c, 0:1],
                                                    rstd[:, column + c:column + c + 1], ALU.subtract, ALU.mult)
                        else:
                            ins = dve.tensor_scalar(dst[:, c, :], src[:, c, :],
                                                    rstd[:, column + c:column + c + 1], None, ALU.mult)
                    return ins

                dve.wait_ge(s_xin.sem, s_xin.at(i, 16))
                moments(xin)
                dve.tensor_scalar(var_in[:, 0:TILES], mv[:, :, 1], LN_EPS, None, ALU.add).then_inc(s_var.sem, 1)
                dve.wait_ge(s_rstd.sem, s_rstd.at(i, N_MAMBA + 1))
                scale_tokens(nrm, xin, 0).then_inc(s_nrm.sem, 1)
                for h in range(HALVES):
                    dve.wait_ge(s_xpad.sem, s_xpad.at(i, h + 1))
                    link(dve.tensor_scalar(cv[:, h, :], xpad[:, h, 0:TOK], conv_w[:, h, 0:1], None, ALU.mult))
                    for k in range(1, CONV):
                        ins = dve.scalar_tensor_tensor(cv[:, h, :], xpad[:, h, k:k + TOK], conv_w[:, h, k:k + 1],
                                                       cv[:, h, :], ALU.mult, ALU.add)
                        if k < CONV - 1:
                            link(ins)
                    ins.then_inc(s_cv.sem, 1)
                for h in range(HALVES):
                    dve.wait_ge(s_cvt.sem, s_cvt.at(i, h + 1))
                    dve.scalar_tensor_tensor(xc[:, h, :], cv_t[:, h, :], 1.0, cv_h[:, h, :], ALU.add, ALU.mult) \
                        .then_inc(s_xc.sem, 1)
                dve.wait_ge(s_z.sem, s_z.at(i, 2))
                dve.scalar_tensor_tensor(z_h[:, :, :], z_t[:, :, :], 1.0, z_h[:, :, :], ALU.add, ALU.mult)
                dve.wait_ge(s_bch.sem, s_bch.at(i, 1))
                link(dve.tensor_tensor(bc_rest[:, :], bank[0:96, 4, :], bc_hi[:, :], ALU.subtract))
                dve.tensor_copy(bc_parts[32:64, :], bc_rest[32:64, :])
                link(dve.tensor_copy(bc_mid[64:96, :], bc_rest[64:96, :]))
                dve.tensor_tensor(bc_parts[64:96, :], bc_rest[64:96, :], bc_mid[64:96, :], ALU.subtract) \
                    .then_inc(s_bcp.sem, 1)
                dve.wait_ge(s_dtp.sem, s_dtp.at(i, 2))
                dve.wait_ge(s_abs.sem, s_abs.at(i, 1))
                for h in range(HALVES):
                    dve.tensor_scalar(sp_max[:, h, :], bank[:, 5 + h, :], dt_b[:, h:h + 1], 0.0, ALU.add, ALU.max)
                dve.wait_ge(s_spe.sem, s_spe.at(i, 1))
                link(dve.tensor_scalar(sp_t[:, :, :], sp_e[:, :, :], LOG1P[-1], None, ALU.mult))
                for c in reversed(LOG1P[:-1]):
                    link(dve.scalar_tensor_tensor(sp_t[:, :, :], sp_t[:, :, :], c, sp_e[:, :, :], ALU.add, ALU.mult))
                link(dve.tensor_tensor(dt[:, :, :], sp_t[:, :, :], sp_max[:, :, :], ALU.add))
                dve.tensor_tensor(u[:, :, :], dt[:, :, :], xc[:, :, :], ALU.mult).then_inc(s_dt.sem, 1)
                dve.wait_ge(s_dt.sem, s_dt.at(i, 1))

                def input_of(n):
                    dve.wait_ge(s_bb.sem, s_bb.at(i, n + 1))
                    dve.tensor_tensor(d_bx[:, n % 2, :, :], u[:, :, :],
                                      bank[:, n % 2, None, :].broadcast_to([P, HALVES, TOK]), ALU.mult) \
                        .then_inc(s_bfree.sem, 1)

                input_of(0)
                for n in range(STATE):
                    if n + 1 < STATE:
                        input_of(n + 1)
                    dve.wait_ge(s_bfree.sem, s_bfree.at(i, n + 1))
                    dve.wait_ge(s_da.sem, s_da.at(i, n + 1))
                    if n >= 2:
                        dve.wait_ge(s_hc.sem, s_hc.at(i, n - 1))
                    for h in range(HALVES):
                        ins = dve.tensor_tensor_scan(hs[:, n % 2, h, :], d_a[:, n % 2, h, :], d_bx[:, n % 2, h, :],
                                                     0.0, ALU.mult, ALU.add)
                    ins.then_inc(s_scan.sem, 1)
                dve.wait_ge(s_yacc.sem, s_yacc.at(i, STATE))
                for h in range(HALVES):
                    ins = dve.scalar_tensor_tensor(sp_t[:, h, :], xc[:, h, :], dp[:, h:h + 1], bank[:, 4 + h, :],
                                                   ALU.mult, ALU.add)
                link(ins)
                dve.tensor_tensor(sp_t[:, :, :], sp_t[:, :, :], z_h[:, :, :], ALU.mult).then_inc(s_yg.sem, 1)
                dve.wait_ge(s_mo.sem, s_mo.at(i, 1))
                dve.tensor_tensor(xr[:, :, :], bank[:, 6, :].rearrange("p (c d) -> p c d", c=TILES), xin[:, :, :],
                                  ALU.add).then_inc(s_x.sem, 1)
                dve.wait_ge(s_x.sem, s_x.at(i, 1))

                def softmax_layer(l, dst):
                    moments(xr)
                    ins = dve.tensor_scalar(var_in[:, 0:TILES], mv[:, :, 1], LN_EPS, None, ALU.add)
                    if l == 0:
                        ins.then_inc(s_xfree.sem, 1)
                    dve.tensor_scalar(var_in[:, TILES:2 * TILES], mv[:, :, 1], 1.0 + RMS_EPS, RMS_EPS * LN_EPS,
                                      ALU.mult, ALU.add).then_inc(s_var.sem, 1)
                    dve.wait_ge(s_rstd.sem, s_rstd.at(i, N_ATT[l] + 1))
                    scale_tokens(scaled, xr, TILES)
                    scale_tokens(nrm, xr, 0).then_inc(s_nrm.sem, 1)
                    dve.wait_ge(s_qp.sem, s_qp.at(i, l + 1))
                    dve.tensor_tensor(q_tok[:, :, :], bank[:, 0, :].rearrange("p (c d) -> p c d", c=TILES),
                                      f_bq[:, None, :].broadcast_to([P, TILES, D]), ALU.add).then_inc(s_qt.sem, 1)

                    def shift(c):
                        sc = score[:, c, :].rearrange("p (h g) -> p h g", g=H)
                        dve.wait_ge(s_qk.sem, s_qk.at(i, tile_of(l, c)))
                        dve.tensor_reduce(score[:, c, :], qk[:, c % 2, :].rearrange("p (a e) -> p a e", e=HD),
                                          AX.X, ALU.add).then_inc(s_qkr.sem, 1)
                        dve.wait_ge(s_qkr.sem, s_qkr.at(i, tile_of(l, c)))
                        link(dve.tensor_reduce(peak[:, c, :], sc, AX.X, ALU.max))
                        dve.tensor_tensor(sc, sc, peak[:, c, :, None].broadcast_to([P, H, H]), ALU.subtract) \
                            .then_inc(s_sh.sem, 1)

                    def weigh(c):
                        pr = score[:, c, :].rearrange("p (h g) -> p h g", g=H)
                        dve.wait_ge(s_e.sem, s_e.at(i, tile_of(l, c)))
                        if c == 0:
                            dve.wait_ge(s_vt.sem, s_vt.at(i, l + 1))
                        if c >= 2:
                            dve.wait_ge(s_av.sem, s_av.at(i, tile_of(l, c - 2)))
                        dve.tensor_tensor(
                            pv[:, c % 2, :, :].rearrange("p g (h e) -> p g h e", e=HD),
                            pr.rearrange("p h g -> p g h")[:, :, :, None].broadcast_to([P, H, H, HD]),
                            va_tok[:, c, :].rearrange("p (g e) -> p g e", e=HD)[:, :, None, :]
                            .broadcast_to([P, H, H, HD]), ALU.mult).then_inc(s_pv.sem, 1)
                        return dve.tensor_reduce(total[:, c, :], pr, AX.X, ALU.add)

                    shift(0)
                    for c in range(TILES):
                        if c + 1 < TILES:
                            shift(c + 1)
                        ins = weigh(c)
                    link(ins)
                    link(dve.reciprocal(rec[:, :, :], total[:, :, :]))
                    dve.wait_ge(s_av.sem, s_av.at(i, tile_of(l, TILES - 1)))
                    dve.tensor_tensor(o_tok[:, :, :].rearrange("p c (h e) -> p (c h) e", e=HD),
                                      bank[:, 4, :].rearrange("p (a e) -> p a e", e=HD),
                                      rec[:, :, :].rearrange("p c h -> p (c h)")[:, :, None]
                                      .broadcast_to([P, TILES * H, HD]), ALU.mult).then_inc(s_on.sem, 1)
                    dve.wait_ge(s_wo.sem, s_wo.at(i, l + 1))
                    dve.wait_ge(s_nb.sem, s_nb.at(i, 2 * l + 1))
                    dve.tensor_tensor(x1[:, :, :], bank[:, 1, :].rearrange("p (c d) -> p c d", c=TILES), nb[:, :, :],
                                      ALU.add).then_inc(s_x1.sem, 1)
                    dve.wait_ge(s_x1.sem, s_x1.at(i, l + 1))
                    moments(x1)
                    link(dve.tensor_tensor(g_sum[:, :], mv[:, :, 0], mv[:, :, 0], ALU.mult))
                    dve.scalar_tensor_tensor(var_in[:, 0:TILES], g_sum[:, :], RMS_EPS, mv[:, :, 1],
                                             ALU.add, ALU.add).then_inc(s_var.sem, 1)
                    dve.wait_ge(s_rstd.sem, s_rstd.at(i, N_MOE[l] + 1))
                    scale_tokens(scaled, x1, 0, centre=False).then_inc(s_nrm.sem, 1)
                    dve.wait_ge(s_gl.sem, s_gl.at(i, l + 1))
                    link(dve.tensor_tensor(gate[:, :, :], bank[:, 3, 0:TILES * EXP].rearrange("p (c e) -> p c e", e=EXP),
                                           f_bg[:, None, :].broadcast_to([P, TILES, EXP]), ALU.add))
                    link(dve.tensor_reduce(g_max[:, :], gate[:, :, :], AX.X, ALU.max))
                    dve.tensor_tensor(gate[:, :, :], gate[:, :, :], g_max[:, :, None].broadcast_to([P, TILES, EXP]),
                                      ALU.subtract).then_inc(s_gs.sem, 1)
                    dve.wait_ge(s_ge.sem, s_ge.at(i, l + 1))
                    link(dve.tensor_reduce(g_sum[:, :], gate[:, :, :], AX.X, ALU.add))
                    link(dve.reciprocal(g_max[:, :], g_sum[:, :]))
                    link(dve.tensor_tensor(gate[:, :, :], gate[:, :, :],
                                           g_max[:, :, None].broadcast_to([P, TILES, EXP]), ALU.mult))
                    dve.wait_ge(s_xx.sem, s_xx.at(i, l + 1))
                    if dst is xo:
                        dve.wait_ge(s_out.sem, s_out.at(i, 16))
                    for e in range(EXP):
                        for c in range(TILES):
                            b = (e // 4) * TILES + c
                            if e % 4 == 0:
                                dve.wait_ge(s_moe.sem, s_moe.at(i, 2 * TILES * l + b + 1))
                            out = dst if e == EXP - 1 else xx1
                            ins = dve.scalar_tensor_tensor(out[:, c, :], bank[:, b, D * (e % 4):D * (e % 4) + D],
                                                           gate[:, c, e:e + 1], xx1[:, c, :], ALU.mult, ALU.add)
                        if e < EXP - 1:
                            link(ins)
                    ins.then_inc(s_x.sem, 1)

                softmax_layer(0, xr)
                dve.wait_ge(s_x.sem, s_x.at(i, 2))

                moments(xr)
                dve.tensor_scalar(var_in[:, 0:TILES], mv[:, :, 1], LN_EPS, None, ALU.add).then_inc(s_var.sem, 1)
                dve.wait_ge(s_rstd.sem, s_rstd.at(i, N_LIN_IN + 1))
                scale_tokens(nrm, xr, 0).then_inc(s_nrm.sem, 1)
                dve.wait_ge(s_lk.sem, s_lk.at(i, 1))
                link(dve.tensor_tensor(k_tok[:, :, :], bank[:, 1, :].rearrange("p (c d) -> p c d", c=TILES),
                                       l_bk[:, None, :].broadcast_to([P, TILES, D]), ALU.add))
                dve.tensor_scalar(k_min[:, :, :], k_tok[:, :, :], 0.0, None, ALU.min).then_inc(s_kmin.sem, 1)
                dve.wait_ge(s_lq.sem, s_lq.at(i, 1))
                dve.tensor_scalar(q_min[:, :], bank[:, 0, :], l_bq[:, 0:1], 0.0, ALU.add, ALU.min) \
                    .then_inc(s_qmin.sem, 1)
                dve.tensor_scalar(q_max[:, :], bank[:, 0, :], l_bq[:, 0:1], 0.0, ALU.add, ALU.max)
                dve.wait_ge(s_lv.sem, s_lv.at(i, 1))
                dve.tensor_tensor(v_tok[:, :, :], bank[:, 2, :].rearrange("p (c d) -> p c d", c=TILES),
                                  l_bv[:, None, :].broadcast_to([P, TILES, D]), ALU.add)
                dve.wait_ge(s_kexp.sem, s_kexp.at(i, 1))
                link(dve.scalar_tensor_tensor(k_tok[:, :, :], k_tok[:, :, :], 0.0, k_exp[:, :, :], ALU.max, ALU.add))
                link(dve.tensor_tensor(k_sq[:, :, :], k_tok[:, :, :], k_tok[:, :, :], ALU.mult))
                link(dve.tensor_reduce(k_ss[:, :], k_sq[:, :, :].rearrange("p c (h e) -> p (c h) e", e=HD),
                                       AX.X, ALU.add))
                link(dve.tensor_scalar(k_ss[:, :], k_ss[:, :], RMS_EPS, None, ALU.add))
                link(dve.tensor_scalar(k_y[:, :].bitcast(I32), k_ss[:, :].bitcast(I32), -0.5, float(0x5F3759DF),
                                       ALU.mult, ALU.add))
                for _ in range(4):
                    link(dve.tensor_tensor(k_a[:, :], k_y[:, :], k_y[:, :], ALU.mult))
                    link(dve.tensor_tensor(k_a[:, :], k_a[:, :], k_ss[:, :], ALU.mult))
                    link(dve.tensor_scalar(k_a[:, :], k_a[:, :], -0.5, 1.5, ALU.mult, ALU.add))
                    link(dve.tensor_tensor(k_y[:, :], k_y[:, :], k_a[:, :], ALU.mult))
                dve.tensor_tensor(k_tok[:, :, :].rearrange("p c (h e) -> p (c h) e", e=HD),
                                  k_tok[:, :, :].rearrange("p c (h e) -> p (c h) e", e=HD),
                                  k_y[:, :, None].broadcast_to([P, TILES * H, HD]), ALU.mult).then_inc(s_lkv.sem, 1)
                dve.wait_ge(s_qexp.sem, s_qexp.at(i, 1))
                dve.tensor_tensor(qT[:, :], q_max[:, :], q_exp[:, :], ALU.add).then_inc(s_lqT.sem, 1)
                dve.wait_ge(s_kv.sem, s_kv.at(i, 1))
                dve.tensor_tensor(kv[:, :], bank[:, 3, 0:D], blocks[:, :], ALU.mult).then_inc(s_kvm.sem, 1)
                dve.wait_ge(s_lo.sem, s_lo.at(i, 1))
                dve.wait_ge(s_nb.sem, s_nb.at(i, 2))
                link(dve.tensor_tensor(lin[:, :, :], bank[:, 5, :].rearrange("p (c d) -> p c d", c=TILES), nb[:, :, :],
                                       ALU.add))
                moments(lin)
                dve.tensor_scalar(var_in[:, 0:TILES], mv[:, :, 1], RMS_EPS, None, ALU.add).then_inc(s_var.sem, 1)
                dve.wait_ge(s_rstd.sem, s_rstd.at(i, N_LIN_OUT + 1))
                link(scale_tokens(lin, lin, 0))
                link(dve.tensor_tensor(lin[:, :, :], lin[:, :, :], l_gamma[:, None, :].broadcast_to([P, TILES, D]),
                                       ALU.mult))
                dve.wait_ge(s_xb.sem, s_xb.at(i, 1))
                dve.tensor_tensor(xr[:, :, :], lin[:, :, :], xx1[:, :, :], ALU.add).then_inc(s_x.sem, 1)
                dve.wait_ge(s_x.sem, s_x.at(i, 3))

                softmax_layer(1, xo)
            assert count[0] == DVE_LINKS, count[0]

        @block.scalar
        def _(act):
            act.wait_ge(s_w.sem, WEIGHTS)
            act.activation(a_neg[:, :, :], a_neg[:, :, :], ACT.Exp).then_inc(s_aexp, 1)
            act.wait_ge(s_aexp, 1)
            act.mul(a_neg[:, :, :], a_neg[:, :, :], -1.0).then_inc(s_aexp, 1)
            act.wait_ge(s_aexp, 2)
            act.wait_ge(s_const.sem, 1)
            with act.Fori(0, BATCH) as i:
                def evacuate(k, dst, src, scale=None):
                    act.wait_ge(s_nT.sem, s_nT.at(i, k + 1))
                    if scale is None:
                        act.activation(dst, src, ACT.Copy).then_inc(s_nTe.sem, 1)
                    else:
                        act.activation(dst, src, ACT.Copy, scale=scale).then_inc(s_nTe.sem, 1)

                evacuate(T_MAMBA, nT[:, :], bank[:, 7, :])
                for h in range(HALVES):
                    act.wait_ge(s_inp.sem, s_inp.at(i, h + 1))
                    act.activation(xpad[:, h, CONV - 1:CONV - 1 + TOK], bank[:, h, :], ACT.Copy) \
                        .then_inc(s_xpad.sem, 1)
                for h in range(HALVES):
                    act.wait_ge(s_inp.sem, s_inp.at(i, HALVES + h + 1))
                    act.activation(z_t[:, h, :], bank[:, 2 + h, :], ACT.Tanh, scale=0.5)
                    act.activation(z_h[:, h, :], bank[:, 2 + h, :], ACT.Copy, scale=0.5).then_inc(s_z.sem, 1)
                for h in range(HALVES):
                    act.wait_ge(s_cv.sem, s_cv.at(i, h + 1))
                    act.activation(cv_t[:, h, :], cv[:, h, :], ACT.Tanh, bias=conv_bh[:, h:h + 1], scale=0.5)
                    act.activation(cv_h[:, h, :], cv[:, h, :], ACT.Identity, bias=conv_bh[:, h:h + 1], scale=0.5) \
                        .then_inc(s_cvt.sem, 1)
                act.wait_ge(s_xp.sem, s_xp.at(i, 1))
                act.activation(dt_lo[96:P, :], bank[96:P, 4, :], ACT.Copy).then_inc(s_dtl.sem, 1)
                act.activation(bc_parts[0:32, :], bank[0:32, 4, :], ACT.Copy)
                act.activation(bc_hi[:, :], bank[0:96, 4, :], ACT.Copy).then_inc(s_bch.sem, 1)
                act.wait_ge(s_dtp.sem, s_dtp.at(i, 2))
                for h in range(HALVES):
                    ins = act.activation(sp_abs[:, h, :], bank[:, 5 + h, :], ACT.Abs, bias=dt_b[:, h:h + 1])
                ins.then_inc(s_abs.sem, 1)
                act.wait_ge(s_abs.sem, s_abs.at(i, 1))
                act.activation(sp_e[:, :, :], sp_abs[:, :, :], ACT.Exp, scale=-1.0).then_inc(s_spe.sem, 1)
                act.wait_ge(s_dt.sem, s_dt.at(i, 1))
                for n in range(STATE):
                    if n >= 2:
                        act.wait_ge(s_scan.sem, s_scan.at(i, n - 1))
                    for h in range(HALVES):
                        ins = act.activation(d_a[:, n % 2, h, :], dt[:, h, :], ACT.Exp, scale=a_neg[:, h, n:n + 1])
                    ins.then_inc(s_da.sem, 1)
                    act.wait_ge(s_cb.sem, s_cb.at(i, n + 1))
                    if n >= 2:
                        act.wait_ge(s_hc.sem, s_hc.at(i, n - 1))
                    act.activation(c_sb[:, n % 2, :], bank[:, 2 + n % 2, :], ACT.Copy).then_inc(s_cs.sem, 1)

                def softmax_layer(l):
                    evacuate(T_ATT[l], hT[:, :], bank[:, 7, :], f_g1[:, 0:1])
                    act.wait_ge(s_lat.sem, s_lat.at(i, l + 1))
                    act.activation(latT[0:LAT, :], bank[0:LAT, 1, :], ACT.Identity, bias=f_bdown[:, 0:1]) \
                        .then_inc(s_late.sem, 1)
                    act.wait_ge(s_kp.sem, s_kp.at(i, l + 1))
                    act.activation(ka_tok[:, :, :], bank[:, 2, :], ACT.Copy).then_inc(s_kt.sem, 1)
                    act.wait_ge(s_vp.sem, s_vp.at(i, l + 1))
                    act.activation(va_tok[:, :, :], bank[:, 3, :], ACT.Copy).then_inc(s_vt.sem, 1)
                    for c in range(TILES):
                        act.wait_ge(s_sh.sem, s_sh.at(i, tile_of(l, c)))
                        act.activation(score[:, c, :], score[:, c, :], ACT.Exp, scale=SCALE).then_inc(s_e.sem, 1)
                    act.wait_ge(s_oT.sem, s_oT.at(i, l + 1))
                    act.activation(oT[:, :], bank[:, 0, :], ACT.Copy).then_inc(s_oTe.sem, 1)
                    evacuate(T_MOE[l], hT[:, :], bank[:, 2, :], f_g2[:, 0:1])
                    act.wait_ge(s_gs.sem, s_gs.at(i, l + 1))
                    act.activation(gate[:, :, :], gate[:, :, :], ACT.Exp).then_inc(s_ge.sem, 1)

                softmax_layer(0)
                evacuate(T_LIN, nT[:, :], bank[:, 7, :])
                act.wait_ge(s_kmin.sem, s_kmin.at(i, 1))
                act.activation(k_exp[:, :, :], k_min[:, :, :], ACT.Exp).then_inc(s_kexp.sem, 1)
                act.wait_ge(s_qmin.sem, s_qmin.at(i, 1))
                act.activation(q_exp[:, :], q_min[:, :], ACT.Exp).then_inc(s_qexp.sem, 1)
                act.wait_ge(s_g.sem, s_g.at(i, 1))
                act.activation(kvo[:, :], bank[:, 4, 0:D], ACT.Copy).then_inc(s_ge2.sem, 1)
                softmax_layer(1)

        @block.tensor
        def _(pe):
            pe.wait_ge(s_w.sem, WEIGHTS)
            pe.wait_ge(s_const.sem, 1)
            with pe.Fori(0, BATCH) as i:
                def mm(out, lhsT, rhs, start=True, stop=True):
                    return pe.matmul(out, lhsT, rhs, start=start, stop=stop)

                def turn(k, src, b):
                    pe.wait_ge(s_nrm.sem, s_nrm.at(i, k + 1))
                    for c in range(TILES):
                        ins = pe.transpose(bank[:, b, P * c:P * c + P], src[:, c, :], ident[:, :])
                    ins.then_inc(s_nT.sem, 1)
                    pe.wait_ge(s_nTe.sem, s_nTe.at(i, k + 1))

                turn(T_MAMBA, nrm, 7)
                for b in range(2 * HALVES):
                    mm(bank[:, b, :], in_w[:, P * b:P * b + P], nT[:, :]).then_inc(s_inp.sem, 1)
                for h in range(HALVES):
                    pe.wait_ge(s_xc.sem, s_xc.at(i, h + 1))
                    ins = mm(bank[:, 4, :], xp_w[:, h, :], xc[:, h, :], h == 0, h == HALVES - 1)
                ins.then_inc(s_xp.sem, 1)
                pe.wait_ge(s_dtl.sem, s_dtl.at(i, 1))
                for h in range(HALVES):
                    mm(bank[:, 5 + h, :], dt_w[96:96 + RANK, P * h:P * h + P], dt_lo[96:96 + RANK, :]) \
                        .then_inc(s_dtp.sem, 1)
                pe.wait_ge(s_bcp.sem, s_bcp.at(i, 1))
                pe.wait_ge(s_z.sem, s_z.at(i, 2))
                pe.wait_ge(s_dt.sem, s_dt.at(i, 1))

                def broadcast(n):
                    if n >= 2:
                        pe.wait_ge(s_bfree.sem, s_bfree.at(i, n - 1))
                        pe.wait_ge(s_cs.sem, s_cs.at(i, n - 1))
                    mm(bank[:, n % 2, :], pickb[:, n, :], bc_parts[:, :]).then_inc(s_bb.sem, 1)
                    mm(bank[:, 2 + n % 2, :], pickb[:, STATE + n, :], bc_parts[:, :]).then_inc(s_cb.sem, 1)

                broadcast(0)
                broadcast(1)
                for n in range(STATE):
                    pe.wait_ge(s_hc.sem, s_hc.at(i, n + 1))
                    for h in range(HALVES):
                        ins = mm(bank[:, 4 + h, :], ident[:, :], hc[:, n % 2, h, :], n == 0, n == STATE - 1)
                    ins.then_inc(s_yacc.sem, 1)
                    if n + 2 < STATE:
                        broadcast(n + 2)
                pe.wait_ge(s_yg.sem, s_yg.at(i, 1))
                for c in range(TILES):
                    for h in range(HALVES):
                        ins = mm(bank[:, 6, D * c:D * c + D], sp_t[:, h, P * c:P * c + P], out_w[:, h, :],
                                 h == 0, h == HALVES - 1)
                ins.then_inc(s_mo.sem, 1)

                def softmax_layer(l):
                    turn(T_ATT[l], scaled, 7)
                    for c in range(TILES):
                        ins = mm(bank[:, 0, D * c:D * c + D], hT[:, P * c:P * c + P], f_wq[:, :])
                    ins.then_inc(s_qp.sem, 1)
                    mm(bank[0:LAT, 1, :], f_wdown[:, :], hT[:, :]).then_inc(s_lat.sem, 1)
                    pe.wait_ge(s_late.sem, s_late.at(i, l + 1))
                    for b, w, done in ((2, f_wupk, s_kp), (3, f_wupv, s_vp)):
                        for c in range(TILES):
                            ins = mm(bank[:, b, D * c:D * c + D], latT[:, P * c:P * c + P], w[:, :])
                        ins.then_inc(done.sem, 1)
                    for c in range(TILES):
                        pe.wait_ge(s_pv.sem, s_pv.at(i, tile_of(l, c)))
                        for g in range(H):
                            ins = mm(bank[:, 4, D * c:D * c + D], ident[:, :], pv[:, c % 2, g, :], g == 0, g == H - 1)
                        ins.then_inc(s_av.sem, 1)
                    pe.wait_ge(s_on.sem, s_on.at(i, l + 1))
                    for c in range(TILES):
                        ins = pe.transpose(bank[:, 0, P * c:P * c + P], o_tok[:, c, :], ident[:, :])
                    ins.then_inc(s_oT.sem, 1)
                    pe.wait_ge(s_oTe.sem, s_oTe.at(i, l + 1))
                    for c in range(TILES):
                        ins = mm(bank[:, 1, D * c:D * c + D], oT[:, P * c:P * c + P], f_wo[:, :])
                    ins.then_inc(s_wo.sem, 1)
                    turn(T_MOE[l], scaled, 2)
                    for c in range(TILES):
                        ins = mm(bank[:, 3, EXP * c:EXP * c + EXP], hT[:, P * c:P * c + P], f_wg[:, :])
                    ins.then_inc(s_gl.sem, 1)
                    pe.wait_ge(s_gs.sem, s_gs.at(i, l + 1))
                    for b in range(2 * TILES):
                        half, c = b // TILES, b % TILES
                        mm(bank[:, b, :], hT[:, P * c:P * c + P], f_we[:, 4 * D * half:4 * D * half + 4 * D]) \
                            .then_inc(s_moe.sem, 1)

                softmax_layer(0)
                turn(T_LIN, nrm, 7)
                for c in range(TILES):
                    ins = mm(bank[:, 1, D * c:D * c + D], nT[:, P * c:P * c + P], l_wk[:, :])
                ins.then_inc(s_lk.sem, 1)
                mm(bank[:, 0, :], l_wq[:, :], nT[:, :]).then_inc(s_lq.sem, 1)
                for c in range(TILES):
                    ins = mm(bank[:, 2, D * c:D * c + D], nT[:, P * c:P * c + P], l_wv[:, :])
                ins.then_inc(s_lv.sem, 1)
                pe.wait_ge(s_lkv.sem, s_lkv.at(i, 1))
                for c in range(TILES):
                    ins = mm(bank[:, 3, 0:D], v_tok[:, c, :], k_tok[:, c, :], c == 0, c == TILES - 1)
                ins.then_inc(s_kv.sem, 1)
                pe.wait_ge(s_kvm.sem, s_kvm.at(i, 1))
                mm(bank[:, 4, 0:D], kv[:, :], l_wo[:, :]).then_inc(s_g.sem, 1)
                pe.wait_ge(s_ge2.sem, s_ge2.at(i, 1))
                pe.wait_ge(s_lqT.sem, s_lqT.at(i, 1))
                for c in range(TILES):
                    ins = mm(bank[:, 5, D * c:D * c + D], qT[:, P * c:P * c + P], kvo[:, :])
                ins.then_inc(s_lo.sem, 1)
                softmax_layer(1)


_OUT = ((BATCH, TOK, D), "float32")


def kernel(**a):
    import concourse.bacc as bacc
    from concourse.bass_utils import run_bass_kernel_spmd

    a = {k: np.asarray(v) for k, v in a.items()}
    A, B, F = "L0_attn_a_", "L0_attn_b_", "L0_ffn_"

    def halves(x):
        return x.reshape((HALVES, P) + x.shape[1:]).swapaxes(0, 1)

    xp = a[A + "x_proj_w"].T
    bc = xp[:, RANK:]
    xp = np.concatenate([bc, bc, bc, xp[:, :RANK], np.zeros((xp.shape[0], 32 - RANK), xp.dtype)], axis=1)
    up = np.concatenate([a[F + "Wup"], a[F + "bup"][None]], axis=0).reshape(LAT + 1, H, 2, HD)
    arrays = {
        "x": a[A + "x"], "in_w": a[A + "in_proj_w"].T, "conv_w": halves(a[A + "conv_w"]),
        "conv_b": halves(a[A + "conv_b"]), "xp_w": halves(xp), "dt_w": a[A + "dt_proj_w"].T,
        "dt_b": halves(a[A + "dt_proj_b"]), "alog": halves(a[A + "A_log"]), "dp": halves(a[A + "Dp"]),
        "out_w": halves(a[A + "out_proj_w"].T),
        "l_wq": a[B + "Wq"], "l_bq": a[B + "bq"][:, None], "l_wk": a[B + "Wk"], "l_bk": a[B + "bk"],
        "l_wv": a[B + "Wv"], "l_bv": a[B + "bv"], "l_wo": a[B + "Wo"], "l_bo": a[B + "bo"],
        "l_gamma": a[B + "gamma"], "l_beta": a[B + "beta"],
        "f_g1": a[F + "gamma1"][:, None], "f_wq": a[F + "Wq"], "f_bq": a[F + "bq"],
        "f_wdown": a[F + "Wdown"], "f_bdown": a[F + "bdown"][:, None],
        "f_wupk": up[:, :, 0].reshape(LAT + 1, D), "f_wupv": up[:, :, 1].reshape(LAT + 1, D),
        "f_wo": a[F + "Wo"], "f_bo": a[F + "bo"], "f_g2": a[F + "gamma2"][:, None],
        "f_wg": a[F + "Wg"], "f_bg": a[F + "bg"], "f_we": a[F + "We"].transpose(1, 0, 2).reshape(D, EXP * D),
        "ident": np.eye(P, dtype=np.float32), "pick": np.tile(np.eye(32, dtype=np.float32), (3, 1)),
        "blocks": np.kron(np.eye(H, dtype=np.float32), np.ones((HD, HD), np.float32)),
    }
    nc = bacc.Bacc("TRN2", target_bir_lowering=False, num_devices=1)
    arrays = {f"in_{k}": np.ascontiguousarray(v) for k, v in arrays.items()}
    args = [nc.dram_tensor(k, v.shape, mybir.dt.from_np(v.dtype), kind="ExternalInput").ap()
            for k, v in arrays.items()]
    out = nc.dram_tensor("out", _OUT[0], FP32, kind="ExternalOutput").ap()
    hybrid_block_kernel(nc, *args, out)
    r = run_bass_kernel_spmd(nc, [arrays], core_ids=[0])
    return r.results[0]["out"]
```

```python
import numpy as np
import concourse.bass as bass
from concourse import mybir
from contextlib import ExitStack

FP32 = mybir.dt.float32
BF16 = mybir.dt.bfloat16
I32 = mybir.dt.int32
ALU = mybir.AluOpType
ACT = mybir.ActivationFunctionType
AX = mybir.AxisListType

P = 128
BATCH, TOK, D = 16, 512, 128
TILES = TOK // P
HALVES = 2
STATE = 16
CONV = 4
RANK = 8
H, HD = 16, 8
PAIRS = H * H
LAT = 64
EXP = 8
LN_EPS, RMS_EPS = 1e-5, 1e-6
SCALE = float(HD) ** -0.5

POOL_PLAN = """
m1.hc:8 m1.hc:9 c3.rstd2 m1.hc:10 m1.hc:11 m1.hc:12 m1.hc:13 m1.hc:14 m1.hc:15 l2.rstd a1.rstd m0.rstd l2.nb
a1.nb a1.xn a1.qk:0 a1.qk:1 l2.xb l2.out_rstd a1.qk:2 a1.qk:3 c2.rstd c2.nb a1.pv c2.xn c2.qk:0 c2.qk:1
m0.hc:0 m0.hc:1 a1.rstd2 m0.hc:2 m0.hc:3 m0.hc:4 c2.qk:2 m0.hc:5 c2.qk:3 m0.hc:6 c2.pv m0.hc:7
"""
VECTOR_PLAN = """
c3.total c3.o m1.bx:10 m1.scan:9 c3.x1 c3.norm2 m1.bx:11 m1.scan:10 m1.bx:12 m1.scan:11 c3.logits c3.gate
m1.bx:13 m1.scan:12 m1.bx:14 m1.scan:13 m1.bx:15 m1.scan:14 m1.scan:15 a2.y l2.norm l2.scale m1.gate m0.norm
m1.xa a1.norm c3.y a1.scale l2.k l2.q l2.k2 m0.scale l2.v a1.q l2.k_rstd l2.q2 l2.kv a1.qk:0 l2.out a1.pv:0
l2.out_scale a1.qk:1 m0.xc:0 l2.xl m0.xc:1 c2.norm a1.pv:1 a1.qk:2 m0.bc c2.scale m0.z m0.relu m0.s a1.pv:2
a1.qk:3 m0.poly:0 c2.q m0.poly:1 m0.poly:2 m0.poly:3 m0.poly:4 m0.u m0.bx:0 a1.total a1.o m0.bx:1 m0.scan:0
c2.qk:0 a1.x1 m0.bx:2 m0.scan:1 a1.norm2 m0.bx:3 m0.scan:2 c2.pv:0 m0.bx:4 a1.logits m0.scan:3 a1.gate m0.bx:5
m0.scan:4 c2.qk:1 m0.bx:6 m0.scan:5 c2.pv:1 c2.qk:2 m0.bx:7 m0.scan:6 c2.pv:2 c2.qk:3 m0.bx:8 m0.scan:7
m0.bx:9 m0.scan:8
"""
SCALAR_PLAN = """
m1.c:9 c3.oT m1.decay:10 m1.c:10 a2.gatedT:5 m1.decay:11 a2.gated:6 m1.c:11 c3.h2 m1.decay:12 c3.h2T m1.c:12
a2.gatedT:6 c3.gate a2.gated:7 c3.gated:0 m1.decay:13 m1.c:13 c3.gatedT:0 c3.gated:1 m1.decay:14 m1.c:14
a2.gatedT:7 c3.gatedT:1 c3.gated:2 m1.decay:15 c3.gatedT:2 c3.gated:3 c3.gatedT:3 c3.gated:4 m1.c:15
c3.gatedT:4 c3.gated:5 c3.gatedT:5 c3.gated:6 l2.nrm c3.gatedT:6 c3.gated:7 c3.gatedT:7 l2.nT a1.scaled
l2.k_exp a1.nrm a1.hT m0.keep l2.q_exp a1.lat a1.k m0.nrm l2.kvo a1.v m0.nT m0.xpad:0 a1.prob:0 m0.xpad:1
l2.out_nrm m0.conv:0 m0.conv:1 a1.prob:1 m0.z:0 m0.z:1 m0.dt_low m0.bc m0.abs m0.exp a1.prob:2 c2.scaled
c2.nrm c2.hT c2.lat m0.s2 a1.prob:3 c2.k m0.decay:0 m0.c:0 m0.decay:1 a1.oT m0.c:1 m0.decay:2 c2.v c2.prob:0
m0.c:2 m0.decay:3 m0.c:3 a1.h2 a1.h2T m0.decay:4 m0.c:4 a1.gate a1.gated:0 m0.decay:5 m0.c:5 a1.gatedT:0
a1.gated:1 c2.prob:1 m0.decay:6 m0.c:6 a1.gatedT:1 a1.gated:2 a1.gatedT:2 a1.gated:3 m0.decay:7 c2.prob:2
a1.gatedT:3 a1.gated:4 a1.gatedT:4 m0.c:7 c2.prob:3 m0.decay:8 a1.gated:5 m0.c:8 m0.decay:9
"""
TENSOR_PLAN = """
c3.sum:3 m1.add:7 m1.bc:10 c3.o a2.expert:3 c3.o_proj a2.gated:5 m1.add:8 m1.bc:11 a2.expert:4 m1.add:9
m1.bc:12 c3.h2 a2.gated:6 c3.logits a2.expert:5 m1.add:10 m1.bc:13 a2.gated:7 c3.gated:0 m1.add:11 m1.bc:14
a2.expert:6 c3.gated:1 c3.expert:0 m1.add:12 m1.bc:15 c3.gated:2 c3.expert:1 m1.add:13 c3.gated:3 a2.expert:7
c3.expert:2 c3.gated:4 c3.expert:3 m1.add:14 c3.gated:5 m1.add:15 c3.expert:4 c3.gated:6 c3.expert:5 m1.out
c3.gated:7 c3.expert:6 c3.expert:7 l2.turn l2.k l2.q a1.turn l2.v a1.lat a1.q a1.k a1.v m0.turn l2.kv l2.kvp
l2.out m0.in:0 m0.in:1 m0.conv:0 m0.conv:1 a1.sum:0 m0.z:0 m0.z:1 m0.xp m0.dt c2.turn c2.lat c2.q m0.bc:0 c2.k
a1.sum:1 a1.sum:2 a1.sum:3 m0.bc:1 a1.o a1.o_proj m0.bc:2 c2.v m0.add:0 m0.bc:3 m0.add:1 m0.bc:4 a1.h2
a1.logits m0.add:2 m0.bc:5 c2.sum:0 a1.gated:0 m0.add:3 m0.bc:6 a1.gated:1 m0.add:4 m0.bc:7 a1.expert:0
a1.gated:2 a1.expert:1 c2.sum:1 a1.gated:3 a1.expert:2 m0.add:5 a1.gated:4 c2.sum:2 m0.bc:8 m0.add:6 m0.bc:9
"""
MOST_BEHIND = max(int(name[1:name.index(".")]) for name in (POOL_PLAN + VECTOR_PLAN + SCALAR_PLAN + TENSOR_PLAN).split())
LOOP_FROM = MOST_BEHIND + 2
STORE_BEHIND = 3


def parse(name):
    layer, behind, (step, _, k) = name[0], int(name[1:name.index(".")]), name[name.index(".") + 1:].partition(":")
    return layer, behind, step, int(k) if k else None


POOL_TILE = TILES - 1

_z = (0.5 - 0.5 * np.cos(np.pi * (np.arange(400) + 0.5) / 400)) / 9
ATANH = [float(c) for c in np.polynomial.Polynomial.fit(
    _z, np.arctanh(np.sqrt(_z)) / np.sqrt(_z) / 2, 4, domain=[0, 1 / 9]).convert().coef]


def hybrid_block_kernel(nc, x_d, in_w_d, conv_w_d, conv_b_d, xp_w_d, dt_w_d, dt_b_d, alog_d, dp_d, out_w_d,
                        l_wq_d, l_bq_d, l_wk_d, l_bk_d, l_wv_d, l_bv_d, l_wo_d, l_bo_d, l_gamma_d, l_beta_d,
                        f_g1_d, f_wq_d, f_bq_d, f_wdown_d, f_bdown_d, f_wupk_d, f_wupv_d, f_wo_d, f_bo_d,
                        f_g2_d, f_wg_d, f_bg_d, f_we_d, ident_d, pick_d, blocks_d, y_d):
    ctx = ExitStack()
    with ctx:
        def sb(name, shape, dt=FP32):
            return ctx.enter_context(nc.sbuf_tensor(name, shape, dt))

        class Signal:

            def __init__(self, name, per):
                self.sem, self.per = ctx.enter_context(nc.semaphore(name)), per

            def at(self, b, k=None):
                return b * self.per + (self.per if k is None else k)

        def began(b):
            return not (isinstance(b, int) and b < 0)

        ident = sb("ident", [P, P])
        pick = sb("pick", [96, 32])
        pickb = sb("pickb", [96, 32, P], BF16)
        blocks = sb("blocks", [P, P])
        in_w = sb("in_w", [P, 2 * HALVES * P])
        conv_w = sb("conv_w", [P, HALVES, CONV])
        conv_d = sb("conv_d", [P, HALVES, CONV, P])
        conv_b = sb("conv_b", [P, HALVES])
        conv_bh = sb("conv_bh", [P, HALVES])
        xp_w = sb("xp_w", [P, HALVES, P])
        dt_w = sb("dt_w", [P, HALVES * P])
        dt_b = sb("dt_b", [P, HALVES])
        a_neg = sb("a_neg", [P, HALVES, STATE])
        dp = sb("dp", [P, HALVES])
        out_w = sb("out_w", [P, HALVES, D])
        l_wq, l_wk, l_wv, l_wo = (sb(n, [P, D]) for n in ("l_wq", "l_wk", "l_wv", "l_wo"))
        l_bq = sb("l_bq", [P, 1])
        l_bk, l_bv, l_bo, l_gamma, l_beta = (sb(n, [P, D]) for n in ("l_bk", "l_bv", "l_bo", "l_gamma", "l_beta"))
        f_g1, f_g2 = (sb(n, [P, 1]) for n in ("f_g1", "f_g2"))
        f_bq = sb("f_bq", [P, D])
        f_wq = sb("f_wq", [P, D])
        f_wdown = sb("f_wdown", [P, LAT])
        f_bdown = sb("f_bdown", [LAT, 1])
        f_wupk = sb("f_wupk", [LAT + 1, D])
        f_wupv = sb("f_wupv", [LAT + 1, D])
        f_wo = sb("f_wo", [P, D])
        f_bo = sb("f_bo", [P, D])
        f_wg = sb("f_wg", [P, EXP])
        f_bg = sb("f_bg", [P, EXP])
        f_we = sb("f_we", [P, EXP, D])
        minus_half = sb("minus_half", [P, 2 * TILES])
        half_ln2 = sb("half_ln2", [P, 1])
        spare = sb("spare", [P, 1])

        xin = sb("xin", [P, TILES, D])
        xkeep = sb("xkeep", [P, TILES, D])
        xpad = sb("xpad", [P, HALVES, CONV - 1 + TOK])
        xc = sb("xc", [P, HALVES, TOK])
        z_h = sb("z_h", [P, HALVES, TOK])
        bc_hi = sb("bc_hi", [96, TOK], BF16)
        bc_parts = sb("bc_parts", [96, TOK], BF16)
        sp_e = sb("sp_e", [P, HALVES, TOK])
        sp_t = sb("sp_t", [P, HALVES, TOK])
        dt = sb("dt", [P, HALVES, TOK])
        u = sb("u", [P, HALVES, TOK])
        d_a = sb("d_a", [P, 2, HALVES, TOK])
        d_bx = sb("d_bx", [P, 2, HALVES, TOK])
        hs = sb("hs", [P, 2, HALVES, TOK])
        c_sb = sb("c_sb", [P, 2, TOK])
        hc = sb("hc", [P, 2, HALVES, TOK])
        cv_t, cv_h, sp_z = sp_t, u, dt
        bc_mid = bc_hi
        m_nrm = hc[:, 1, 0, :].rearrange("p (c d) -> p c d", c=TILES)
        m_nT, z_t, sp_max = hs[:, 0, 0, :], hc[:, 0, :, :], d_bx[:, 0, :, :]
        bc_rest, dt_lo = d_a[0:96, 0, 0, :], d_a[:, 1, 0, :]
        xa = sb("xa", [P, TILES, D])
        xb = sb("xb", [P, TILES, D])
        xl = sb("xl", [P, TILES, D])
        xo = sb("xo", [P, TILES, D])

        bank = ctx.enter_context(nc.psum_tensor("bank", [P, 8, 512], FP32))

        class Norm:

            def __init__(self, name, rises):
                self.stats = sb(name + "_stats", [P, TILES, 6])
                self.mv = sb(name + "_mv", [P, TILES, 2])
                self.var = sb(name + "_var", [P, 2 * TILES])
                self.rstd = sb(name + "_rstd", [P, 2 * TILES])
                self.shift = sb(name + "_shift", [P, 2 * TILES])
                self.var_ready = Signal(name + "_var_ready", rises)
                self.rstd_ready = Signal(name + "_rstd_ready", rises)

        class Attention:

            def __init__(self, name, x, y, banks):
                self.x, self.y, self.banks, self.name = x, y, banks, name
                self.norm = Norm(name, 2)
                self.scaled = sb(name + "_scaled", [P, TILES, D])
                self.nrm = sb(name + "_nrm", [P, TILES, D])
                self.hT = sb(name + "_hT", [P, TOK])
                self.latT = sb(name + "_latT", [LAT + 1, TOK])
                self.q = sb(name + "_q", [P, TILES, D])
                self.gatedT = sb(name + "_k_v", [P, 2, TOK])
                self.k, self.v = (self.gatedT[:, i, :].rearrange("p (c d) -> p c d", c=TILES) for i in range(2))
                self.score = sb(name + "_score", [P, TILES, PAIRS])
                self.peak = sb(name + "_peak", [P, TILES, H])
                self.total = sb(name + "_total", [P, TILES, H])
                self.rec = sb(name + "_rec", [P, TILES, H])
                self.nb = sb(name + "_nb", [P, TILES, D])
                self.xn = sb(name + "_xn", [P, TILES, D])
                self.x1 = sb(name + "_x1", [P, TILES, D])
                self.gate = sb(name + "_gate", [P, TILES, EXP])
                self.g_max = sb(name + "_g_max", [P, TILES])
                self.g_sum = sb(name + "_g_sum", [P, TILES])
                self.o, self.oT, self.h2, self.xx1 = self.q, self.hT, self.scaled, self.xn
                self.h2T = self.hT
                self.gated = self.score[:, :, :].rearrange("p c (s d) -> p (c s) d", d=D) \
                    .rearrange("p (u c) d -> p u c d", u=2)
                self.signals = {}
                for signal, per in (("scales_ready", 1), ("normalized", 1), ("nrm_ready", 1), ("turned", 1), ("hT_ready", 1),
                                    ("q_projected", 1), ("q_ready", 1), ("lat_projected", 1), ("lat_ready", 1),
                                    ("k_projected", 1), ("k_ready", 1), ("v_projected", 1), ("v_ready", 1),
                                    ("qk_ready", TILES), ("score_ready", TILES), ("shifted", TILES),
                                    ("prob_ready", TILES), ("pv_ready", TILES - 1), ("pool_pv_ready", 1),
                                    ("pv_summed", TILES), ("o_ready", 1), ("o_turned", 1), ("oT_ready", 1),
                                    ("o_projected", 1), ("nb_ready", 1), ("xn_ready", 1), 
                                    ("xx1_ready", 1), ("h2_ready", 1), ("h2_turned", 1), ("h2T_ready", 1),
                                    ("logits_ready", 1), ("logits_shifted", 1), ("gate_exp_ready", 1),
                                    ("gate_ready", 1), ("gated_ready", EXP), ("gated_turned", EXP),
                                    ("gatedT_ready", EXP), ("expert_added", EXP), ("y_ready", 1)):
                    self.signals[signal] = Signal(name + "_" + signal, per)

            def __getitem__(self, signal):
                return self.signals[signal]

        m_norm, li_norm, lo_norm = Norm("m", 1), Norm("li", 1), Norm("lo", 1)
        first = Attention("a", xa, xb, (4, 5))
        second = Attention("c", xl, xo, (6, 7))
        qk = sb("qk", [P, 2, PAIRS * HD])
        pv = sb("pv", [P, 2, H, D])
        l_nrm, l_nT = second.nrm, sb("l_nT", [P, TOK])
        l_nb, l_xb = second.nb, second.xn
        q_min, q_max = sb("q_min", [P, TOK]), sb("q_max", [P, TOK])
        k_tok = sb("k_tok", [P, TILES, D])
        k_min = sb("k_min", [P, TILES, D])
        k_ss, k_y, k_a = (sb(n, [P, TILES * H]) for n in ("k_ss", "k_y", "k_a"))
        q_exp, qT, k_exp, k_sq = q_min, q_max, k_min, k_min
        v_tok = sb("v_tok", [P, TILES, D])
        kv = sb("kv", [P, D])
        kvo = sb("kvo", [P, D])
        lin = l_nT[:, :].rearrange("p (c d) -> p c d", c=TILES)

        s_w = Signal("weights_loaded", 0)
        s_const = Signal("constants_made", 0)
        s_pool_const = Signal("pool_constants_made", 0)
        s_rates = Signal("decay_rates_ready", 0)
        s_xin = Signal("x_loaded", 16)
        s_out = Signal("y_stored", 16)
        s_xkeep = Signal("x_kept", 1)
        s_mscale = Signal("m_scales_ready", 1)
        s_mnrm = Signal("m_normalized", 1)
        s_mturn = Signal("m_turned", 1)
        s_mnT = Signal("m_nT_ready", 1)
        s_inp = Signal("x_in_projected", HALVES)
        s_xpad = Signal("x_padded", HALVES)
        s_conv = Signal("convolved", HALVES)
        s_cvt = Signal("conv_tanh_ready", HALVES)
        s_xc = Signal("xc_ready", HALVES)
        s_zp = Signal("z_projected", HALVES)
        s_z = Signal("z_tanh_ready", HALVES)
        s_xp = Signal("x_projected", 1)
        s_dtl = Signal("dt_low_ready", 1)
        s_bch = Signal("bc_high_ready", 1)
        s_bcp = Signal("bc_parts_ready", 1)
        s_dtp = Signal("dt_projected", 1)
        s_abs = Signal("softplus_abs_ready", 1)
        s_spe = Signal("softplus_exp_ready", 1)
        s_sps = Signal("softplus_s_ready", 1)
        s_spz = Signal("softplus_s2_ready", 1)
        s_dt = Signal("dt_ready", 1)
        s_u = Signal("u_ready", 1)
        s_da = Signal("decay_ready", STATE)
        s_bb = Signal("b_broadcast", STATE)
        s_bx = Signal("b_consumed", STATE)
        s_cb = Signal("c_broadcast", STATE)
        s_cs = Signal("c_in_sbuf", STATE)
        s_scan = Signal("scanned", STATE)
        s_hc = Signal("h_times_c", STATE)
        s_yacc = Signal("y_accumulated", STATE)
        s_yg = Signal("y_gated", 1)
        s_mo = Signal("mamba_projected", 1)
        s_xa = Signal("xa_ready", 1)
        s_lscale = Signal("l_scales_ready", 1)
        s_lnrm = Signal("l_normalized", 1)
        s_lturn = Signal("l_turned", 1)
        s_lnT = Signal("l_nT_ready", 1)
        s_lk = Signal("lin_k_projected", 1)
        s_lq = Signal("lin_q_projected", 1)
        s_lv = Signal("lin_v_projected", 1)
        s_kmin = Signal("k_min_ready", 1)
        s_kexp = Signal("k_exp_ready", 1)
        s_qmin = Signal("q_min_ready", 1)
        s_qexp = Signal("q_exp_ready", 1)
        s_vr = Signal("lin_v_ready", 1)
        s_kr = Signal("k_normed", 1)
        s_qr = Signal("lin_q_ready", 1)
        s_kv = Signal("kv_summed", 1)
        s_kvm = Signal("kv_masked", 1)
        s_kvp = Signal("kv_projected", 1)
        s_kvo = Signal("kvo_ready", 1)
        s_lo = Signal("lin_projected", 1)
        s_lin = Signal("lin_moments_ready", 1)
        s_lon = Signal("lin_normalized", 1)
        s_lnb = Signal("lin_nb_ready", 1)
        s_lxb = Signal("x_plus_beta", 1)
        s_xl = Signal("xl_ready", 1)

        loads = [(ident[:, :], ident_d), (pick[:, :], pick_d), (in_w[:, :], in_w_d), (conv_w[:, :, :], conv_w_d),
                 (conv_b[:, :], conv_b_d), (xp_w[:, :, :], xp_w_d), (dt_w[96:96 + RANK, :], dt_w_d),
                 (dt_b[:, :], dt_b_d), (a_neg[:, :, :], alog_d), (dp[:, :], dp_d), (out_w[:, :, :], out_w_d),
                 (l_wq[:, :], l_wq_d), (l_wk[:, :], l_wk_d), (l_wv[:, :], l_wv_d), (l_wo[:, :], l_wo_d),
                 (l_bq[:, :], l_bq_d), (f_g1[:, :], f_g1_d), (f_g2[:, :], f_g2_d), (f_wq[:, :], f_wq_d),
                 (f_wdown[:, :], f_wdown_d), (f_bdown[:, :], f_bdown_d), (f_wupk[:, :], f_wupk_d),
                 (f_wupv[:, :], f_wupv_d), (f_wo[:, :], f_wo_d), (f_wg[:, :], f_wg_d), (f_we[:, :, :], f_we_d)]
        for t, s in ((l_bk, l_bk_d), (l_bv, l_bv_d), (l_bo, l_bo_d), (l_gamma, l_gamma_d), (l_beta, l_beta_d),
                     (f_bo, f_bo_d), (f_bq, f_bq_d), (f_bg, f_bg_d)):
            loads.append((t[:, :], s.partition_broadcast(P)))
        WEIGHTS = 16 * len(loads)

        def by_tile(b):
            return bank[:, b, :].rearrange("p (c d) -> p c d", c=TILES)

        def by_head(t):
            return t.rearrange("p (h e) -> p h e", e=HD)

        def over_tiles(row):
            return row[:, None, :].broadcast_to([P, TILES, D])

        def rounds(eng, plan, mamba, linear, attention):
            def one(r):
                for name in plan.split():
                    layer, behind, step, k = parse(name)
                    b = r - behind
                    if isinstance(r, int) and not 0 <= b < BATCH:
                        continue
                    if layer == "m":
                        mamba(b, step, k)
                    elif layer == "l":
                        linear(b, step, k)
                    else:
                        attention(first if layer == "a" else second, b, step, k)

            for r in range(LOOP_FROM):
                one(r)
            with eng.Fori(LOOP_FROM, BATCH) as r:
                one(r)
            for r in range(BATCH, BATCH + MOST_BEHIND):
                one(r)

        block = ctx.enter_context(nc.Block())

        @block.sync
        def _(sp):
            for t, s in loads:
                sp.dma_start(t, s).then_inc(s_w.sem, 16)
            sp.dma_start(blocks[:, :], blocks_d).then_inc(s_out.sem, 16)

            def load(b):
                sp.dma_start(xin[:, :, :], x_d[bass.ds(b, 1), :, :].rearrange("o (c p) d -> p (o c) d", p=P)) \
                    .then_inc(s_xin.sem, 16)

            def next_load(r):
                sp.wait_ge(s_xkeep.sem, s_xkeep.at(r))
                sp.wait_ge(s_mnrm.sem, s_mnrm.at(r))
                load(r + 1)

            def store(b):
                sp.wait_ge(second["y_ready"].sem, second["y_ready"].at(b))
                sp.dma_start(y_d[bass.ds(b, 1), :, :].rearrange("o (c p) d -> p (o c) d", p=P), xo[:, :, :]) \
                    .then_inc(s_out.sem, 16)

            load(0)
            for r in range(LOOP_FROM):
                next_load(r)
                if r >= STORE_BEHIND:
                    store(r - STORE_BEHIND)
            with sp.Fori(LOOP_FROM, BATCH - 1) as r:
                next_load(r)
                store(r - STORE_BEHIND)
            for b in range(BATCH - 1 - STORE_BEHIND, BATCH):
                store(b)
            sp.wait_ge(s_out.sem, 16 * (BATCH + 1))

        def products(eng, a, c):
            return eng.tensor_tensor(
                pv[:, c % 2, :, :].rearrange("p g (h e) -> p g h e", e=HD),
                a.score[:, c, :].rearrange("p (h g) -> p g h", g=H)[:, :, :, None].broadcast_to([P, H, H, HD]),
                by_head(a.v[:, c, :])[:, :, None, :].broadcast_to([P, H, H, HD]), ALU.mult)

        @block.gpsimd
        def _(pool):
            pool.memset(minus_half[:, :], -0.5)
            pool.memset(half_ln2[:, :], 0.5 * float(np.log(2.0)))
            pool.memset(xpad[:, :, 0:CONV - 1], 0.0).then_inc(s_pool_const.sem, 1)
            pool.wait_ge(s_pool_const.sem, 1)
            pool.wait_ge(s_w.sem, WEIGHTS)

            def rsqrt(norm, b, k, n):
                pool.wait_ge(norm.var_ready.sem, norm.var_ready.at(b, k))
                pool.tensor_tensor(norm.rstd[:, 0:n], norm.var[:, 0:n], minus_half[:, 0:n], ALU.pow) \
                    .then_inc(norm.rstd_ready.sem, 1)

            def mamba(b, step, k):
                if step == "rstd":
                    rsqrt(m_norm, b, 1, TILES)
                if step == "hc":
                    pool.wait_ge(s_cs.sem, s_cs.at(b, k + 1))
                    pool.wait_ge(s_scan.sem, s_scan.at(b, k + 1))
                    if k >= 2:
                        pool.wait_ge(s_yacc.sem, s_yacc.at(b, k - 1))
                    else:
                        if began(b - 1):
                            pool.wait_ge(s_yacc.sem, s_yacc.at(b - 1))
                    pool.tensor_tensor(hc[:, k % 2, :, :], hs[:, k % 2, :, :],
                                       c_sb[:, k % 2, None, :].broadcast_to([P, HALVES, TOK]), ALU.mult) \
                        .then_inc(s_hc.sem, 1)

            def linear(b, step, k):
                if step == "rstd":
                    rsqrt(li_norm, b, 1, TILES)
                if step == "nb":
                    pool.wait_ge(s_lnrm.sem, s_lnrm.at(b))
                    if began(b - 1):
                        pool.wait_ge(second["xx1_ready"].sem, second["xx1_ready"].at(b - 1))
                    pool.tensor_tensor(l_nb[:, :, :], l_nrm[:, :, :], over_tiles(l_bo), ALU.add) \
                        .then_inc(s_lnb.sem, 1)
                if step == "xb":
                    if began(b - 1):
                        pool.wait_ge(second["y_ready"].sem, second["y_ready"].at(b - 1))
                    pool.tensor_tensor(l_xb[:, :, :], xb[:, :, :], over_tiles(l_beta), ALU.add).then_inc(s_lxb.sem, 1)
                if step == "out_rstd":
                    rsqrt(lo_norm, b, 1, TILES)

            def attention(a, b, step, k):
                if step == "rstd":
                    rsqrt(a.norm, b, 1, 2 * TILES)
                if step == "nb":
                    pool.wait_ge(a["nrm_ready"].sem, a["nrm_ready"].at(b))
                    if a is second:
                        pool.wait_ge(s_lin.sem, s_lin.at(b))
                        pool.wait_ge(s_xl.sem, s_xl.at(b))
                    else:
                        if began(b - 1):
                            pool.wait_ge(a["xx1_ready"].sem, a["xx1_ready"].at(b - 1))
                        if began(b - 1):
                            pool.wait_ge(a["y_ready"].sem, a["y_ready"].at(b - 1))
                    pool.tensor_tensor(a.nb[:, :, :], a.nrm[:, :, :], over_tiles(f_bo), ALU.add) \
                        .then_inc(a["nb_ready"].sem, 1)
                if step == "xn":
                    pool.wait_ge(a["nb_ready"].sem, a["nb_ready"].at(b))
                    pool.tensor_tensor(a.xn[:, :, :], a.x[:, :, :], a.nb[:, :, :], ALU.add) \
                        .then_inc(a["xn_ready"].sem, 1)
                c = k
                if step == "qk":
                    if c == 0:
                        pool.wait_ge(a["q_ready"].sem, a["q_ready"].at(b))
                        pool.wait_ge(a["k_ready"].sem, a["k_ready"].at(b))
                        if a is first:
                            if began(b - 2):
                                pool.wait_ge(second["score_ready"].sem, second["score_ready"].at(b - 2))
                        elif not (isinstance(b, int) and b + 1 >= BATCH):
                            pool.wait_ge(first["score_ready"].sem, first["score_ready"].at(b + 1))
                    if c >= 2:
                        pool.wait_ge(a["score_ready"].sem, a["score_ready"].at(b, c - 1))
                    pool.tensor_tensor(
                        qk[:, c % 2, :].rearrange("p (h g e) -> p h g e", h=H, g=H),
                        by_head(a.q[:, c, :])[:, :, None, :].broadcast_to([P, H, H, HD]),
                        a.k[:, c, None, :].broadcast_to([P, H, D]).rearrange("p h (g e) -> p h g e", e=HD),
                        ALU.mult).then_inc(a["qk_ready"].sem, 1)
                if step == "pv":
                    pool.wait_ge(a["prob_ready"].sem, a["prob_ready"].at(b, POOL_TILE + 1))
                    pool.wait_ge(a["pv_summed"].sem, a["pv_summed"].at(b, POOL_TILE - 1))
                    products(pool, a, POOL_TILE).then_inc(a["pool_pv_ready"].sem, 1)
                if step == "rstd2":
                    rsqrt(a.norm, b, 2, TILES)

            rounds(pool, POOL_PLAN, mamba, linear, attention)

        @block.vector
        def _(dve):
            for a in (first, second):
                dve.memset(a.latT[LAT:LAT + 1, :], 1.0)
            dve.wait_ge(s_pool_const.sem, 1)
            dve.wait_ge(s_w.sem, WEIGHTS)
            dve.wait_ge(s_out.sem, 16)
            dve.tensor_copy(pickb[:, :, :], pick[:, :, None].broadcast_to([96, 32, P]))
            for h in range(HALVES):
                for t in range(CONV):
                    dve.tensor_scalar(conv_d[:, h, t, :], ident[:, :], conv_w[:, h, t:t + 1], None, ALU.mult)
            dve.tensor_scalar(conv_bh[:, :], conv_b[:, :], 0.5, None, ALU.mult).then_inc(s_const.sem, 1)

            class Chain(Signal):
                count = 0

            m_steps, l_steps = Chain("mamba_steps", 10), Chain("linear_steps", 28)
            steps = {first: Chain("a_steps", 15), second: Chain("c_steps", 15)}

            def link(chain, b, ins):
                chain.count = chain.count % chain.per + 1
                ins.then_inc(chain.sem, 1)
                dve.wait_ge(chain.sem, chain.at(b, chain.count))

            def moments(chain, b, norm, src):
                for c in range(TILES):
                    ins = dve.bn_stats(norm.stats[:, c, :], src[:, c, :])
                link(chain, b, ins)
                dve.memset(spare[:, :], 0.0)
                for c in range(TILES):
                    ins = dve.bn_aggr(norm.mv[:, c, :], norm.stats[:, c, :])
                link(chain, b, ins)

            def scales(norm, b, k, kinds, done):
                dve.wait_ge(norm.rstd_ready.sem, norm.rstd_ready.at(b, k))
                dve.scalar_tensor_tensor(
                    norm.shift[:, 0:kinds * TILES].rearrange("p (a c) -> p a c", a=kinds),
                    norm.mv[:, None, :, 0].broadcast_to([P, kinds, TILES]), -1.0,
                    norm.rstd[:, 0:kinds * TILES].rearrange("p (a c) -> p a c", a=kinds),
                    ALU.mult, ALU.mult).then_inc(done.sem, 1)

            def input_of(b, k):
                dve.wait_ge(s_bb.sem, s_bb.at(b, k + 1))
                if k >= 2:
                    dve.wait_ge(s_scan.sem, s_scan.at(b, k - 1))
                dve.tensor_tensor(d_bx[:, k % 2, :, :], u[:, :, :],
                                  bank[:, 0, None, :].broadcast_to([P, HALVES, TOK]), ALU.mult) \
                    .then_inc(s_bx.sem, 1)

            def mamba(b, step, k):
                if step == "norm":
                    dve.wait_ge(s_xin.sem, s_xin.at(b))
                    moments(m_steps, b, m_norm, xin)
                    dve.tensor_scalar(m_norm.var[:, 0:TILES], m_norm.mv[:, :, 1], LN_EPS, None, ALU.add) \
                        .then_inc(m_norm.var_ready.sem, 1)
                if step == "scale":
                    scales(m_norm, b, 1, 1, s_mscale)
                if step == "xc":
                    h = k
                    dve.wait_ge(s_cvt.sem, s_cvt.at(b, h + 1))
                    dve.scalar_tensor_tensor(xc[:, h, :], cv_t[:, h, :], 1.0, cv_h[:, h, :],
                                             ALU.add, ALU.mult).then_inc(s_xc.sem, 1)
                if step == "bc":
                    dve.wait_ge(s_bch.sem, s_bch.at(b))
                    link(m_steps, b, dve.tensor_tensor(bc_rest[:, :], bank[0:96, 1, :], bc_hi[:, :], ALU.subtract))
                    dve.tensor_copy(bc_parts[32:64, :], bc_rest[32:64, :])
                    link(m_steps, b, dve.tensor_copy(bc_mid[64:96, :], bc_rest[64:96, :]))
                    dve.tensor_tensor(bc_parts[64:96, :], bc_rest[64:96, :], bc_mid[64:96, :], ALU.subtract) \
                        .then_inc(s_bcp.sem, 1)
                if step == "z":
                    dve.wait_ge(s_z.sem, s_z.at(b))
                    dve.scalar_tensor_tensor(z_h[:, :, :], z_t[:, :, :], 1.0, z_h[:, :, :], ALU.add, ALU.mult)
                if step == "relu":
                    dve.wait_ge(s_spe.sem, s_spe.at(b))
                    for h in range(HALVES):
                        dve.tensor_scalar(sp_max[:, h, :], bank[:, 2 + h, :], dt_b[:, h:h + 1], 0.0,
                                          ALU.add, ALU.max)
                if step == "s":
                    dve.scalar_tensor_tensor(sp_e[:, :, :], sp_t[:, :, :], 1.0, sp_e[:, :, :], ALU.add, ALU.mult) \
                        .then_inc(s_sps.sem, 1)
                if step == "poly":
                    if k == 0:
                        dve.wait_ge(s_spz.sem, s_spz.at(b))
                        link(m_steps, b, dve.tensor_scalar(sp_t[:, :, :], sp_z[:, :, :], ATANH[-1], None, ALU.mult))
                    elif k < len(ATANH) - 1:
                        q = ATANH[-1 - k]
                        link(m_steps, b, dve.scalar_tensor_tensor(sp_t[:, :, :], sp_t[:, :, :], q, sp_z[:, :, :],
                                                      ALU.add, ALU.mult))
                    else:
                        link(m_steps, b, dve.scalar_tensor_tensor(sp_t[:, :, :], sp_t[:, :, :], ATANH[0],
                                                                  sp_e[:, :, :], ALU.add, ALU.mult))
                if step == "u":
                    dve.tensor_tensor(dt[:, :, :], sp_t[:, :, :], sp_max[:, :, :], ALU.add).then_inc(s_dt.sem, 1)
                    dve.wait_ge(s_dt.sem, s_dt.at(b))
                    dve.tensor_tensor(u[:, :, :], dt[:, :, :], xc[:, :, :], ALU.mult).then_inc(s_u.sem, 1)
                    dve.wait_ge(s_u.sem, s_u.at(b))
                if step == "bx":
                    input_of(b, k)
                if step == "scan":
                    dve.wait_ge(s_bx.sem, s_bx.at(b, k + 1))
                    dve.wait_ge(s_da.sem, s_da.at(b, k + 1))
                    if k >= 2:
                        dve.wait_ge(s_hc.sem, s_hc.at(b, k - 1))
                    for h in range(HALVES):
                        ins = dve.tensor_tensor_scan(hs[:, k % 2, h, :], d_a[:, k % 2, h, :], d_bx[:, k % 2, h, :],
                                                     0.0, ALU.mult, ALU.add)
                    ins.then_inc(s_scan.sem, 1)
                if step == "gate":
                    dve.wait_ge(s_yacc.sem, s_yacc.at(b))
                    for h in range(HALVES):
                        ins = dve.scalar_tensor_tensor(sp_e[:, h, :], xc[:, h, :], dp[:, h:h + 1], bank[:, 2 + h, :],
                                                       ALU.mult, ALU.add)
                    link(m_steps, b, ins)
                    dve.tensor_tensor(sp_e[:, :, :], sp_e[:, :, :], z_h[:, :, :], ALU.mult).then_inc(s_yg.sem, 1)
                if step == "xa":
                    dve.wait_ge(s_mo.sem, s_mo.at(b))
                    if began(b - 1):
                        dve.wait_ge(first["xn_ready"].sem, first["xn_ready"].at(b - 1))
                    dve.tensor_tensor(xa[:, :, :], by_tile(2), xkeep[:, :, :], ALU.add).then_inc(s_xa.sem, 1)

            def linear(b, step, k):
                if step == "norm":
                    dve.wait_ge(first["y_ready"].sem, first["y_ready"].at(b))
                    moments(l_steps, b, li_norm, xb)
                    dve.tensor_scalar(li_norm.var[:, 0:TILES], li_norm.mv[:, :, 1], LN_EPS, None, ALU.add) \
                        .then_inc(li_norm.var_ready.sem, 1)
                if step == "scale":
                    scales(li_norm, b, 1, 1, s_lscale)
                if step == "k":
                    dve.wait_ge(s_lk.sem, s_lk.at(b))
                    link(l_steps, b, dve.tensor_tensor(k_tok[:, :, :], by_tile(7), over_tiles(l_bk), ALU.add))
                    dve.tensor_scalar(k_min[:, :, :], k_tok[:, :, :], 0.0, None, ALU.min).then_inc(s_kmin.sem, 1)
                if step == "q":
                    dve.wait_ge(s_lq.sem, s_lq.at(b))
                    dve.tensor_scalar(q_max[:, :], bank[:, 6, :], l_bq[:, 0:1], 0.0, ALU.add, ALU.max)
                    dve.tensor_scalar(q_min[:, :], bank[:, 6, :], l_bq[:, 0:1], 0.0, ALU.add, ALU.min) \
                        .then_inc(s_qmin.sem, 1)
                if step == "k2":
                    dve.wait_ge(s_kexp.sem, s_kexp.at(b))
                    link(l_steps, b, dve.scalar_tensor_tensor(k_tok[:, :, :], k_tok[:, :, :], 0.0, k_exp[:, :, :],
                                                  ALU.max, ALU.add))
                    link(l_steps, b, dve.tensor_tensor(k_sq[:, :, :], k_tok[:, :, :], k_tok[:, :, :], ALU.mult))
                    link(l_steps, b, dve.tensor_reduce(k_ss[:, :], k_sq[:, :, :].rearrange("p c (h e) -> p (c h) e", e=HD),
                                           AX.X, ALU.add))
                    link(l_steps, b, dve.tensor_scalar(k_ss[:, :], k_ss[:, :], RMS_EPS, None, ALU.add))
                if step == "v":
                    dve.wait_ge(s_lv.sem, s_lv.at(b))
                    dve.tensor_tensor(v_tok[:, :, :], by_tile(7), over_tiles(l_bv), ALU.add).then_inc(s_vr.sem, 1)
                if step == "k_rstd":
                    link(l_steps, b, dve.tensor_scalar(k_y[:, :].bitcast(I32), k_ss[:, :].bitcast(I32), -0.5, float(0x5F3759DF),
                                           ALU.mult, ALU.add))
                    for _ in range(4):
                        link(l_steps, b, dve.tensor_tensor(k_a[:, :], k_y[:, :], k_y[:, :], ALU.mult))
                        link(l_steps, b, dve.tensor_tensor(k_a[:, :], k_a[:, :], k_ss[:, :], ALU.mult))
                        link(l_steps, b, dve.tensor_scalar(k_a[:, :], k_a[:, :], -0.5, 1.5, ALU.mult, ALU.add))
                        link(l_steps, b, dve.tensor_tensor(k_y[:, :], k_y[:, :], k_a[:, :], ALU.mult))
                    dve.tensor_tensor(k_tok[:, :, :].rearrange("p c (h e) -> p (c h) e", e=HD),
                                      k_tok[:, :, :].rearrange("p c (h e) -> p (c h) e", e=HD),
                                      k_y[:, :, None].broadcast_to([P, TILES * H, HD]), ALU.mult).then_inc(s_kr.sem, 1)
                if step == "q2":
                    dve.wait_ge(s_qexp.sem, s_qexp.at(b))
                    dve.tensor_tensor(qT[:, :], q_max[:, :], q_exp[:, :], ALU.add).then_inc(s_qr.sem, 1)
                if step == "kv":
                    dve.wait_ge(s_kv.sem, s_kv.at(b))
                    dve.tensor_tensor(kv[:, :], bank[:, 6, 0:D], blocks[:, :], ALU.mult).then_inc(s_kvm.sem, 1)
                if step == "out":
                    dve.wait_ge(s_lo.sem, s_lo.at(b))
                    dve.wait_ge(s_lnb.sem, s_lnb.at(b))
                    link(l_steps, b, dve.tensor_tensor(lin, by_tile(6), l_nb[:, :, :], ALU.add))
                    moments(l_steps, b, lo_norm, lin)
                    dve.tensor_scalar(lo_norm.var[:, 0:TILES], lo_norm.mv[:, :, 1], RMS_EPS, None, ALU.add) \
                        .then_inc(lo_norm.var_ready.sem, 1)
                if step == "out_scale":
                    scales(lo_norm, b, 1, 1, s_lin)
                if step == "xl":
                    dve.wait_ge(s_lon.sem, s_lon.at(b))
                    link(l_steps, b, dve.tensor_tensor(lin, lin, over_tiles(l_gamma), ALU.mult))
                    dve.wait_ge(s_lxb.sem, s_lxb.at(b))
                    if began(b - 1):
                        dve.wait_ge(second["xn_ready"].sem, second["xn_ready"].at(b - 1))
                    dve.tensor_tensor(xl[:, :, :], lin, l_xb[:, :, :], ALU.add).then_inc(s_xl.sem, 1)

            def attention(a, b, step, k):
                low, high = a.banks
                if step == "norm":
                    x_ready = s_xa if a is first else s_xl
                    dve.wait_ge(x_ready.sem, x_ready.at(b))
                    moments(steps[a], b, a.norm, a.x)
                    dve.tensor_scalar(a.norm.var[:, 0:TILES], a.norm.mv[:, :, 1], LN_EPS, None, ALU.add)
                    dve.tensor_scalar(a.norm.var[:, TILES:2 * TILES], a.norm.mv[:, :, 1], 1.0 + RMS_EPS,
                                      RMS_EPS * LN_EPS, ALU.mult, ALU.add).then_inc(a.norm.var_ready.sem, 1)
                if step == "scale":
                    scales(a.norm, b, 1, 2, a["scales_ready"])
                if step == "q":
                    dve.wait_ge(a["q_projected"].sem, a["q_projected"].at(b))
                    dve.tensor_tensor(a.q[:, :, :], by_tile(low), over_tiles(f_bq), ALU.add) \
                        .then_inc(a["q_ready"].sem, 1)
                c = k
                if step == "pv":
                    dve.wait_ge(a["prob_ready"].sem, a["prob_ready"].at(b, c + 1))
                    if c == 0:
                        dve.wait_ge(a["v_ready"].sem, a["v_ready"].at(b))
                        if a is first:
                            if began(b - 2):
                                dve.wait_ge(second["pv_summed"].sem, second["pv_summed"].at(b - 2))
                        elif not (isinstance(b, int) and b + 1 >= BATCH):
                            dve.wait_ge(first["pv_summed"].sem, first["pv_summed"].at(b + 1))
                    if c >= 2:
                        dve.wait_ge(a["pv_summed"].sem, a["pv_summed"].at(b, c - 1))
                    products(dve, a, c).then_inc(a["pv_ready"].sem, 1)
                if step == "qk":
                    sc = a.score[:, c, :].rearrange("p (h g) -> p h g", g=H)
                    dve.wait_ge(a["qk_ready"].sem, a["qk_ready"].at(b, c + 1))
                    dve.tensor_reduce(a.score[:, c, :], qk[:, c % 2, :].rearrange("p (a e) -> p a e", e=HD),
                                      AX.X, ALU.add).then_inc(a["score_ready"].sem, 1)
                    dve.wait_ge(a["score_ready"].sem, a["score_ready"].at(b, c + 1))
                    link(steps[a], b, dve.tensor_reduce(a.peak[:, c, :], sc, AX.X, ALU.max))
                    dve.tensor_tensor(sc, sc, a.peak[:, c, :, None].broadcast_to([P, H, H]), ALU.subtract) \
                        .then_inc(a["shifted"].sem, 1)
                if step == "total":
                    dve.wait_ge(a["prob_ready"].sem, a["prob_ready"].at(b))
                    link(steps[a], b, dve.tensor_reduce(a.total[:, :, :].rearrange("p c h -> p (c h)"),
                                           a.score[:, :, :].rearrange("p c (h g) -> p (c h) g", g=H), AX.X, ALU.add))
                    link(steps[a], b, dve.reciprocal(a.rec[:, :, :], a.total[:, :, :]))
                if step == "o":
                    dve.wait_ge(a["pv_summed"].sem, a["pv_summed"].at(b))
                    dve.tensor_tensor(a.o[:, :, :].rearrange("p c (h e) -> p (c h) e", e=HD),
                                      by_head(bank[:, high, :]),
                                      a.rec[:, :, :].rearrange("p c h -> p (c h)")[:, :, None]
                                      .broadcast_to([P, TILES * H, HD]), ALU.mult).then_inc(a["o_ready"].sem, 1)
                if step == "x1":
                    dve.wait_ge(a["o_projected"].sem, a["o_projected"].at(b))
                    dve.wait_ge(a["nb_ready"].sem, a["nb_ready"].at(b))
                    dve.wait_ge(a["xn_ready"].sem, a["xn_ready"].at(b))
                    dve.tensor_tensor(a.x1[:, :, :], by_tile(high), a.nb[:, :, :], ALU.add)
                    dve.tensor_tensor(a.xx1[:, :, :], by_tile(high), a.xn[:, :, :], ALU.add) \
                        .then_inc(a["xx1_ready"].sem, 1)
                if step == "norm2":
                    dve.wait_ge(a["xx1_ready"].sem, a["xx1_ready"].at(b))
                    moments(steps[a], b, a.norm, a.x1)
                    link(steps[a], b, dve.tensor_tensor(a.g_sum[:, :], a.norm.mv[:, :, 0], a.norm.mv[:, :, 0], ALU.mult))
                    dve.scalar_tensor_tensor(a.norm.var[:, 0:TILES], a.g_sum[:, :], RMS_EPS, a.norm.mv[:, :, 1],
                                             ALU.add, ALU.add).then_inc(a.norm.var_ready.sem, 1)
                if step == "logits":
                    dve.wait_ge(a["logits_ready"].sem, a["logits_ready"].at(b))
                    link(steps[a], b, dve.tensor_tensor(a.gate[:, :, :],
                                           bank[:, high, 0:TILES * EXP].rearrange("p (c e) -> p c e", e=EXP),
                                           f_bg[:, None, :].broadcast_to([P, TILES, EXP]), ALU.add))
                    link(steps[a], b, dve.tensor_reduce(a.g_max[:, :], a.gate[:, :, :], AX.X, ALU.max))
                    dve.tensor_tensor(a.gate[:, :, :], a.gate[:, :, :],
                                      a.g_max[:, :, None].broadcast_to([P, TILES, EXP]), ALU.subtract) \
                        .then_inc(a["logits_shifted"].sem, 1)
                if step == "gate":
                    dve.wait_ge(a["gate_exp_ready"].sem, a["gate_exp_ready"].at(b))
                    link(steps[a], b, dve.tensor_reduce(a.g_sum[:, :], a.gate[:, :, :], AX.X, ALU.add))
                    link(steps[a], b, dve.reciprocal(a.g_max[:, :], a.g_sum[:, :]))
                    dve.tensor_tensor(a.gate[:, :, :], a.gate[:, :, :],
                                      a.g_max[:, :, None].broadcast_to([P, TILES, EXP]), ALU.mult) \
                        .then_inc(a["gate_ready"].sem, 1)
                if step == "y":
                    dve.wait_ge(a["expert_added"].sem, a["expert_added"].at(b))
                    if a is second:
                        dve.wait_ge(s_out.sem, 16 * (b + 1))
                    else:
                        if began(b - 1):
                            dve.wait_ge(s_lxb.sem, s_lxb.at(b - 1))
                    dve.tensor_tensor(a.y[:, :, :], by_tile(high), a.xx1[:, :, :], ALU.add) \
                        .then_inc(a["y_ready"].sem, 1)

            rounds(dve, VECTOR_PLAN, mamba, linear, attention)
            assert all(c.count == c.per for c in (m_steps, l_steps, steps[first], steps[second]))

        @block.scalar
        def _(act):
            act.wait_ge(s_w.sem, WEIGHTS)
            act.activation(a_neg[:, :, :], a_neg[:, :, :], ACT.Exp).then_inc(s_rates.sem, 1)
            act.wait_ge(s_rates.sem, 1)
            act.mul(a_neg[:, :, :], a_neg[:, :, :], -1.0).then_inc(s_rates.sem, 1)
            act.wait_ge(s_rates.sem, 2)
            act.wait_ge(s_const.sem, 1)

            def normalize(dst, src, norm, column):
                for c in range(TILES):
                    j = column + c
                    ins = act.activation(dst[:, c, :], src[:, c, :], ACT.Identity, scale=norm.rstd[:, j:j + 1],
                                         bias=norm.shift[:, j:j + 1])
                return ins

            def mamba(b, step, k):
                if step == "keep":
                    act.wait_ge(s_xin.sem, s_xin.at(b))
                    if began(b - 1):
                        act.wait_ge(s_xa.sem, s_xa.at(b - 1))
                    act.activation(xkeep[:, :, :], xin[:, :, :], ACT.Copy).then_inc(s_xkeep.sem, 1)
                if step == "nrm":
                    if began(b - 1):
                        act.wait_ge(s_yacc.sem, s_yacc.at(b - 1))
                    act.wait_ge(s_mscale.sem, s_mscale.at(b))
                    normalize(m_nrm, xin, m_norm, 0).then_inc(s_mnrm.sem, 1)
                if step == "nT":
                    act.wait_ge(s_mturn.sem, s_mturn.at(b))
                    act.activation(m_nT[:, :], bank[:, 0, :], ACT.Copy).then_inc(s_mnT.sem, 1)
                if step == "xpad":
                    h = k
                    act.wait_ge(s_inp.sem, s_inp.at(b, h + 1))
                    act.activation(xpad[:, h, CONV - 1:CONV - 1 + TOK], bank[:, 1 - h, :], ACT.Copy) \
                        .then_inc(s_xpad.sem, 1)
                if step == "conv":
                    h = k
                    act.wait_ge(s_conv.sem, s_conv.at(b, h + 1))
                    act.activation(cv_t[:, h, :], bank[:, 1 - h, :], ACT.Tanh, bias=conv_bh[:, h:h + 1],
                                   scale=0.5)
                    act.activation(cv_h[:, h, :], bank[:, 1 - h, :], ACT.Identity, bias=conv_bh[:, h:h + 1],
                                   scale=0.5).then_inc(s_cvt.sem, 1)
                if step == "z":
                    if began(b - 1):
                        act.wait_ge(s_yg.sem, s_yg.at(b - 1))
                    h = k
                    act.wait_ge(s_zp.sem, s_zp.at(b, h + 1))
                    act.activation(z_t[:, h, :], bank[:, 1 - h, :], ACT.Tanh, scale=0.5)
                    act.activation(z_h[:, h, :], bank[:, 1 - h, :], ACT.Copy, scale=0.5).then_inc(s_z.sem, 1)
                if step == "dt_low":
                    act.wait_ge(s_xp.sem, s_xp.at(b))
                    act.activation(dt_lo[96:P, :], bank[96:P, 1, :], ACT.Copy).then_inc(s_dtl.sem, 1)
                if step == "bc":
                    act.activation(bc_parts[0:32, :], bank[0:32, 1, :], ACT.Copy)
                    act.activation(bc_hi[:, :], bank[0:96, 1, :], ACT.Copy).then_inc(s_bch.sem, 1)
                if step == "abs":
                    act.wait_ge(s_dtp.sem, s_dtp.at(b))
                    if began(b - 1):
                        act.wait_ge(s_mo.sem, s_mo.at(b - 1))
                    for h in range(HALVES):
                        ins = act.activation(sp_max[:, h, :], bank[:, 2 + h, :], ACT.Abs, bias=dt_b[:, h:h + 1])
                    ins.then_inc(s_abs.sem, 1)
                if step == "exp":
                    act.wait_ge(s_abs.sem, s_abs.at(b))
                    act.activation(sp_e[:, :, :], sp_max[:, :, :], ACT.Exp, scale=-1.0)
                    act.activation(sp_t[:, :, :], sp_max[:, :, :], ACT.Tanh, bias=half_ln2[:, 0:1], scale=0.5) \
                        .then_inc(s_spe.sem, 1)
                if step == "s2":
                    act.wait_ge(s_sps.sem, s_sps.at(b))
                    act.activation(sp_z[:, :, :], sp_e[:, :, :], ACT.Square, scale=0.25).then_inc(s_spz.sem, 1)
                if step == "decay":
                    if k == 0:
                        act.wait_ge(s_dt.sem, s_dt.at(b))
                    if k >= 2:
                        act.wait_ge(s_scan.sem, s_scan.at(b, k - 1))
                    for h in range(HALVES):
                        ins = act.activation(d_a[:, k % 2, h, :], dt[:, h, :], ACT.Exp, scale=a_neg[:, h, k:k + 1])
                    ins.then_inc(s_da.sem, 1)
                if step == "c":
                    act.wait_ge(s_cb.sem, s_cb.at(b, k + 1))
                    if k >= 2:
                        act.wait_ge(s_hc.sem, s_hc.at(b, k - 1))
                    act.activation(c_sb[:, k % 2, :], bank[:, 1, :], ACT.Copy).then_inc(s_cs.sem, 1)

            def linear(b, step, k):
                if step == "nrm":
                    act.wait_ge(s_lscale.sem, s_lscale.at(b))
                    normalize(l_nrm, xb, li_norm, 0).then_inc(s_lnrm.sem, 1)
                if step == "nT":
                    act.wait_ge(s_lturn.sem, s_lturn.at(b))
                    act.activation(l_nT[:, :], bank[:, 6, :], ACT.Copy).then_inc(s_lnT.sem, 1)
                if step == "k_exp":
                    act.wait_ge(s_kmin.sem, s_kmin.at(b))
                    act.activation(k_exp[:, :, :], k_min[:, :, :], ACT.Exp).then_inc(s_kexp.sem, 1)
                if step == "q_exp":
                    act.wait_ge(s_qmin.sem, s_qmin.at(b))
                    act.activation(q_exp[:, :], q_min[:, :], ACT.Exp).then_inc(s_qexp.sem, 1)
                if step == "kvo":
                    act.wait_ge(s_kvp.sem, s_kvp.at(b))
                    act.activation(kvo[:, :], bank[:, 7, 0:D], ACT.Copy).then_inc(s_kvo.sem, 1)
                if step == "out_nrm":
                    act.wait_ge(s_lin.sem, s_lin.at(b))
                    normalize(lin, lin, lo_norm, 0).then_inc(s_lon.sem, 1)

            def attention(a, b, step, k):
                low, high = a.banks
                if step == "scaled":
                    act.wait_ge(a["scales_ready"].sem, a["scales_ready"].at(b))
                    normalize(a.scaled, a.x, a.norm, TILES).then_inc(a["normalized"].sem, 1)
                if step == "nrm":
                    normalize(a.nrm, a.x, a.norm, 0).then_inc(a["nrm_ready"].sem, 1)
                if step == "hT":
                    act.wait_ge(a["turned"].sem, a["turned"].at(b))
                    act.activation(a.hT[:, :], bank[:, low, :], ACT.Copy, scale=f_g1[:, 0:1]) \
                        .then_inc(a["hT_ready"].sem, 1)
                if step == "lat":
                    act.wait_ge(a["lat_projected"].sem, a["lat_projected"].at(b))
                    act.activation(a.latT[0:LAT, :], bank[0:LAT, high, :], ACT.Identity, bias=f_bdown[:, 0:1]) \
                        .then_inc(a["lat_ready"].sem, 1)
                if step == "k":
                    act.wait_ge(a["k_projected"].sem, a["k_projected"].at(b))
                    act.activation(a.k[:, :, :], bank[:, high, :], ACT.Copy).then_inc(a["k_ready"].sem, 1)
                if step == "v":
                    act.wait_ge(a["v_projected"].sem, a["v_projected"].at(b))
                    act.activation(a.v[:, :, :], bank[:, low, :], ACT.Copy).then_inc(a["v_ready"].sem, 1)
                c = k
                if step == "prob":
                    act.wait_ge(a["shifted"].sem, a["shifted"].at(b, c + 1))
                    act.activation(a.score[:, c, :], a.score[:, c, :], ACT.Exp, scale=SCALE) \
                        .then_inc(a["prob_ready"].sem, 1)
                if step == "oT":
                    act.wait_ge(a["o_turned"].sem, a["o_turned"].at(b))
                    act.activation(a.oT[:, :], bank[:, low, :], ACT.Copy).then_inc(a["oT_ready"].sem, 1)
                if step == "h2":
                    act.wait_ge(a.norm.rstd_ready.sem, a.norm.rstd_ready.at(b, 2))
                    for c in range(TILES):
                        ins = act.activation(a.h2[:, c, :], a.x1[:, c, :], ACT.Copy, scale=a.norm.rstd[:, c:c + 1])
                    ins.then_inc(a["h2_ready"].sem, 1)
                if step == "h2T":
                    act.wait_ge(a["h2_turned"].sem, a["h2_turned"].at(b))
                    act.activation(a.h2T[:, :], bank[:, low, :], ACT.Copy, scale=f_g2[:, 0:1]) \
                        .then_inc(a["h2T_ready"].sem, 1)
                if step == "gate":
                    act.wait_ge(a["logits_shifted"].sem, a["logits_shifted"].at(b))
                    act.activation(a.gate[:, :, :], a.gate[:, :, :], ACT.Exp).then_inc(a["gate_exp_ready"].sem, 1)
                e = k
                if step == "gated":
                    if e == 0:
                        act.wait_ge(a["gate_ready"].sem, a["gate_ready"].at(b))
                    if e >= 2:
                        act.wait_ge(a["gated_turned"].sem, a["gated_turned"].at(b, e - 1))
                    for c in range(TILES):
                        ins = act.activation(a.gated[:, e % 2, c, :], a.h2[:, c, :], ACT.Copy,
                                             scale=a.gate[:, c, e:e + 1])
                    ins.then_inc(a["gated_ready"].sem, 1)
                if step == "gatedT":
                    act.wait_ge(a["gated_turned"].sem, a["gated_turned"].at(b, e + 1))
                    if e >= 2:
                        act.wait_ge(a["expert_added"].sem, a["expert_added"].at(b, e - 1))
                    act.activation(a.gatedT[:, e % 2, :], bank[:, low, :], ACT.Copy, scale=f_g2[:, 0:1]) \
                        .then_inc(a["gatedT_ready"].sem, 1)

            rounds(act, SCALAR_PLAN, mamba, linear, attention)

        @block.tensor
        def _(pe):
            pe.wait_ge(s_w.sem, WEIGHTS)
            pe.wait_ge(s_const.sem, 1)

            def mm(out, lhsT, rhs, start=True, stop=True, together=False):
                return pe.matmul(out, lhsT, rhs, start=start, stop=stop, skip_group_check=together)

            def turn(b, src):
                for c in range(TILES):
                    ins = pe.transpose(bank[:, b, P * c:P * c + P], src[:, c, :], ident[:, :])
                return ins

            def by_tokens(b, lhsT, rhs):
                for c in range(TILES):
                    ins = mm(bank[:, b, D * c:D * c + D], lhsT[:, P * c:P * c + P], rhs)
                return ins

            def mamba(b, step, k):
                if step == "turn":
                    pe.wait_ge(s_mnrm.sem, s_mnrm.at(b))
                    if began(b - 1):
                        pe.wait_ge(s_bx.sem, s_bx.at(b - 1))
                    turn(0, m_nrm).then_inc(s_mturn.sem, 1)
                if step == "in":
                    pe.wait_ge(s_mnT.sem, s_mnT.at(b))
                    if began(b - 1):
                        pe.wait_ge(s_cs.sem, s_cs.at(b - 1))
                    h = k
                    mm(bank[:, 1 - h, :], in_w[:, P * h:P * h + P], m_nT[:, :]).then_inc(s_inp.sem, 1)
                if step == "conv":
                    h = k
                    pe.wait_ge(s_xpad.sem, s_xpad.at(b, h + 1))
                    for t in range(CONV):
                        ins = mm(bank[:, 1 - h, :], conv_d[:, h, t, :], xpad[:, h, t:t + TOK],
                                 t == 0, t == CONV - 1)
                    ins.then_inc(s_conv.sem, 1)
                if step == "z":
                    h = k
                    pe.wait_ge(s_cvt.sem, s_cvt.at(b, h + 1))
                    mm(bank[:, 1 - h, :], in_w[:, P * (HALVES + h):P * (HALVES + h + 1)], m_nT[:, :]) \
                        .then_inc(s_zp.sem, 1)
                if step == "xp":
                    pe.wait_ge(s_z.sem, s_z.at(b, 1))
                    pe.wait_ge(s_xc.sem, s_xc.at(b))
                    for h in range(HALVES):
                        ins = mm(bank[:, 1, :], xp_w[:, h, :], xc[:, h, :], h == 0, h == HALVES - 1)
                    ins.then_inc(s_xp.sem, 1)
                if step == "dt":
                    pe.wait_ge(s_dtl.sem, s_dtl.at(b))
                    if began(b - 1):
                        pe.wait_ge(s_xa.sem, s_xa.at(b - 1))
                    for h in range(HALVES):
                        ins = mm(bank[:, 2 + h, :], dt_w[96:96 + RANK, P * h:P * h + P], dt_lo[96:96 + RANK, :])
                    ins.then_inc(s_dtp.sem, 1)
                if step == "bc":
                    if k == 0:
                        pe.wait_ge(s_z.sem, s_z.at(b))
                        pe.wait_ge(s_bcp.sem, s_bcp.at(b))
                    broadcast(b, k)
                if step == "add":
                    add_state(b, k)
                if step == "out":
                    pe.wait_ge(s_yg.sem, s_yg.at(b))
                    for c in range(TILES):
                        for h in range(HALVES):
                            ins = mm(bank[:, 2, D * c:D * c + D], sp_e[:, h, P * c:P * c + P], out_w[:, h, :],
                                     h == 0, h == HALVES - 1)
                    ins.then_inc(s_mo.sem, 1)

            def broadcast(b, k):
                if k >= 1:
                    pe.wait_ge(s_bx.sem, s_bx.at(b, k))
                mm(bank[:, 0, :], pickb[:, k, :], bc_parts[:, :]).then_inc(s_bb.sem, 1)
                if k >= 1:
                    pe.wait_ge(s_cs.sem, s_cs.at(b, k))
                mm(bank[:, 1, :], pickb[:, STATE + k, :], bc_parts[:, :]).then_inc(s_cb.sem, 1)

            def add_state(b, k):
                pe.wait_ge(s_hc.sem, s_hc.at(b, k + 1))
                if k == 0:
                    pe.wait_ge(s_dt.sem, s_dt.at(b))
                for h in range(HALVES):
                    ins = mm(bank[:, 2 + h, :], ident[:, :], hc[:, k % 2, h, :], k == 0, k == STATE - 1)
                ins.then_inc(s_yacc.sem, 1)

            def linear(b, step, k):
                if step == "turn":
                    pe.wait_ge(s_lnrm.sem, s_lnrm.at(b))
                    if began(b - 1):
                        pe.wait_ge(second["gatedT_ready"].sem, second["gatedT_ready"].at(b - 1))
                    turn(6, l_nrm).then_inc(s_lturn.sem, 1)
                if step == "k":
                    pe.wait_ge(s_lnT.sem, s_lnT.at(b))
                    if began(b - 1):
                        pe.wait_ge(second["y_ready"].sem, second["y_ready"].at(b - 1))
                    by_tokens(7, l_nT, l_wk[:, :]).then_inc(s_lk.sem, 1)
                if step == "q":
                    mm(bank[:, 6, :], l_wq[:, :], l_nT[:, :]).then_inc(s_lq.sem, 1)
                if step == "v":
                    pe.wait_ge(s_kmin.sem, s_kmin.at(b))
                    by_tokens(7, l_nT, l_wv[:, :]).then_inc(s_lv.sem, 1)
                if step == "kv":
                    pe.wait_ge(s_qmin.sem, s_qmin.at(b))
                    pe.wait_ge(s_vr.sem, s_vr.at(b))
                    pe.wait_ge(s_kr.sem, s_kr.at(b))
                    for c in range(TILES):
                        ins = mm(bank[:, 6, 0:D], v_tok[:, c, :], k_tok[:, c, :], c == 0, c == TILES - 1)
                    ins.then_inc(s_kv.sem, 1)
                if step == "kvp":
                    pe.wait_ge(s_kvm.sem, s_kvm.at(b))
                    mm(bank[:, 7, 0:D], kv[:, :], l_wo[:, :]).then_inc(s_kvp.sem, 1)
                if step == "out":
                    pe.wait_ge(s_kvo.sem, s_kvo.at(b))
                    pe.wait_ge(s_qr.sem, s_qr.at(b))
                    by_tokens(6, qT, kvo[:, :]).then_inc(s_lo.sem, 1)

            def attention(a, b, step, k):
                low, high = a.banks
                if step == "turn":
                    pe.wait_ge(a["normalized"].sem, a["normalized"].at(b))
                    if a is second:
                        pe.wait_ge(s_lin.sem, s_lin.at(b))
                    else:
                        if began(b - 1):
                            pe.wait_ge(a["gatedT_ready"].sem, a["gatedT_ready"].at(b - 1))
                    turn(low, a.scaled).then_inc(a["turned"].sem, 1)
                if step == "lat":
                    pe.wait_ge(a["hT_ready"].sem, a["hT_ready"].at(b))
                    if a is first:
                        if began(b - 1):
                            pe.wait_ge(a["y_ready"].sem, a["y_ready"].at(b - 1))
                    mm(bank[0:LAT, high, :], f_wdown[:, :], a.hT[:, :]).then_inc(a["lat_projected"].sem, 1)
                if step == "q":
                    by_tokens(low, a.hT, f_wq[:, :]).then_inc(a["q_projected"].sem, 1)
                if step == "k":
                    pe.wait_ge(a["lat_ready"].sem, a["lat_ready"].at(b))
                    by_tokens(high, a.latT, f_wupk[:, :]).then_inc(a["k_projected"].sem, 1)
                if step == "v":
                    pe.wait_ge(a["q_ready"].sem, a["q_ready"].at(b))
                    by_tokens(low, a.latT, f_wupv[:, :]).then_inc(a["v_projected"].sem, 1)
                c = k
                if step == "sum":
                    if c == 0:
                        pe.wait_ge(a["k_ready"].sem, a["k_ready"].at(b))
                    if c == POOL_TILE:
                        pe.wait_ge(a["pool_pv_ready"].sem, a["pool_pv_ready"].at(b))
                    else:
                        pe.wait_ge(a["pv_ready"].sem, a["pv_ready"].at(b, c + 1))
                    for g in range(H):
                        ins = mm(bank[:, high, D * c:D * c + D], ident[:, :], pv[:, c % 2, g, :], g == 0, g == H - 1)
                    ins.then_inc(a["pv_summed"].sem, 1)
                if step == "o":
                    pe.wait_ge(a["o_ready"].sem, a["o_ready"].at(b))
                    turn(low, a.o).then_inc(a["o_turned"].sem, 1)
                if step == "o_proj":
                    pe.wait_ge(a["oT_ready"].sem, a["oT_ready"].at(b))
                    by_tokens(high, a.oT, f_wo[:, :]).then_inc(a["o_projected"].sem, 1)
                if step == "h2":
                    pe.wait_ge(a["h2_ready"].sem, a["h2_ready"].at(b))
                    turn(low, a.h2).then_inc(a["h2_turned"].sem, 1)
                if step == "logits":
                    pe.wait_ge(a["h2T_ready"].sem, a["h2T_ready"].at(b))
                    pe.wait_ge(a["xx1_ready"].sem, a["xx1_ready"].at(b))
                    for c in range(TILES):
                        ins = mm(bank[:, high, EXP * c:EXP * c + EXP], a.h2T[:, P * c:P * c + P], f_wg[:, :])
                    ins.then_inc(a["logits_ready"].sem, 1)
                e = k
                if step == "gated":
                    pe.wait_ge(a["gated_ready"].sem, a["gated_ready"].at(b, e + 1))
                    if e >= 1:
                        pe.wait_ge(a["gatedT_ready"].sem, a["gatedT_ready"].at(b, e))
                    turn(low, a.gated[:, e % 2, :, :]).then_inc(a["gated_turned"].sem, 1)
                if step == "expert":
                    expert(a, b, e)

            def expert(a, b, e):
                pe.wait_ge(a["gatedT_ready"].sem, a["gatedT_ready"].at(b, e + 1))
                if e == 0:
                    pe.wait_ge(a["logits_shifted"].sem, a["logits_shifted"].at(b))
                for c in range(TILES):
                    ins = mm(bank[:, a.banks[1], D * c:D * c + D], a.gatedT[:, e % 2, P * c:P * c + P], f_we[:, e, :],
                             e == 0 and c == 0, e == EXP - 1, together=True)
                ins.then_inc(a["expert_added"].sem, 1)

            rounds(pe, TENSOR_PLAN, mamba, linear, attention)


_OUT = ((BATCH, TOK, D), "float32")


def kernel(**a):
    import concourse.bacc as bacc
    from concourse.bass_utils import run_bass_kernel_spmd

    a = {k: np.asarray(v) for k, v in a.items()}
    A, B, F = "L0_attn_a_", "L0_attn_b_", "L0_ffn_"

    def halves(x):
        return x.reshape((HALVES, P) + x.shape[1:]).swapaxes(0, 1)

    xp = a[A + "x_proj_w"].T
    bc = xp[:, RANK:]
    xp = np.concatenate([bc, bc, bc, xp[:, :RANK], np.zeros((xp.shape[0], 32 - RANK), xp.dtype)], axis=1)
    up = np.concatenate([a[F + "Wup"], a[F + "bup"][None]], axis=0).reshape(LAT + 1, H, 2, HD)
    arrays = {
        "x": a[A + "x"], "in_w": a[A + "in_proj_w"].T, "conv_w": halves(a[A + "conv_w"]),
        "conv_b": halves(a[A + "conv_b"]), "xp_w": halves(xp), "dt_w": a[A + "dt_proj_w"].T,
        "dt_b": halves(a[A + "dt_proj_b"]), "alog": halves(a[A + "A_log"]), "dp": halves(a[A + "Dp"]),
        "out_w": halves(a[A + "out_proj_w"].T),
        "l_wq": a[B + "Wq"], "l_bq": a[B + "bq"][:, None], "l_wk": a[B + "Wk"], "l_bk": a[B + "bk"],
        "l_wv": a[B + "Wv"], "l_bv": a[B + "bv"], "l_wo": a[B + "Wo"], "l_bo": a[B + "bo"],
        "l_gamma": a[B + "gamma"], "l_beta": a[B + "beta"],
        "f_g1": a[F + "gamma1"][:, None], "f_wq": a[F + "Wq"], "f_bq": a[F + "bq"],
        "f_wdown": a[F + "Wdown"], "f_bdown": a[F + "bdown"][:, None],
        "f_wupk": up[:, :, 0].reshape(LAT + 1, D), "f_wupv": up[:, :, 1].reshape(LAT + 1, D),
        "f_wo": a[F + "Wo"], "f_bo": a[F + "bo"], "f_g2": a[F + "gamma2"][:, None],
        "f_wg": a[F + "Wg"], "f_bg": a[F + "bg"], "f_we": a[F + "We"].transpose(1, 0, 2),
        "ident": np.eye(P, dtype=np.float32), "pick": np.tile(np.eye(32, dtype=np.float32), (3, 1)),
        "blocks": np.kron(np.eye(H, dtype=np.float32), np.ones((HD, HD), np.float32)),
    }
    nc = bacc.Bacc("TRN2", target_bir_lowering=False, num_devices=1)
    arrays = {f"in_{k}": np.ascontiguousarray(v) for k, v in arrays.items()}
    args = [nc.dram_tensor(k, v.shape, mybir.dt.from_np(v.dtype), kind="ExternalInput").ap()
            for k, v in arrays.items()]
    out = nc.dram_tensor("out", _OUT[0], FP32, kind="ExternalOutput").ap()
    hybrid_block_kernel(nc, *args, out)
    r = run_bass_kernel_spmd(nc, [arrays], core_ids=[0])
    return r.results[0]["out"]
```

```python
import numpy as np
import concourse.bass as bass
from concourse import mybir
from contextlib import ExitStack

FP32 = mybir.dt.float32
BF16 = mybir.dt.bfloat16
I32 = mybir.dt.int32
ALU = mybir.AluOpType
ACT = mybir.ActivationFunctionType
AX = mybir.AxisListType

P = 128
BATCH, TOK, D = 16, 512, 128
TILES = TOK // P
HALVES = 2
STATE = 16
CONV = 4
RANK = 8
H, HD = 16, 8
PAIRS = H * H
LAT = 64
EXP = 8
LN_EPS, RMS_EPS = 1e-5, 1e-6
SCALE = float(HD) ** -0.5

POOL_PLAN = """
m1.hc:8 m1.hc:9 a2.rstd2 a2.xx1 m1.hc:10 m1.hc:11 l3.out_rstd m1.hc:12 m1.hc:13 c3.rstd m1.hc:14 m1.hc:15
c3.nb m0.rstd c3.qk:0 c3.qk:1 a2.share:5 c3.qk:2 c3.qk:3 a2.share:6 a2.share:7 c3.pv:2 c3.pv:3 a1.rstd l2.rstd
a1.nb c3.rstd2 c3.xx1 a1.qk:0 m0.hc:0 m0.hc:1 a1.qk:1 m0.hc:2 a1.qk:2 m0.hc:3 a1.qk:3 c3.share:5 c3.share:6
m0.hc:4 c3.share:7 m0.hc:5 a1.pv:2 a1.pv:3 m0.hc:6 m0.hc:7 l2.nb l2.xb
"""
VECTOR_PLAN = """
a2.x1 l3.kv a2.norm2 m1.bx:11 m1.scan:10 m1.bx:12 m1.scan:11 l3.out a2.logits m1.bx:13 l3.out_scale a2.gate
m1.scan:12 m1.bx:14 l3.xl m1.scan:13 c3.norm m1.bx:15 m1.scan:14 c3.scale m1.scan:15 m1.gate m0.norm c3.q
m1.xa m0.scale c3.qk:0 c3.pv:0 c3.qk:1 m0.xc:0 m0.xc:1 c3.pv:1 c3.qk:2 m0.bc c3.qk:3 m0.bc_low a2.y a1.norm
m0.z m0.s l2.norm a1.scale c3.total c3.o m0.poly m0.u c3.x1 c3.norm2 m0.bx:0 a1.q m0.bx:1 m0.scan:0 c3.logits
c3.gate m0.bx:2 m0.scan:1 a1.qk:0 l2.scale m0.bx:3 m0.scan:2 a1.pv:0 m0.bx:4 m0.scan:3 a1.qk:1 m0.bx:5
m0.scan:4 a1.pv:1 a1.qk:2 m0.bx:6 m0.scan:5 a1.qk:3 c3.y m0.bx:7 l2.k m0.scan:6 a1.total m0.bx:8 l2.k2
m0.scan:7 l2.k_sum l2.v l2.k_rstd a1.o l2.q2 m0.bx:9 m0.scan:8 m0.bx:10 m0.scan:9
"""
SCALAR_PLAN = """
m1.decay:10 m1.c:10 m1.decay:11 m1.c:11 l3.kvo a2.h2 a2.h2T m1.decay:12 m1.c:12 m1.decay:13 m1.c:13 a2.gate
l3.out_nrm a2.gated:0 m1.decay:14 m1.c:14 a2.gated:1 m1.decay:15 m1.c:15 a2.gated:2 c3.scaled c3.nrm c3.hT
c3.lat a2.gated:3 c3.k a2.gated:4 m0.keep m0.nrm a2.gated:5 m0.nT c3.v a2.gated:6 c3.prob:0 m0.conv:0
m0.conv:1 m0.z:0 c3.prob:1 a2.gated:7 m0.z:1 m0.dt_low m0.bc c3.prob:2 m0.bc_mid m0.abs c3.prob:3 m0.exp m0.s2
a1.scaled a1.nrm a1.hT c3.oT a1.lat m0.decay:0 a1.k m0.c:0 c3.h2 m0.decay:1 c3.h2T m0.c:1 c3.gate c3.gated:0
m0.decay:2 m0.c:2 c3.gated:1 a1.v c3.gated:2 a1.prob:0 m0.decay:3 c3.gated:3 m0.c:3 m0.decay:4 m0.c:4
c3.gated:4 c3.gated:5 a1.prob:1 m0.decay:5 c3.gated:6 l2.nrm m0.c:5 a1.prob:2 c3.gated:7 m0.decay:6 l2.nT
m0.c:6 m0.decay:7 m0.c:7 a1.prob:3 l2.k_exp l2.k_sq l2.q_exp m0.decay:8 m0.c:8 m0.decay:9 m0.c:9 a1.oT
"""
TENSOR_PLAN = """
l3.kv a2.o_proj m1.add:8 m1.bc:11 l3.kvp m1.add:9 m1.bc:12 l3.out a2.h2 a2.logits m1.add:10 m1.bc:13
a2.expert:0 m1.add:11 m1.bc:14 a2.expert:1 a2.share:0 m1.add:12 m1.bc:15 a2.expert:2 a2.share:1 m1.add:13
a2.expert:3 a2.share:2 c3.turn m1.add:14 m1.add:15 c3.lat c3.q c3.k a2.expert:4 m1.out c3.v a2.share:3
a2.expert:5 a2.share:4 m0.turn a2.expert:6 m0.conv:0 m0.conv:1 m0.z:0 a2.expert:7 m0.z:1 m0.xp c3.sum:0 m0.dt
c3.sum:1 c3.sum:2 m0.bc:0 c3.sum:3 a1.turn c3.o c3.o_proj a1.lat a1.q a1.k m0.bc:1 c3.h2 c3.logits c3.expert:0
m0.bc:2 a1.v c3.expert:1 c3.share:0 m0.add:0 c3.expert:2 m0.bc:3 c3.share:1 c3.expert:3 m0.add:1 c3.share:2
m0.bc:4 c3.expert:4 c3.share:3 m0.add:2 c3.expert:5 m0.bc:5 c3.share:4 c3.expert:6 a1.sum:0 c3.expert:7
m0.add:3 m0.bc:6 a1.sum:1 l2.turn m0.add:4 m0.bc:7 l2.k l2.q m0.add:5 m0.bc:8 l2.v a1.sum:2 a1.sum:3 m0.add:6
m0.bc:9 m0.add:7 m0.bc:10 a1.o
"""
MOST_BEHIND = max(int(name[1:name.index(".")])
                  for name in (POOL_PLAN + VECTOR_PLAN + SCALAR_PLAN + TENSOR_PLAN).split())
LOOP_FROM = MOST_BEHIND + 2
STORE_BEHIND = 3


def parse(name):
    layer, behind, (step, _, k) = name[0], int(name[1:name.index(".")]), name[name.index(".") + 1:].partition(":")
    return layer, behind, step, int(k) if k else None


TENSOR_EXPERTS = 5
VECTOR_TILES = 2

_z = (0.5 - 0.5 * np.cos(np.pi * (np.arange(400) + 0.5) / 400)) / 9
_atanh = np.polynomial.Polynomial.fit(_z, np.arctanh(np.sqrt(_z)) / np.sqrt(_z) / 2, 4, domain=[0, 1 / 9]).convert()
_roots = [root for root in _atanh.roots() if root.imag > 0]
LEAD, SHIFTS, RESTS = float(_atanh.coef[-1]), [-float(z.real) for z in _roots], [float(z.imag) ** 2 for z in _roots]


def hybrid_block_kernel(nc, x_d, in_w_d, conv_w_d, conv_b_d, xp_w_d, dt_w_d, dt_b_d, alog_d, dp_d, out_w_d,
                        l_wq_d, l_bq_d, l_wk_d, l_bk_d, l_wv_d, l_bv_d, l_wo_d, l_bo_d, l_gamma_d, l_beta_d,
                        f_g1_d, f_wq_d, f_bq_d, f_wdown_d, f_bdown_d, f_wupk_d, f_wupv_d, f_wo_d, f_bo_d,
                        f_g2_d, f_wg_d, f_bg_d, f_we_d, ident_d, pick_d, blocks_d, y_d):
    ctx = ExitStack()
    with ctx:
        def sb(name, shape, dt=FP32):
            return ctx.enter_context(nc.sbuf_tensor(name, shape, dt))

        class Signal:

            def __init__(self, name, per):
                self.sem, self.per = ctx.enter_context(nc.semaphore(name)), per

            def at(self, b, k=None):
                return b * self.per + (self.per if k is None else k)

        def began(b):
            return not (isinstance(b, int) and b < 0)

        ident = sb("ident", [P, P])
        pick = sb("pick", [96, 32])
        pickb = sb("pickb", [96, 32, P], BF16)
        blocks = sb("blocks", [P, P])
        in_w = sb("in_w", [P, 2 * HALVES * P])
        conv_in_w = sb("conv_in_w", [P, CONV * HALVES * P])
        poly_bias = sb("poly_bias", [P, 2])
        l_bqn = sb("l_bqn", [P, 1])
        conv_b = sb("conv_b", [P, HALVES])
        conv_bh = sb("conv_bh", [P, HALVES])
        xp_w = sb("xp_w", [P, HALVES, P])
        dt_w = sb("dt_w", [P, HALVES * P])
        dt_b = sb("dt_b", [P, HALVES])
        a_neg = sb("a_neg", [P, HALVES, STATE])
        dp = sb("dp", [P, HALVES])
        out_w = sb("out_w", [P, HALVES, D])
        l_wq, l_wk, l_wv, l_wo = (sb(n, [P, D]) for n in ("l_wq", "l_wk", "l_wv", "l_wo"))
        l_bq = sb("l_bq", [P, 1])
        l_bk, l_bv, l_bo, l_gamma, l_beta = (sb(n, [P, D]) for n in ("l_bk", "l_bv", "l_bo", "l_gamma", "l_beta"))
        f_g1, f_g2 = (sb(n, [P, 1]) for n in ("f_g1", "f_g2"))
        f_bq = sb("f_bq", [P, D])
        f_wq = sb("f_wq", [P, D])
        f_wdown = sb("f_wdown", [P, LAT])
        f_bdown = sb("f_bdown", [LAT, 1])
        f_wupk = sb("f_wupk", [LAT + 1, D])
        f_wupv = sb("f_wupv", [LAT + 1, D])
        f_wo = sb("f_wo", [P, D])
        f_bo = sb("f_bo", [P, D])
        f_wg = sb("f_wg", [P, EXP])
        f_bg = sb("f_bg", [P, EXP])
        f_we = sb("f_we", [P, EXP, D])
        minus_half = sb("minus_half", [P, 2 * TILES])
        half_ln2 = sb("half_ln2", [P, 1])
        spare = sb("spare", [P, 1])

        xin = sb("xin", [P, TILES, D])
        xkeep = sb("xkeep", [P, TILES, D])
        m_nT = sb("m_nT", [P, CONV - 1 + TOK])
        xc = sb("xc", [P, HALVES, TOK])
        z_h = sb("z_h", [P, HALVES, TOK])
        bc_hi = sb("bc_hi", [96, TOK], BF16)
        bc_parts = sb("bc_parts", [96, TOK], BF16)
        sp_e = sb("sp_e", [P, HALVES, TOK])
        sp_t = sb("sp_t", [P, HALVES, TOK])
        dt = sb("dt", [P, HALVES, TOK])
        u = sb("u", [P, HALVES, TOK])
        d_a = sb("d_a", [P, 2, HALVES, TOK])
        d_bx = sb("d_bx", [P, 2, HALVES, TOK])
        hs = sb("hs", [P, 2, HALVES, TOK])
        c_sb = sb("c_sb", [P, 2, TOK])
        hc = sb("hc", [P, 2, HALVES, TOK])
        cv_t, cv_h, sp_z = sp_t, u, dt
        bc_mid = bc_hi
        m_nrm = hc[:, 1, 0, :].rearrange("p (c d) -> p c d", c=TILES)
        z_t, sp_abs, sp_max = hc[:, 0, :, :], d_bx[:, 0, :, :], c_sb
        sp_a, sp_b = sp_t, u
        bc_rest, dt_lo = d_a[0:96, 0, 0, :], d_a[:, 1, 0, :]
        xa = sb("xa", [P, TILES, D])
        xb = sb("xb", [P, TILES, D])
        xl = sb("xl", [P, TILES, D])
        xo = sb("xo", [P, TILES, D])

        bank = ctx.enter_context(nc.psum_tensor("bank", [P, 8, 512], FP32))

        class Norm:

            def __init__(self, name, rises):
                self.stats = sb(name + "_stats", [P, TILES, 6])
                self.mv = sb(name + "_mv", [P, TILES, 2])
                self.var = sb(name + "_var", [P, 2 * TILES])
                self.rstd = sb(name + "_rstd", [P, 2 * TILES])
                self.shift = sb(name + "_shift", [P, 2 * TILES])
                self.var_ready = Signal(name + "_var_ready", rises)
                self.rstd_ready = Signal(name + "_rstd_ready", rises)

        class Attention:

            def __init__(self, name, x, y, banks):
                self.x, self.y, self.banks, self.name = x, y, banks, name
                self.norm = Norm(name, 2)
                self.scaled = sb(name + "_scaled", [P, TILES, D])
                self.nrm = sb(name + "_nrm", [P, TILES, D])
                self.hT = sb(name + "_hT", [P, TOK])
                self.latT = sb(name + "_latT", [LAT + 1, TOK])
                self.q = sb(name + "_q", [P, TILES, D])
                self.kv = sb(name + "_k_v", [P, 2, TOK])
                self.k, self.v = (self.kv[:, i, :].rearrange("p (c d) -> p c d", c=TILES) for i in range(2))
                self.score = sb(name + "_score", [P, TILES, PAIRS])
                self.peak = sb(name + "_peak", [P, TILES, H])
                self.total = sb(name + "_total", [P, TILES, H])
                self.rec = sb(name + "_rec", [P, TILES, H])
                self.nb = sb(name + "_nb", [P, TILES, D])
                self.xx1 = sb(name + "_xx1", [P, TILES, D])
                self.x1 = sb(name + "_x1", [P, TILES, D])
                self.gate = sb(name + "_gate", [P, TILES, EXP])
                self.g_max = sb(name + "_g_max", [P, TILES])
                self.g_sum = sb(name + "_g_sum", [P, TILES])
                self.o, self.oT, self.h2 = self.q, self.hT, self.scaled
                self.h2T = self.hT
                self.gated = self.score[:, :, :].rearrange("p c (s d) -> p (c s) d", d=D) \
                    .rearrange("p (u c) d -> p u c d", u=2)
                self.signals = {}
                for signal, per in (("scales_ready", 1), ("normalized", 1), ("nrm_ready", 1), ("turned", 1),
                                    ("hT_ready", 1),
                                    ("q_projected", 1), ("q_ready", 1), ("lat_projected", 1), ("lat_ready", 1),
                                    ("k_projected", 1), ("k_ready", 1), ("v_projected", 1), ("v_ready", 1),
                                    ("qk_ready", TILES), ("score_ready", TILES), ("shifted", TILES),
                                    ("prob_ready", TILES), ("pv_ready", VECTOR_TILES),
                                    ("pool_pv_ready", TILES - VECTOR_TILES),
                                    ("pv_summed", TILES), ("o_ready", 1), ("o_turned", 1), ("oT_ready", 1),
                                    ("o_projected", 1), ("nb_ready", 1), ("x1_ready", 1),
                                    ("xx1_ready", 1), ("h2_ready", 1), ("h2_turned", 1), ("h2T_ready", 1),
                                    ("logits_ready", 1), ("gate_exp_ready", 1),
                                    ("gate_ready", 2), ("share_ready", EXP), ("gated_ready", EXP),
                                    ("expert_added", TENSOR_EXPERTS),
                                    ("pool_expert_added", EXP - TENSOR_EXPERTS), ("y_ready", 1)):
                    self.signals[signal] = Signal(name + "_" + signal, per)

            def __getitem__(self, signal):
                return self.signals[signal]

        m_norm, li_norm, lo_norm = Norm("m", 1), Norm("li", 1), Norm("lo", 1)
        first = Attention("a", xa, xb, (4, 5))
        second = Attention("c", xl, xo, (6, 7))
        qk = sb("qk", [P, 2, PAIRS * HD])
        pv = sb("pv", [P, 2, H, D])
        l_nrm, l_nT = second.nrm, sb("l_nT", [P, TOK])
        l_nb, l_xb = second.nb, second.xx1
        q_min, q_max = sb("q_min", [P, TOK]), sb("q_max", [P, TOK])
        k_tok = sb("k_tok", [P, TILES, D])
        k_min = sb("k_min", [P, TILES, D])
        k_ss, k_y, k_a = (sb(n, [P, TILES * H]) for n in ("k_ss", "k_y", "k_a"))
        q_exp, qT, k_exp, k_sq = q_min, q_max, k_min, k_min
        v_tok = sb("v_tok", [P, TILES, D])
        kv = sb("kv", [P, D])
        kvo = sb("kvo", [P, D])
        lin = l_nT[:, :].rearrange("p (c d) -> p c d", c=TILES)

        s_w = Signal("weights_loaded", 0)
        s_const = Signal("constants_made", 0)
        s_pool_const = Signal("pool_constants_made", 0)
        s_rates = Signal("decay_rates_ready", 0)
        s_xin = Signal("x_loaded", 16)
        s_out = Signal("y_stored", 16)
        s_xkeep = Signal("x_kept", 1)
        s_mscale = Signal("m_scales_ready", 1)
        s_mnrm = Signal("m_normalized", 1)
        s_mturn = Signal("m_turned", 1)
        s_mnT = Signal("m_nT_ready", 1)
        s_conv = Signal("convolved", HALVES)
        s_cvt = Signal("conv_tanh_ready", HALVES)
        s_xc = Signal("xc_ready", HALVES)
        s_zp = Signal("z_projected", HALVES)
        s_z = Signal("z_tanh_ready", HALVES)
        s_xp = Signal("x_projected", 1)
        s_dtl = Signal("dt_low_ready", 1)
        s_bch = Signal("bc_high_ready", 1)
        s_bcr = Signal("bc_rest_ready", 1)
        s_bcm = Signal("bc_mid_ready", 1)
        s_bcp = Signal("bc_parts_ready", 1)
        s_dtp = Signal("dt_projected", 1)
        s_abs = Signal("softplus_abs_ready", 1)
        s_spe = Signal("softplus_exp_ready", 1)
        s_sps = Signal("softplus_s_ready", 1)
        s_spz = Signal("softplus_s2_ready", 1)
        s_spq = Signal("softplus_squares_ready", 1)
        s_dt = Signal("dt_ready", 1)
        s_u = Signal("u_ready", 1)
        s_da = Signal("decay_ready", STATE)
        s_bb = Signal("b_broadcast", STATE)
        s_bx = Signal("b_consumed", STATE)
        s_cb = Signal("c_broadcast", STATE)
        s_cs = Signal("c_in_sbuf", STATE)
        s_scan = Signal("scanned", STATE)
        s_hc = Signal("h_times_c", STATE)
        s_yacc = Signal("y_accumulated", STATE)
        s_yg = Signal("y_gated", 1)
        s_mo = Signal("mamba_projected", 1)
        s_xa = Signal("xa_ready", 1)
        s_lscale = Signal("l_scales_ready", 1)
        s_lnrm = Signal("l_normalized", 1)
        s_lturn = Signal("l_turned", 1)
        s_lnT = Signal("l_nT_ready", 1)
        s_lk = Signal("lin_k_projected", 1)
        s_lq = Signal("lin_q_projected", 1)
        s_lv = Signal("lin_v_projected", 1)
        s_kb = Signal("k_biased", 1)
        s_kact = Signal("k_activation_steps", 3)
        s_ka = Signal("k_activated", 1)
        s_qact = Signal("q_activation_steps", 2)
        s_vr = Signal("lin_v_ready", 1)
        s_kr = Signal("k_normed", 1)
        s_qr = Signal("lin_q_ready", 1)
        s_kv = Signal("kv_summed", 1)
        s_kvm = Signal("kv_masked", 1)
        s_kvp = Signal("kv_projected", 1)
        s_kvo = Signal("kvo_ready", 1)
        s_lo = Signal("lin_projected", 1)
        s_lin = Signal("lin_moments_ready", 1)
        s_lon = Signal("lin_normalized", 1)
        s_lnb = Signal("lin_nb_ready", 1)
        s_lxb = Signal("x_plus_beta", 1)
        s_xl = Signal("xl_ready", 1)

        loads = [(ident[:, :], ident_d), (pick[:, :], pick_d), (in_w[:, :], in_w_d),
                 (conv_b[:, :], conv_b_d), (xp_w[:, :, :], xp_w_d), (dt_w[96:96 + RANK, :], dt_w_d),
                 (dt_b[:, :], dt_b_d), (a_neg[:, :, :], alog_d), (dp[:, :], dp_d), (out_w[:, :, :], out_w_d),
                 (l_wq[:, :], l_wq_d), (l_wk[:, :], l_wk_d), (l_wv[:, :], l_wv_d), (l_wo[:, :], l_wo_d),
                 (l_bq[:, :], l_bq_d), (f_g1[:, :], f_g1_d), (f_g2[:, :], f_g2_d), (f_wq[:, :], f_wq_d),
                 (f_wdown[:, :], f_wdown_d), (f_bdown[:, :], f_bdown_d), (f_wupk[:, :], f_wupk_d),
                 (f_wupv[:, :], f_wupv_d), (f_wo[:, :], f_wo_d), (f_wg[:, :], f_wg_d), (f_we[:, :, :], f_we_d)]
        for t, s in ((l_bk, l_bk_d), (l_bv, l_bv_d), (l_bo, l_bo_d), (l_gamma, l_gamma_d), (l_beta, l_beta_d),
                     (f_bo, f_bo_d), (f_bq, f_bq_d), (f_bg, f_bg_d), (conv_in_w, conv_w_d)):
            loads.append((t[:, :], s.partition_broadcast(P)))
        WEIGHTS = 16 * len(loads)

        def by_tile(b):
            return bank[:, b, :].rearrange("p (c d) -> p c d", c=TILES)

        def by_head(t):
            return t.rearrange("p (h e) -> p h e", e=HD)

        def over_tiles(row):
            return row[:, None, :].broadcast_to([P, TILES, D])

        def rounds(eng, plan, mamba, linear, attention):
            def one(r):
                for name in plan.split():
                    layer, behind, step, k = parse(name)
                    b = r - behind
                    if isinstance(r, int) and not 0 <= b < BATCH:
                        continue
                    if layer == "m":
                        mamba(b, step, k)
                    elif layer == "l":
                        linear(b, step, k)
                    else:
                        attention(first if layer == "a" else second, b, step, k)

            for r in range(LOOP_FROM):
                one(r)
            with eng.Fori(LOOP_FROM, BATCH) as r:
                one(r)
            for r in range(BATCH, BATCH + MOST_BEHIND):
                one(r)

        block = ctx.enter_context(nc.Block())

        @block.sync
        def _(sp):
            for t, s in loads:
                sp.dma_start(t, s).then_inc(s_w.sem, 16)
            sp.dma_start(blocks[:, :], blocks_d).then_inc(s_out.sem, 16)

            def load(b):
                sp.dma_start(xin[:, :, :], x_d[bass.ds(b, 1), :, :].rearrange("o (c p) d -> p (o c) d", p=P)) \
                    .then_inc(s_xin.sem, 16)

            def next_load(r):
                sp.wait_ge(s_xkeep.sem, s_xkeep.at(r))
                sp.wait_ge(s_mnrm.sem, s_mnrm.at(r))
                load(r + 1)

            def store(b):
                sp.wait_ge(second["y_ready"].sem, second["y_ready"].at(b))
                sp.dma_start(y_d[bass.ds(b, 1), :, :].rearrange("o (c p) d -> p (o c) d", p=P), xo[:, :, :]) \
                    .then_inc(s_out.sem, 16)

            load(0)
            for r in range(LOOP_FROM):
                next_load(r)
                if r >= STORE_BEHIND:
                    store(r - STORE_BEHIND)
            with sp.Fori(LOOP_FROM, BATCH - 1) as r:
                next_load(r)
                store(r - STORE_BEHIND)
            for b in range(BATCH - 1 - STORE_BEHIND, BATCH):
                store(b)
            sp.wait_ge(s_out.sem, 16 * (BATCH + 1))

        def products(eng, a, c):
            return eng.tensor_tensor(
                pv[:, c % 2, :, :].rearrange("p g (h e) -> p g h e", e=HD),
                a.score[:, c, :].rearrange("p (h g) -> p g h", g=H)[:, :, :, None].broadcast_to([P, H, H, HD]),
                by_head(a.v[:, c, :])[:, :, None, :].broadcast_to([P, H, H, HD]), ALU.mult)

        @block.gpsimd
        def _(pool):
            pool.memset(minus_half[:, :], -0.5)
            pool.memset(half_ln2[:, :], 0.5 * float(np.log(2.0)))
            pool.memset(poly_bias[:, 0:1], SHIFTS[0] * LEAD ** 0.5)
            pool.memset(poly_bias[:, 1:2], SHIFTS[1])
            pool.memset(m_nT[:, 0:CONV - 1], 0.0).then_inc(s_pool_const.sem, 1)
            pool.wait_ge(s_pool_const.sem, 1)
            pool.wait_ge(s_w.sem, WEIGHTS)

            def rsqrt(norm, b, k, n):
                pool.wait_ge(norm.var_ready.sem, norm.var_ready.at(b, k))
                pool.tensor_tensor(norm.rstd[:, 0:n], norm.var[:, 0:n], minus_half[:, 0:n], ALU.pow) \
                    .then_inc(norm.rstd_ready.sem, 1)

            def mamba(b, step, k):
                if step == "rstd":
                    rsqrt(m_norm, b, 1, TILES)
                if step == "hc":
                    pool.wait_ge(s_cs.sem, s_cs.at(b, k + 1))
                    pool.wait_ge(s_scan.sem, s_scan.at(b, k + 1))
                    if k >= 2:
                        pool.wait_ge(s_yacc.sem, s_yacc.at(b, k - 1))
                    else:
                        if began(b - 1):
                            pool.wait_ge(s_yacc.sem, s_yacc.at(b - 1))
                    pool.tensor_tensor(hc[:, k % 2, :, :], hs[:, k % 2, :, :],
                                       c_sb[:, k % 2, None, :].broadcast_to([P, HALVES, TOK]), ALU.mult) \
                        .then_inc(s_hc.sem, 1)

            def linear(b, step, k):
                if step == "rstd":
                    rsqrt(li_norm, b, 1, TILES)
                if step == "nb":
                    pool.wait_ge(s_lnrm.sem, s_lnrm.at(b))
                    if began(b - 1):
                        pool.wait_ge(second["x1_ready"].sem, second["x1_ready"].at(b - 1))
                    pool.tensor_tensor(l_nb[:, :, :], l_nrm[:, :, :], over_tiles(l_bo), ALU.add) \
                        .then_inc(s_lnb.sem, 1)
                if step == "xb":
                    if began(b - 1):
                        pool.wait_ge(second["y_ready"].sem, second["y_ready"].at(b - 1))
                    pool.tensor_tensor(l_xb[:, :, :], xb[:, :, :], over_tiles(l_beta), ALU.add).then_inc(s_lxb.sem, 1)
                if step == "out_rstd":
                    rsqrt(lo_norm, b, 1, TILES)

            def attention(a, b, step, k):
                if step == "rstd":
                    rsqrt(a.norm, b, 1, 2 * TILES)
                if step == "nb":
                    pool.wait_ge(a["nrm_ready"].sem, a["nrm_ready"].at(b))
                    if a is second:
                        pool.wait_ge(s_lin.sem, s_lin.at(b))
                        pool.wait_ge(s_xl.sem, s_xl.at(b))
                    else:
                        if began(b - 1):
                            pool.wait_ge(a["x1_ready"].sem, a["x1_ready"].at(b - 1))
                    pool.tensor_tensor(a.nb[:, :, :], a.nrm[:, :, :], over_tiles(f_bo), ALU.add) \
                        .then_inc(a["nb_ready"].sem, 1)
                c = k
                if step == "qk":
                    if c == 0:
                        pool.wait_ge(a["q_ready"].sem, a["q_ready"].at(b))
                        pool.wait_ge(a["k_ready"].sem, a["k_ready"].at(b))
                        if a is first:
                            if began(b - 2):
                                pool.wait_ge(second["score_ready"].sem, second["score_ready"].at(b - 2))
                        elif not (isinstance(b, int) and b + 1 >= BATCH):
                            pool.wait_ge(first["score_ready"].sem, first["score_ready"].at(b + 1))
                    if c >= 2:
                        pool.wait_ge(a["score_ready"].sem, a["score_ready"].at(b, c - 1))
                    pool.tensor_tensor(
                        qk[:, c % 2, :].rearrange("p (h g e) -> p h g e", h=H, g=H),
                        by_head(a.q[:, c, :])[:, :, None, :].broadcast_to([P, H, H, HD]),
                        a.k[:, c, None, :].broadcast_to([P, H, D]).rearrange("p h (g e) -> p h g e", e=HD),
                        ALU.mult).then_inc(a["qk_ready"].sem, 1)
                if step == "pv":
                    pool.wait_ge(a["prob_ready"].sem, a["prob_ready"].at(b, c + 1))
                    pool.wait_ge(a["pv_summed"].sem, a["pv_summed"].at(b, c - 1))
                    products(pool, a, c).then_inc(a["pool_pv_ready"].sem, 1)
                if step == "rstd2":
                    rsqrt(a.norm, b, 2, TILES)
                if step == "xx1":
                    pool.wait_ge(a["x1_ready"].sem, a["x1_ready"].at(b))
                    if began(b - 1):
                        pool.wait_ge(a["y_ready"].sem, a["y_ready"].at(b - 1))
                    pool.tensor_tensor(a.xx1[:, :, :], a.x[:, :, :], a.x1[:, :, :], ALU.add) \
                        .then_inc(a["xx1_ready"].sem, 1)
                if step == "share":
                    e = k
                    pool.wait_ge(a["gated_ready"].sem, a["gated_ready"].at(b, e + 1))
                    if e == TENSOR_EXPERTS:
                        pool.wait_ge(a["xx1_ready"].sem, a["xx1_ready"].at(b))
                    else:
                        pool.wait_ge(a["pool_expert_added"].sem, a["pool_expert_added"].at(b, e - TENSOR_EXPERTS))
                    pool.tensor_tensor(a.xx1[:, :, :], a.xx1[:, :, :], a.gated[:, e % 2, :, :], ALU.add) \
                        .then_inc(a["pool_expert_added"].sem, 1)

            rounds(pool, POOL_PLAN, mamba, linear, attention)

        @block.vector
        def _(dve):
            for a in (first, second):
                dve.memset(a.latT[LAT:LAT + 1, :], 1.0)
            dve.wait_ge(s_pool_const.sem, 1)
            dve.wait_ge(s_w.sem, WEIGHTS)
            dve.wait_ge(s_out.sem, 16)
            dve.tensor_copy(pickb[:, :, :], pick[:, :, None].broadcast_to([96, 32, P]))
            for t in range(CONV):
                taps = conv_in_w[:, t * HALVES * P:(t + 1) * HALVES * P]
                dve.tensor_tensor(taps, taps, in_w[:, 0:HALVES * P], ALU.mult)
            dve.tensor_scalar(l_bqn[:, :], l_bq[:, :], -1.0, None, ALU.mult)
            dve.tensor_scalar(conv_bh[:, :], conv_b[:, :], 0.5, None, ALU.mult).then_inc(s_const.sem, 1)

            class Chain(Signal):
                count = 0

            m_steps, l_steps = Chain("mamba_steps", 5), Chain("linear_steps", 18)
            steps = {first: Chain("a_steps", 15), second: Chain("c_steps", 15)}

            def link(chain, b, ins):
                chain.count = chain.count % chain.per + 1
                ins.then_inc(chain.sem, 1)
                dve.wait_ge(chain.sem, chain.at(b, chain.count))

            def moments(chain, b, norm, src):
                for c in range(TILES):
                    ins = dve.bn_stats(norm.stats[:, c, :], src[:, c, :])
                link(chain, b, ins)
                dve.memset(spare[:, :], 0.0)
                for c in range(TILES):
                    ins = dve.bn_aggr(norm.mv[:, c, :], norm.stats[:, c, :])
                link(chain, b, ins)

            def scales(norm, b, k, kinds, done):
                dve.wait_ge(norm.rstd_ready.sem, norm.rstd_ready.at(b, k))
                dve.scalar_tensor_tensor(
                    norm.shift[:, 0:kinds * TILES].rearrange("p (a c) -> p a c", a=kinds),
                    norm.mv[:, None, :, 0].broadcast_to([P, kinds, TILES]), -1.0,
                    norm.rstd[:, 0:kinds * TILES].rearrange("p (a c) -> p a c", a=kinds),
                    ALU.mult, ALU.mult).then_inc(done.sem, 1)

            def input_of(b, k):
                dve.wait_ge(s_bb.sem, s_bb.at(b, k + 1))
                if k >= 2:
                    dve.wait_ge(s_scan.sem, s_scan.at(b, k - 1))
                dve.tensor_tensor(d_bx[:, k % 2, :, :], u[:, :, :],
                                  bank[:, 0, None, :].broadcast_to([P, HALVES, TOK]), ALU.mult) \
                    .then_inc(s_bx.sem, 1)

            def mamba(b, step, k):
                if step == "norm":
                    dve.wait_ge(s_xin.sem, s_xin.at(b))
                    moments(m_steps, b, m_norm, xin)
                    dve.tensor_scalar(m_norm.var[:, 0:TILES], m_norm.mv[:, :, 1], LN_EPS, None, ALU.add) \
                        .then_inc(m_norm.var_ready.sem, 1)
                if step == "scale":
                    scales(m_norm, b, 1, 1, s_mscale)
                if step == "xc":
                    h = k
                    dve.wait_ge(s_cvt.sem, s_cvt.at(b, h + 1))
                    dve.scalar_tensor_tensor(xc[:, h, :], cv_t[:, h, :], 1.0, cv_h[:, h, :],
                                             ALU.add, ALU.mult).then_inc(s_xc.sem, 1)
                if step == "bc":
                    dve.wait_ge(s_bch.sem, s_bch.at(b))
                    dve.tensor_tensor(bc_rest[:, :], bank[0:96, 1, :], bc_hi[:, :], ALU.subtract).then_inc(s_bcr.sem, 1)
                if step == "bc_low":
                    dve.wait_ge(s_bcm.sem, s_bcm.at(b))
                    dve.tensor_tensor(bc_parts[64:96, :], bc_rest[64:96, :], bc_mid[64:96, :], ALU.subtract) \
                        .then_inc(s_bcp.sem, 1)
                if step == "z":
                    dve.wait_ge(s_z.sem, s_z.at(b))
                    dve.scalar_tensor_tensor(z_h[:, :, :], z_t[:, :, :], 1.0, z_h[:, :, :], ALU.add, ALU.mult)
                if step == "s":
                    dve.wait_ge(s_spe.sem, s_spe.at(b))
                    dve.scalar_tensor_tensor(sp_e[:, :, :], sp_t[:, :, :], 1.0, sp_e[:, :, :], ALU.add, ALU.mult) \
                        .then_inc(s_sps.sem, 1)
                if step == "poly":
                    dve.wait_ge(s_spq.sem, s_spq.at(b))
                    link(m_steps, b, dve.scalar_tensor_tensor(sp_b[:, :, :], sp_b[:, :, :], RESTS[1], sp_e[:, :, :],
                                                              ALU.add, ALU.mult))
                    link(m_steps, b, dve.scalar_tensor_tensor(sp_a[:, :, :], sp_a[:, :, :], LEAD * RESTS[0],
                                                              sp_b[:, :, :], ALU.add, ALU.mult))
                if step == "u":
                    dve.tensor_tensor(dt[:, :, :], sp_a[:, :, :], sp_max[:, :, :], ALU.add).then_inc(s_dt.sem, 1)
                    dve.wait_ge(s_dt.sem, s_dt.at(b))
                    dve.tensor_tensor(u[:, :, :], dt[:, :, :], xc[:, :, :], ALU.mult).then_inc(s_u.sem, 1)
                    dve.wait_ge(s_u.sem, s_u.at(b))
                if step == "bx":
                    input_of(b, k)
                if step == "scan":
                    dve.wait_ge(s_bx.sem, s_bx.at(b, k + 1))
                    dve.wait_ge(s_da.sem, s_da.at(b, k + 1))
                    if k >= 2:
                        dve.wait_ge(s_hc.sem, s_hc.at(b, k - 1))
                    for h in range(HALVES):
                        ins = dve.tensor_tensor_scan(hs[:, k % 2, h, :], d_a[:, k % 2, h, :], d_bx[:, k % 2, h, :],
                                                     0.0, ALU.mult, ALU.add)
                    ins.then_inc(s_scan.sem, 1)
                if step == "gate":
                    dve.wait_ge(s_yacc.sem, s_yacc.at(b))
                    for h in range(HALVES):
                        ins = dve.scalar_tensor_tensor(sp_e[:, h, :], xc[:, h, :], dp[:, h:h + 1], bank[:, 2 + h, :],
                                                       ALU.mult, ALU.add)
                    link(m_steps, b, ins)
                    dve.tensor_tensor(sp_e[:, :, :], sp_e[:, :, :], z_h[:, :, :], ALU.mult).then_inc(s_yg.sem, 1)
                if step == "xa":
                    dve.wait_ge(s_mo.sem, s_mo.at(b))
                    if began(b - 1):
                        dve.wait_ge(first["xx1_ready"].sem, first["xx1_ready"].at(b - 1))
                    dve.tensor_tensor(xa[:, :, :], by_tile(2), xkeep[:, :, :], ALU.add).then_inc(s_xa.sem, 1)

            def linear(b, step, k):
                if step == "norm":
                    dve.wait_ge(first["y_ready"].sem, first["y_ready"].at(b))
                    moments(l_steps, b, li_norm, xb)
                    dve.tensor_scalar(li_norm.var[:, 0:TILES], li_norm.mv[:, :, 1], LN_EPS, None, ALU.add) \
                        .then_inc(li_norm.var_ready.sem, 1)
                if step == "scale":
                    scales(li_norm, b, 1, 1, s_lscale)
                if step == "k":
                    dve.wait_ge(s_lk.sem, s_lk.at(b))
                    dve.tensor_tensor(k_tok[:, :, :], by_tile(7), over_tiles(l_bk), ALU.add).then_inc(s_kb.sem, 1)
                if step == "k2":
                    dve.wait_ge(s_kact.sem, s_kact.at(b, 2))
                    dve.scalar_tensor_tensor(k_tok[:, :, :], k_tok[:, :, :], 0.0, k_exp[:, :, :],
                                             ALU.max, ALU.add).then_inc(s_ka.sem, 1)
                if step == "k_sum":
                    dve.wait_ge(s_kact.sem, s_kact.at(b, 3))
                    link(l_steps, b, dve.tensor_reduce(
                        k_ss[:, :], k_sq[:, :, :].rearrange("p c (h e) -> p (c h) e", e=HD), AX.X, ALU.add))
                    link(l_steps, b, dve.tensor_scalar(k_ss[:, :], k_ss[:, :], RMS_EPS, None, ALU.add))
                if step == "v":
                    dve.wait_ge(s_lv.sem, s_lv.at(b))
                    dve.tensor_tensor(v_tok[:, :, :], by_tile(7), over_tiles(l_bv), ALU.add).then_inc(s_vr.sem, 1)
                if step == "k_rstd":
                    link(l_steps, b, dve.tensor_scalar(k_y[:, :].bitcast(I32), k_ss[:, :].bitcast(I32), -0.5,
                                                       float(0x5F3759DF), ALU.mult, ALU.add))
                    for _ in range(3):
                        link(l_steps, b, dve.tensor_tensor(k_a[:, :], k_y[:, :], k_y[:, :], ALU.mult))
                        link(l_steps, b, dve.scalar_tensor_tensor(k_a[:, :], k_a[:, :], -0.5, k_ss[:, :],
                                                                  ALU.mult, ALU.mult))
                        link(l_steps, b, dve.scalar_tensor_tensor(k_y[:, :], k_a[:, :], 1.5, k_y[:, :],
                                                                  ALU.add, ALU.mult))
                    dve.tensor_tensor(k_tok[:, :, :].rearrange("p c (h e) -> p (c h) e", e=HD),
                                      k_tok[:, :, :].rearrange("p c (h e) -> p (c h) e", e=HD),
                                      k_y[:, :, None].broadcast_to([P, TILES * H, HD]), ALU.mult).then_inc(s_kr.sem, 1)
                if step == "q2":
                    dve.wait_ge(s_qact.sem, s_qact.at(b, 2))
                    dve.tensor_tensor(qT[:, :], q_max[:, :], q_exp[:, :], ALU.add).then_inc(s_qr.sem, 1)
                if step == "kv":
                    dve.wait_ge(s_kv.sem, s_kv.at(b))
                    dve.tensor_tensor(kv[:, :], bank[:, 6, 0:D], blocks[:, :], ALU.mult).then_inc(s_kvm.sem, 1)
                if step == "out":
                    dve.wait_ge(s_lo.sem, s_lo.at(b))
                    dve.wait_ge(s_lnb.sem, s_lnb.at(b))
                    link(l_steps, b, dve.tensor_tensor(lin, by_tile(6), l_nb[:, :, :], ALU.add))
                    moments(l_steps, b, lo_norm, lin)
                    dve.tensor_scalar(lo_norm.var[:, 0:TILES], lo_norm.mv[:, :, 1], RMS_EPS, None, ALU.add) \
                        .then_inc(lo_norm.var_ready.sem, 1)
                if step == "out_scale":
                    scales(lo_norm, b, 1, 1, s_lin)
                if step == "xl":
                    dve.wait_ge(s_lon.sem, s_lon.at(b))
                    link(l_steps, b, dve.tensor_tensor(lin, lin, over_tiles(l_gamma), ALU.mult))
                    dve.wait_ge(s_lxb.sem, s_lxb.at(b))
                    if began(b - 1):
                        dve.wait_ge(second["xx1_ready"].sem, second["xx1_ready"].at(b - 1))
                    dve.tensor_tensor(xl[:, :, :], lin, l_xb[:, :, :], ALU.add).then_inc(s_xl.sem, 1)

            def attention(a, b, step, k):
                low, high = a.banks
                if step == "norm":
                    x_ready = s_xa if a is first else s_xl
                    dve.wait_ge(x_ready.sem, x_ready.at(b))
                    moments(steps[a], b, a.norm, a.x)
                    dve.tensor_scalar(a.norm.var[:, 0:TILES], a.norm.mv[:, :, 1], LN_EPS, None, ALU.add)
                    dve.tensor_scalar(a.norm.var[:, TILES:2 * TILES], a.norm.mv[:, :, 1], 1.0 + RMS_EPS,
                                      RMS_EPS * LN_EPS, ALU.mult, ALU.add).then_inc(a.norm.var_ready.sem, 1)
                if step == "scale":
                    scales(a.norm, b, 1, 2, a["scales_ready"])
                if step == "q":
                    dve.wait_ge(a["q_projected"].sem, a["q_projected"].at(b))
                    dve.tensor_tensor(a.q[:, :, :], by_tile(low), over_tiles(f_bq), ALU.add) \
                        .then_inc(a["q_ready"].sem, 1)
                c = k
                if step == "pv":
                    dve.wait_ge(a["prob_ready"].sem, a["prob_ready"].at(b, c + 1))
                    if c == 0:
                        dve.wait_ge(a["v_ready"].sem, a["v_ready"].at(b))
                        if a is first:
                            if began(b - 2):
                                dve.wait_ge(second["pv_summed"].sem, second["pv_summed"].at(b - 2))
                        elif not (isinstance(b, int) and b + 1 >= BATCH):
                            dve.wait_ge(first["pv_summed"].sem, first["pv_summed"].at(b + 1))
                    if c >= 2:
                        dve.wait_ge(a["pv_summed"].sem, a["pv_summed"].at(b, c - 1))
                    products(dve, a, c).then_inc(a["pv_ready"].sem, 1)
                if step == "qk":
                    sc = a.score[:, c, :].rearrange("p (h g) -> p h g", g=H)
                    dve.wait_ge(a["qk_ready"].sem, a["qk_ready"].at(b, c + 1))
                    dve.tensor_reduce(a.score[:, c, :], qk[:, c % 2, :].rearrange("p (a e) -> p a e", e=HD),
                                      AX.X, ALU.add).then_inc(a["score_ready"].sem, 1)
                    dve.wait_ge(a["score_ready"].sem, a["score_ready"].at(b, c + 1))
                    link(steps[a], b, dve.tensor_reduce(a.peak[:, c, :], sc, AX.X, ALU.max))
                    dve.tensor_tensor(sc, sc, a.peak[:, c, :, None].broadcast_to([P, H, H]), ALU.subtract) \
                        .then_inc(a["shifted"].sem, 1)
                if step == "total":
                    dve.wait_ge(a["prob_ready"].sem, a["prob_ready"].at(b))
                    link(steps[a], b, dve.tensor_reduce(a.total[:, :, :].rearrange("p c h -> p (c h)"),
                                           a.score[:, :, :].rearrange("p c (h g) -> p (c h) g", g=H), AX.X, ALU.add))
                    link(steps[a], b, dve.reciprocal(a.rec[:, :, :], a.total[:, :, :]))
                if step == "o":
                    dve.wait_ge(a["pv_summed"].sem, a["pv_summed"].at(b))
                    dve.tensor_tensor(a.o[:, :, :].rearrange("p c (h e) -> p (c h) e", e=HD),
                                      by_head(bank[:, high, :]),
                                      a.rec[:, :, :].rearrange("p c h -> p (c h)")[:, :, None]
                                      .broadcast_to([P, TILES * H, HD]), ALU.mult).then_inc(a["o_ready"].sem, 1)
                if step == "x1":
                    dve.wait_ge(a["o_projected"].sem, a["o_projected"].at(b))
                    dve.wait_ge(a["nb_ready"].sem, a["nb_ready"].at(b))
                    dve.tensor_tensor(a.x1[:, :, :], by_tile(high), a.nb[:, :, :], ALU.add) \
                        .then_inc(a["x1_ready"].sem, 1)
                if step == "norm2":
                    dve.wait_ge(a["x1_ready"].sem, a["x1_ready"].at(b))
                    moments(steps[a], b, a.norm, a.x1)
                    link(steps[a], b, dve.tensor_tensor(a.g_sum[:, :], a.norm.mv[:, :, 0], a.norm.mv[:, :, 0],
                                                        ALU.mult))
                    dve.scalar_tensor_tensor(a.norm.var[:, 0:TILES], a.g_sum[:, :], RMS_EPS, a.norm.mv[:, :, 1],
                                             ALU.add, ALU.add).then_inc(a.norm.var_ready.sem, 1)
                if step == "logits":
                    dve.wait_ge(a["logits_ready"].sem, a["logits_ready"].at(b))
                    link(steps[a], b, dve.tensor_tensor(a.gate[:, :, :],
                                           bank[:, high, 0:TILES * EXP].rearrange("p (c e) -> p c e", e=EXP),
                                           f_bg[:, None, :].broadcast_to([P, TILES, EXP]), ALU.add))
                    link(steps[a], b, dve.tensor_reduce(a.g_max[:, :], a.gate[:, :, :], AX.X, ALU.max))
                    dve.tensor_tensor(a.gate[:, :, :], a.gate[:, :, :],
                                      a.g_max[:, :, None].broadcast_to([P, TILES, EXP]), ALU.subtract) \
                        .then_inc(a["gate_ready"].sem, 1)
                if step == "gate":
                    dve.wait_ge(a["gate_exp_ready"].sem, a["gate_exp_ready"].at(b))
                    link(steps[a], b, dve.tensor_reduce(a.g_sum[:, :], a.gate[:, :, :], AX.X, ALU.add))
                    link(steps[a], b, dve.reciprocal(a.g_max[:, :], a.g_sum[:, :]))
                    dve.tensor_tensor(a.gate[:, :, :], a.gate[:, :, :],
                                      a.g_max[:, :, None].broadcast_to([P, TILES, EXP]), ALU.mult) \
                        .then_inc(a["gate_ready"].sem, 1)
                if step == "y":
                    dve.wait_ge(a["expert_added"].sem, a["expert_added"].at(b))
                    dve.wait_ge(a["pool_expert_added"].sem, a["pool_expert_added"].at(b))
                    if a is second:
                        dve.wait_ge(s_out.sem, 16 * (b + 1))
                    else:
                        if began(b - 1):
                            dve.wait_ge(s_lxb.sem, s_lxb.at(b - 1))
                    dve.tensor_tensor(a.y[:, :, :], by_tile(high), a.xx1[:, :, :], ALU.add) \
                        .then_inc(a["y_ready"].sem, 1)

            rounds(dve, VECTOR_PLAN, mamba, linear, attention)
            assert all(c.count == c.per for c in (m_steps, l_steps, steps[first], steps[second]))

        @block.scalar
        def _(act):
            act.wait_ge(s_w.sem, WEIGHTS)
            act.activation(a_neg[:, :, :], a_neg[:, :, :], ACT.Exp).then_inc(s_rates.sem, 1)
            act.wait_ge(s_rates.sem, 1)
            act.mul(a_neg[:, :, :], a_neg[:, :, :], -1.0).then_inc(s_rates.sem, 1)
            act.wait_ge(s_rates.sem, 2)
            act.wait_ge(s_const.sem, 1)

            def normalize(dst, src, norm, column):
                for c in range(TILES):
                    j = column + c
                    ins = act.activation(dst[:, c, :], src[:, c, :], ACT.Identity, scale=norm.rstd[:, j:j + 1],
                                         bias=norm.shift[:, j:j + 1])
                return ins

            def mamba(b, step, k):
                if step == "keep":
                    act.wait_ge(s_xin.sem, s_xin.at(b))
                    if began(b - 1):
                        act.wait_ge(s_xa.sem, s_xa.at(b - 1))
                    act.activation(xkeep[:, :, :], xin[:, :, :], ACT.Copy).then_inc(s_xkeep.sem, 1)
                if step == "nrm":
                    if began(b - 1):
                        act.wait_ge(s_yacc.sem, s_yacc.at(b - 1))
                    act.wait_ge(s_mscale.sem, s_mscale.at(b))
                    normalize(m_nrm, xin, m_norm, 0).then_inc(s_mnrm.sem, 1)
                if step == "nT":
                    act.wait_ge(s_mturn.sem, s_mturn.at(b))
                    act.activation(m_nT[:, CONV - 1:CONV - 1 + TOK], bank[:, 0, :], ACT.Copy).then_inc(s_mnT.sem, 1)
                if step == "conv":
                    h = k
                    act.wait_ge(s_conv.sem, s_conv.at(b, h + 1))
                    act.activation(cv_t[:, h, :], bank[:, 1 - h, :], ACT.Tanh, bias=conv_bh[:, h:h + 1],
                                   scale=0.5)
                    act.activation(cv_h[:, h, :], bank[:, 1 - h, :], ACT.Identity, bias=conv_bh[:, h:h + 1],
                                   scale=0.5).then_inc(s_cvt.sem, 1)
                if step == "z":
                    if began(b - 1):
                        act.wait_ge(s_yg.sem, s_yg.at(b - 1))
                    h = k
                    act.wait_ge(s_zp.sem, s_zp.at(b, h + 1))
                    act.activation(z_t[:, h, :], bank[:, 1 - h, :], ACT.Tanh, scale=0.5)
                    act.activation(z_h[:, h, :], bank[:, 1 - h, :], ACT.Copy, scale=0.5).then_inc(s_z.sem, 1)
                if step == "dt_low":
                    act.wait_ge(s_xp.sem, s_xp.at(b))
                    act.activation(dt_lo[96:P, :], bank[96:P, 1, :], ACT.Copy).then_inc(s_dtl.sem, 1)
                if step == "bc":
                    act.activation(bc_parts[0:32, :], bank[0:32, 1, :], ACT.Copy)
                    act.activation(bc_hi[:, :], bank[0:96, 1, :], ACT.Copy).then_inc(s_bch.sem, 1)
                if step == "bc_mid":
                    act.wait_ge(s_bcr.sem, s_bcr.at(b))
                    act.activation(bc_parts[32:64, :], bc_rest[32:64, :], ACT.Copy)
                    act.activation(bc_mid[64:96, :], bc_rest[64:96, :], ACT.Copy).then_inc(s_bcm.sem, 1)
                if step == "abs":
                    act.wait_ge(s_dtp.sem, s_dtp.at(b))
                    if began(b - 1):
                        act.wait_ge(s_mo.sem, s_mo.at(b - 1))
                    for h in range(HALVES):
                        act.activation(sp_abs[:, h, :], bank[:, 2 + h, :], ACT.Abs, bias=dt_b[:, h:h + 1])
                        ins = act.activation(sp_max[:, h, :], bank[:, 2 + h, :], ACT.Relu, bias=dt_b[:, h:h + 1])
                    ins.then_inc(s_abs.sem, 1)
                if step == "exp":
                    act.wait_ge(s_abs.sem, s_abs.at(b))
                    act.activation(sp_e[:, :, :], sp_abs[:, :, :], ACT.Exp, scale=-1.0)
                    act.activation(sp_t[:, :, :], sp_abs[:, :, :], ACT.Tanh, bias=half_ln2[:, 0:1], scale=0.5) \
                        .then_inc(s_spe.sem, 1)
                if step == "s2":
                    act.wait_ge(s_sps.sem, s_sps.at(b))
                    act.activation(sp_z[:, :, :], sp_e[:, :, :], ACT.Square, scale=0.25).then_inc(s_spz.sem, 1)
                    act.wait_ge(s_spz.sem, s_spz.at(b))
                    act.activation(sp_b[:, :, :], sp_z[:, :, :], ACT.Square, bias=poly_bias[:, 1:2])
                    act.activation(sp_a[:, :, :], sp_z[:, :, :], ACT.Square, bias=poly_bias[:, 0:1],
                                   scale=LEAD ** 0.5).then_inc(s_spq.sem, 1)
                if step == "decay":
                    if k == 0:
                        act.wait_ge(s_dt.sem, s_dt.at(b))
                    if k >= 2:
                        act.wait_ge(s_scan.sem, s_scan.at(b, k - 1))
                    for h in range(HALVES):
                        ins = act.activation(d_a[:, k % 2, h, :], dt[:, h, :], ACT.Exp, scale=a_neg[:, h, k:k + 1])
                    ins.then_inc(s_da.sem, 1)
                if step == "c":
                    act.wait_ge(s_cb.sem, s_cb.at(b, k + 1))
                    if k >= 2:
                        act.wait_ge(s_hc.sem, s_hc.at(b, k - 1))
                    act.activation(c_sb[:, k % 2, :], bank[:, 1, :], ACT.Copy).then_inc(s_cs.sem, 1)

            def linear(b, step, k):
                if step == "nrm":
                    act.wait_ge(s_lscale.sem, s_lscale.at(b))
                    normalize(l_nrm, xb, li_norm, 0).then_inc(s_lnrm.sem, 1)
                if step == "nT":
                    act.wait_ge(s_lturn.sem, s_lturn.at(b))
                    act.activation(l_nT[:, :], bank[:, 6, :], ACT.Copy).then_inc(s_lnT.sem, 1)
                if step == "k_exp":
                    act.wait_ge(s_kb.sem, s_kb.at(b))
                    act.activation(k_min[:, :, :], k_tok[:, :, :], ACT.Relu, scale=-1.0).then_inc(s_kact.sem, 1)
                    act.wait_ge(s_kact.sem, s_kact.at(b, 1))
                    act.activation(k_exp[:, :, :], k_min[:, :, :], ACT.Exp, scale=-1.0).then_inc(s_kact.sem, 1)
                if step == "k_sq":
                    act.wait_ge(s_ka.sem, s_ka.at(b))
                    act.activation(k_sq[:, :, :], k_tok[:, :, :], ACT.Square).then_inc(s_kact.sem, 1)
                if step == "q_exp":
                    act.wait_ge(s_lq.sem, s_lq.at(b))
                    act.activation(q_min[:, :], bank[:, 6, :], ACT.Relu, bias=l_bqn[:, 0:1], scale=-1.0)
                    act.activation(q_max[:, :], bank[:, 6, :], ACT.Relu, bias=l_bq[:, 0:1]).then_inc(s_qact.sem, 1)
                    act.wait_ge(s_qact.sem, s_qact.at(b, 1))
                    act.activation(q_exp[:, :], q_min[:, :], ACT.Exp, scale=-1.0).then_inc(s_qact.sem, 1)
                if step == "kvo":
                    act.wait_ge(s_kvp.sem, s_kvp.at(b))
                    act.activation(kvo[:, :], bank[:, 7, 0:D], ACT.Copy).then_inc(s_kvo.sem, 1)
                if step == "out_nrm":
                    act.wait_ge(s_lin.sem, s_lin.at(b))
                    normalize(lin, lin, lo_norm, 0).then_inc(s_lon.sem, 1)

            def attention(a, b, step, k):
                low, high = a.banks
                if step == "scaled":
                    act.wait_ge(a["scales_ready"].sem, a["scales_ready"].at(b))
                    normalize(a.scaled, a.x, a.norm, TILES).then_inc(a["normalized"].sem, 1)
                if step == "nrm":
                    normalize(a.nrm, a.x, a.norm, 0).then_inc(a["nrm_ready"].sem, 1)
                if step == "hT":
                    act.wait_ge(a["turned"].sem, a["turned"].at(b))
                    act.activation(a.hT[:, :], bank[:, low, :], ACT.Copy, scale=f_g1[:, 0:1]) \
                        .then_inc(a["hT_ready"].sem, 1)
                if step == "lat":
                    act.wait_ge(a["lat_projected"].sem, a["lat_projected"].at(b))
                    act.activation(a.latT[0:LAT, :], bank[0:LAT, high, :], ACT.Identity, bias=f_bdown[:, 0:1]) \
                        .then_inc(a["lat_ready"].sem, 1)
                if step == "k":
                    act.wait_ge(a["k_projected"].sem, a["k_projected"].at(b))
                    act.activation(a.k[:, :, :], bank[:, high, :], ACT.Copy).then_inc(a["k_ready"].sem, 1)
                if step == "v":
                    act.wait_ge(a["v_projected"].sem, a["v_projected"].at(b))
                    act.activation(a.v[:, :, :], bank[:, low, :], ACT.Copy).then_inc(a["v_ready"].sem, 1)
                c = k
                if step == "prob":
                    act.wait_ge(a["shifted"].sem, a["shifted"].at(b, c + 1))
                    act.activation(a.score[:, c, :], a.score[:, c, :], ACT.Exp, scale=SCALE) \
                        .then_inc(a["prob_ready"].sem, 1)
                if step == "oT":
                    act.wait_ge(a["o_turned"].sem, a["o_turned"].at(b))
                    act.activation(a.oT[:, :], bank[:, low, :], ACT.Copy).then_inc(a["oT_ready"].sem, 1)
                if step == "h2":
                    act.wait_ge(a.norm.rstd_ready.sem, a.norm.rstd_ready.at(b, 2))
                    for c in range(TILES):
                        ins = act.activation(a.h2[:, c, :], a.x1[:, c, :], ACT.Copy, scale=a.norm.rstd[:, c:c + 1])
                    ins.then_inc(a["h2_ready"].sem, 1)
                if step == "h2T":
                    act.wait_ge(a["h2_turned"].sem, a["h2_turned"].at(b))
                    act.activation(a.h2T[:, :], bank[:, low, :], ACT.Copy, scale=f_g2[:, 0:1]) \
                        .then_inc(a["h2T_ready"].sem, 1)
                if step == "gate":
                    act.wait_ge(a["gate_ready"].sem, a["gate_ready"].at(b, 1))
                    act.activation(a.gate[:, :, :], a.gate[:, :, :], ACT.Exp).then_inc(a["gate_exp_ready"].sem, 1)
                e = k
                if step == "gated":
                    if e == 0:
                        act.wait_ge(a["gate_ready"].sem, a["gate_ready"].at(b, 2))
                    act.wait_ge(a["share_ready"].sem, a["share_ready"].at(b, e + 1))
                    if 2 <= e < 2 + TENSOR_EXPERTS:
                        act.wait_ge(a["expert_added"].sem, a["expert_added"].at(b, e - 1))
                    elif e >= 2:
                        act.wait_ge(a["pool_expert_added"].sem, a["pool_expert_added"].at(b, e - 1 - TENSOR_EXPERTS))
                    for c in range(TILES):
                        ins = act.activation(a.gated[:, e % 2, c, :], bank[:, low, D * c:D * c + D], ACT.Copy,
                                             scale=a.gate[:, c, e:e + 1])
                    ins.then_inc(a["gated_ready"].sem, 1)

            rounds(act, SCALAR_PLAN, mamba, linear, attention)

        @block.tensor
        def _(pe):
            pe.wait_ge(s_w.sem, WEIGHTS)
            pe.wait_ge(s_const.sem, 1)

            def mm(out, lhsT, rhs, start=True, stop=True):
                return pe.matmul(out, lhsT, rhs, start=start, stop=stop)

            def turn(b, src):
                for c in range(TILES):
                    ins = pe.transpose(bank[:, b, P * c:P * c + P], src[:, c, :], ident[:, :])
                return ins

            def by_tokens(b, lhsT, rhs):
                for c in range(TILES):
                    ins = mm(bank[:, b, D * c:D * c + D], lhsT[:, P * c:P * c + P], rhs)
                return ins

            def mamba(b, step, k):
                if step == "turn":
                    pe.wait_ge(s_mnrm.sem, s_mnrm.at(b))
                    if began(b - 1):
                        pe.wait_ge(s_bx.sem, s_bx.at(b - 1))
                    turn(0, m_nrm).then_inc(s_mturn.sem, 1)
                if step == "conv":
                    h = k
                    pe.wait_ge(s_mnT.sem, s_mnT.at(b))
                    if began(b - 1):
                        pe.wait_ge(s_cs.sem, s_cs.at(b - 1))
                    for t in range(CONV):
                        ins = mm(bank[:, 1 - h, :], conv_in_w[:, P * (HALVES * t + h):P * (HALVES * t + h + 1)],
                                 m_nT[:, t:t + TOK], t == 0, t == CONV - 1)
                    ins.then_inc(s_conv.sem, 1)
                if step == "z":
                    h = k
                    pe.wait_ge(s_cvt.sem, s_cvt.at(b, h + 1))
                    mm(bank[:, 1 - h, :], in_w[:, P * (HALVES + h):P * (HALVES + h + 1)],
                       m_nT[:, CONV - 1:CONV - 1 + TOK]) \
                        .then_inc(s_zp.sem, 1)
                if step == "xp":
                    pe.wait_ge(s_z.sem, s_z.at(b, 1))
                    pe.wait_ge(s_xc.sem, s_xc.at(b))
                    for h in range(HALVES):
                        ins = mm(bank[:, 1, :], xp_w[:, h, :], xc[:, h, :], h == 0, h == HALVES - 1)
                    ins.then_inc(s_xp.sem, 1)
                if step == "dt":
                    pe.wait_ge(s_dtl.sem, s_dtl.at(b))
                    if began(b - 1):
                        pe.wait_ge(s_xa.sem, s_xa.at(b - 1))
                    for h in range(HALVES):
                        ins = mm(bank[:, 2 + h, :], dt_w[96:96 + RANK, P * h:P * h + P], dt_lo[96:96 + RANK, :])
                    ins.then_inc(s_dtp.sem, 1)
                if step == "bc":
                    if k == 0:
                        pe.wait_ge(s_z.sem, s_z.at(b))
                        pe.wait_ge(s_bcp.sem, s_bcp.at(b))
                    broadcast(b, k)
                if step == "add":
                    add_state(b, k)
                if step == "out":
                    pe.wait_ge(s_yg.sem, s_yg.at(b))
                    for c in range(TILES):
                        for h in range(HALVES):
                            ins = mm(bank[:, 2, D * c:D * c + D], sp_e[:, h, P * c:P * c + P], out_w[:, h, :],
                                     h == 0, h == HALVES - 1)
                    ins.then_inc(s_mo.sem, 1)

            def broadcast(b, k):
                if k >= 1:
                    pe.wait_ge(s_bx.sem, s_bx.at(b, k))
                mm(bank[:, 0, :], pickb[:, k, :], bc_parts[:, :]).then_inc(s_bb.sem, 1)
                if k >= 1:
                    pe.wait_ge(s_cs.sem, s_cs.at(b, k))
                mm(bank[:, 1, :], pickb[:, STATE + k, :], bc_parts[:, :]).then_inc(s_cb.sem, 1)

            def add_state(b, k):
                pe.wait_ge(s_hc.sem, s_hc.at(b, k + 1))
                if k == 0:
                    pe.wait_ge(s_dt.sem, s_dt.at(b))
                for h in range(HALVES):
                    ins = mm(bank[:, 2 + h, :], ident[:, :], hc[:, k % 2, h, :], k == 0, k == STATE - 1)
                ins.then_inc(s_yacc.sem, 1)

            def linear(b, step, k):
                if step == "turn":
                    pe.wait_ge(s_lnrm.sem, s_lnrm.at(b))
                    if began(b - 1):
                        pe.wait_ge(second["gated_ready"].sem, second["gated_ready"].at(b - 1))
                    turn(6, l_nrm).then_inc(s_lturn.sem, 1)
                if step == "k":
                    pe.wait_ge(s_lnT.sem, s_lnT.at(b))
                    if began(b - 1):
                        pe.wait_ge(second["y_ready"].sem, second["y_ready"].at(b - 1))
                    by_tokens(7, l_nT, l_wk[:, :]).then_inc(s_lk.sem, 1)
                if step == "q":
                    mm(bank[:, 6, :], l_wq[:, :], l_nT[:, :]).then_inc(s_lq.sem, 1)
                if step == "v":
                    pe.wait_ge(s_kb.sem, s_kb.at(b))
                    by_tokens(7, l_nT, l_wv[:, :]).then_inc(s_lv.sem, 1)
                if step == "kv":
                    pe.wait_ge(s_qact.sem, s_qact.at(b, 1))
                    pe.wait_ge(s_vr.sem, s_vr.at(b))
                    pe.wait_ge(s_kr.sem, s_kr.at(b))
                    for c in range(TILES):
                        ins = mm(bank[:, 6, 0:D], v_tok[:, c, :], k_tok[:, c, :], c == 0, c == TILES - 1)
                    ins.then_inc(s_kv.sem, 1)
                if step == "kvp":
                    pe.wait_ge(s_kvm.sem, s_kvm.at(b))
                    mm(bank[:, 7, 0:D], kv[:, :], l_wo[:, :]).then_inc(s_kvp.sem, 1)
                if step == "out":
                    pe.wait_ge(s_kvo.sem, s_kvo.at(b))
                    pe.wait_ge(s_qr.sem, s_qr.at(b))
                    by_tokens(6, qT, kvo[:, :]).then_inc(s_lo.sem, 1)

            def attention(a, b, step, k):
                low, high = a.banks
                if step == "turn":
                    pe.wait_ge(a["normalized"].sem, a["normalized"].at(b))
                    if a is second:
                        pe.wait_ge(s_lin.sem, s_lin.at(b))
                    else:
                        if began(b - 1):
                            pe.wait_ge(a["gated_ready"].sem, a["gated_ready"].at(b - 1))
                    turn(low, a.scaled).then_inc(a["turned"].sem, 1)
                if step == "lat":
                    pe.wait_ge(a["hT_ready"].sem, a["hT_ready"].at(b))
                    if a is first:
                        if began(b - 1):
                            pe.wait_ge(a["y_ready"].sem, a["y_ready"].at(b - 1))
                    mm(bank[0:LAT, high, :], f_wdown[:, :], a.hT[:, :]).then_inc(a["lat_projected"].sem, 1)
                if step == "q":
                    by_tokens(low, a.hT, f_wq[:, :]).then_inc(a["q_projected"].sem, 1)
                if step == "k":
                    pe.wait_ge(a["lat_ready"].sem, a["lat_ready"].at(b))
                    by_tokens(high, a.latT, f_wupk[:, :]).then_inc(a["k_projected"].sem, 1)
                if step == "v":
                    pe.wait_ge(a["q_ready"].sem, a["q_ready"].at(b))
                    by_tokens(low, a.latT, f_wupv[:, :]).then_inc(a["v_projected"].sem, 1)
                c = k
                if step == "sum":
                    if c == 0:
                        pe.wait_ge(a["k_ready"].sem, a["k_ready"].at(b))
                    if c >= VECTOR_TILES:
                        pe.wait_ge(a["pool_pv_ready"].sem, a["pool_pv_ready"].at(b, c + 1 - VECTOR_TILES))
                    else:
                        pe.wait_ge(a["pv_ready"].sem, a["pv_ready"].at(b, c + 1))
                    for g in range(H):
                        ins = mm(bank[:, high, D * c:D * c + D], ident[:, :], pv[:, c % 2, g, :], g == 0, g == H - 1)
                    ins.then_inc(a["pv_summed"].sem, 1)
                if step == "o":
                    pe.wait_ge(a["o_ready"].sem, a["o_ready"].at(b))
                    turn(low, a.o).then_inc(a["o_turned"].sem, 1)
                if step == "o_proj":
                    pe.wait_ge(a["oT_ready"].sem, a["oT_ready"].at(b))
                    by_tokens(high, a.oT, f_wo[:, :]).then_inc(a["o_projected"].sem, 1)
                if step == "h2":
                    pe.wait_ge(a["h2_ready"].sem, a["h2_ready"].at(b))
                    turn(low, a.h2).then_inc(a["h2_turned"].sem, 1)
                if step == "logits":
                    pe.wait_ge(a["h2T_ready"].sem, a["h2T_ready"].at(b))
                    pe.wait_ge(a["x1_ready"].sem, a["x1_ready"].at(b))
                    for c in range(TILES):
                        ins = mm(bank[:, high, EXP * c:EXP * c + EXP], a.h2T[:, P * c:P * c + P], f_wg[:, :])
                    ins.then_inc(a["logits_ready"].sem, 1)
                e = k
                if step == "expert":
                    if e >= 1:
                        pe.wait_ge(a["gated_ready"].sem, a["gated_ready"].at(b, e))
                    by_tokens(low, a.h2T, f_we[:, e, :]).then_inc(a["share_ready"].sem, 1)
                if step == "share":
                    pe.wait_ge(a["gated_ready"].sem, a["gated_ready"].at(b, e + 1))
                    if e == 0:
                        pe.wait_ge(a["gate_ready"].sem, a["gate_ready"].at(b, 1))
                    mm(bank[:, high, :], ident[:, :], a.gated[:, e % 2, :, :], e == 0, e == TENSOR_EXPERTS - 1) \
                        .then_inc(a["expert_added"].sem, 1)

            rounds(pe, TENSOR_PLAN, mamba, linear, attention)


_OUT = ((BATCH, TOK, D), "float32")


def kernel(**a):
    import concourse.bacc as bacc
    from concourse.bass_utils import run_bass_kernel_spmd

    a = {k: np.asarray(v) for k, v in a.items()}
    A, B, F = "L0_attn_a_", "L0_attn_b_", "L0_ffn_"

    def halves(x):
        return x.reshape((HALVES, P) + x.shape[1:]).swapaxes(0, 1)

    xp = a[A + "x_proj_w"].T
    bc = xp[:, RANK:]
    xp = np.concatenate([bc, bc, bc, xp[:, :RANK], np.zeros((xp.shape[0], 32 - RANK), xp.dtype)], axis=1)
    up = np.concatenate([a[F + "Wup"], a[F + "bup"][None]], axis=0).reshape(LAT + 1, H, 2, HD)
    arrays = {
        "x": a[A + "x"], "in_w": a[A + "in_proj_w"].T, "conv_w": a[A + "conv_w"].T.reshape(-1),
        "conv_b": halves(a[A + "conv_b"]), "xp_w": halves(xp), "dt_w": a[A + "dt_proj_w"].T,
        "dt_b": halves(a[A + "dt_proj_b"]), "alog": halves(a[A + "A_log"]), "dp": halves(a[A + "Dp"]),
        "out_w": halves(a[A + "out_proj_w"].T),
        "l_wq": a[B + "Wq"], "l_bq": a[B + "bq"][:, None], "l_wk": a[B + "Wk"], "l_bk": a[B + "bk"],
        "l_wv": a[B + "Wv"], "l_bv": a[B + "bv"], "l_wo": a[B + "Wo"], "l_bo": a[B + "bo"],
        "l_gamma": a[B + "gamma"], "l_beta": a[B + "beta"],
        "f_g1": a[F + "gamma1"][:, None], "f_wq": a[F + "Wq"], "f_bq": a[F + "bq"],
        "f_wdown": a[F + "Wdown"], "f_bdown": a[F + "bdown"][:, None],
        "f_wupk": up[:, :, 0].reshape(LAT + 1, D), "f_wupv": up[:, :, 1].reshape(LAT + 1, D),
        "f_wo": a[F + "Wo"], "f_bo": a[F + "bo"], "f_g2": a[F + "gamma2"][:, None],
        "f_wg": a[F + "Wg"], "f_bg": a[F + "bg"], "f_we": a[F + "We"].transpose(1, 0, 2),
        "ident": np.eye(P, dtype=np.float32), "pick": np.tile(np.eye(32, dtype=np.float32), (3, 1)),
        "blocks": np.kron(np.eye(H, dtype=np.float32), np.ones((HD, HD), np.float32)),
    }
    nc = bacc.Bacc("TRN2", target_bir_lowering=False, num_devices=1)
    arrays = {f"in_{k}": np.ascontiguousarray(v) for k, v in arrays.items()}
    args = [nc.dram_tensor(k, v.shape, mybir.dt.from_np(v.dtype), kind="ExternalInput").ap()
            for k, v in arrays.items()]
    out = nc.dram_tensor("out", _OUT[0], FP32, kind="ExternalOutput").ap()
    hybrid_block_kernel(nc, *args, out)
    r = run_bass_kernel_spmd(nc, [arrays], core_ids=[0])
    return r.results[0]["out"]
```
